# Optimizing a Trainium2 kernel written in Bass

```python
import numpy as np
import jax
import jax.numpy as jnp

def _softmax(x, axis=-1):
    return jax.nn.softmax(x, axis=axis)

def _gelu(x):
    return jax.nn.gelu(x, approximate=True)

def _silu(x):
    return jax.nn.silu(x)

def _sigmoid(x):
    return jax.nn.sigmoid(x)

def _layernorm(x, axis=-1, eps=1e-05):
    m = jnp.mean(x, axis=axis, keepdims=True)
    v = jnp.var(x, axis=axis, keepdims=True)
    return (x - m) / jnp.sqrt(v + eps)

def _scatter_add(tgt, idx, src, axis=0):
    return tgt.at[idx].add(src)

def _segment_sum(src, seg, n):
    return jax.ops.segment_sum(src, seg, n)
kernel_name = 'mk_gnn_ffn_d1_gnn_r8_4ae0c5'

def setup_inputs(seed: int=0):
    np.random.seed(seed)
    _w = jnp.asarray

    def _rec_inputs():
        import jax
        import jax.numpy as jnp
        _gk = jax.random.key(seed)
        x = -2.695e-06 + 0.04999 * jax.random.normal(jax.random.fold_in(_gk, 1), (12500, 256), jnp.float32)
        src = jax.random.randint(jax.random.fold_in(_gk, 2), (200000,), 0, 12500, jnp.int32)
        dst = jnp.minimum((12500 * jax.random.uniform(jax.random.fold_in(_gk, 3), (200000,)) ** 2.0).astype(jnp.int32), 99999)
        _o = jnp.argsort(dst, stable=True)
        src = src[_o]
        dst = dst[_o]
        return (x, src, dst)
    x, src, dst = _rec_inputs()

    def _L0_gnn_setup():
        import jax, jax.numpy as jnp
        import numpy as np
        N = 12500
        D = 256
        E = 400000
        BN_EPS = 1e-05

        def gcn_conv(x, W, b, src, dst, num_nodes):
            loop = jnp.arange(num_nodes, dtype=src.dtype)
            src = jnp.concatenate([src, loop])
            dst = jnp.concatenate([dst, loop])
            deg = jax.ops.segment_sum(jnp.ones_like(dst, dtype=x.dtype), dst, num_segments=num_nodes)
            dinv = jnp.where(deg > 0, jax.lax.rsqrt(deg), 0.0)
            norm = dinv[src] * dinv[dst]
            xw = x @ W
            msg = xw[src] * norm[:, None]
            out = jax.ops.segment_sum(msg, dst, num_segments=num_nodes)
            return out + b

        def batch_norm(x, gamma, beta):
            mean = jnp.mean(x, axis=0)
            var = jnp.mean((x - mean) ** 2, axis=0)
            return gamma * (x - mean) * jax.lax.rsqrt(var + BN_EPS) + beta
        key = jax.random.key(seed)
        ks = jax.random.split(key, 5)
        edge_index = jax.random.randint(ks[0], (2, E), 0, N, dtype=jnp.int64)
        emb_weight = jax.random.normal(ks[1], (N, D), dtype=jnp.float32) * 0.05
        W1 = jax.random.normal(ks[2], (D, 2 * D), dtype=jnp.float32) * 0.05
        b1 = jnp.zeros((2 * D,), dtype=jnp.float32)
        W2 = jax.random.normal(ks[3], (2 * D, D), dtype=jnp.float32) * 0.05
        b2 = jnp.zeros((D,), dtype=jnp.float32)
        gamma = jnp.ones((D,), dtype=jnp.float32)
        beta = jnp.zeros((D,), dtype=jnp.float32)
        return {'edge_index': edge_index, 'emb_weight': emb_weight, 'W1': W1, 'b1': b1, 'W2': W2, 'b2': b2, 'gamma': gamma, 'beta': beta}
    _L0_gnn_all = _L0_gnn_setup()
    _L0_gnn_in = {k: v for k, v in _L0_gnn_all.items() if k in ('W1', 'b1', 'W2', 'b2', 'gamma', 'beta')}
    del _L0_gnn_all

    def _L0_ffn_setup():
        import jax, jax.numpy as jnp
        import numpy as np
        B, N, D = (16, 512, 256)
        NUM_EXPERTS, TOP_K, HEADS = (4, 2, 4)
        N_EDGES = 131072
        LN_EPS = 1e-05

        def _layernorm(x, g, b):
            mu = x.mean(-1, keepdims=True)
            var = ((x - mu) ** 2).mean(-1, keepdims=True)
            return (x - mu) * jax.lax.rsqrt(var + LN_EPS) * g + b

        def _forward(x, edge_index, W_gat, att_src, att_dst, b_gat, ln_gamma, ln_beta, W1, b1, W2, b2):
            Bc, Nc, Dc = x.shape
            M = Bc * Nc
            x_flat = x.reshape(M, Dc)
            h = (x_flat @ W_gat).reshape(M, HEADS, NUM_EXPERTS)
            loops = jnp.arange(M, dtype=edge_index.dtype)
            src = jnp.concatenate([edge_index[0], loops])
            dst = jnp.concatenate([edge_index[1], loops])
            a_src = (h * att_src).sum(-1)
            a_dst = (h * att_dst).sum(-1)
            e = jax.nn.leaky_relu(a_src[src] + a_dst[dst], negative_slope=0.2)
            e_max = jax.ops.segment_max(e, dst, num_segments=M)
            ee = jnp.exp(e - e_max[dst])
            denom = jax.ops.segment_sum(ee, dst, num_segments=M)
            alpha = ee / (denom[dst] + 1e-16)
            msg = h[src] * alpha[:, :, None]
            agg = jax.ops.segment_sum(msg, dst, num_segments=M).reshape(M, HEADS * NUM_EXPERTS) + b_gat
            scores = _layernorm(agg, ln_gamma, ln_beta).reshape(M, HEADS, NUM_EXPERTS).mean(1)
            scores = scores.reshape(Bc, Nc, NUM_EXPERTS)
            topk_s, topk_i = jax.lax.top_k(scores, TOP_K)
            w = jax.nn.softmax(topk_s, axis=-1)
            out = jnp.zeros_like(x)
            for ei in range(NUM_EXPERTS):
                g = jnp.where(topk_i == ei, w, 0.0).sum(-1)
                hh = jax.nn.gelu(x @ W1[ei] + b1[ei], approximate=False)
                out = out + g[..., None] * (hh @ W2[ei] + b2[ei])
            return out
        key = jax.random.key(seed)
        ks = jax.random.split(key, 8)
        s = 0.05
        return {'x': jax.random.normal(ks[0], (B, N, D), jnp.float32), 'W_gat': jax.random.normal(ks[1], (D, HEADS * NUM_EXPERTS), jnp.float32) * s, 'att_src': jax.random.normal(ks[2], (HEADS, NUM_EXPERTS), jnp.float32) * s, 'att_dst': jax.random.normal(ks[3], (HEADS, NUM_EXPERTS), jnp.float32) * s, 'b_gat': jnp.zeros((HEADS * NUM_EXPERTS,), jnp.float32), 'ln_gamma': jnp.ones((HEADS * NUM_EXPERTS,), jnp.float32), 'ln_beta': jnp.zeros((HEADS * NUM_EXPERTS,), jnp.float32), 'W1': jax.random.normal(ks[4], (NUM_EXPERTS, D, 2 * D), jnp.float32) * s, 'b1': jnp.zeros((NUM_EXPERTS, 2 * D), jnp.float32), 'W2': jax.random.normal(ks[5], (NUM_EXPERTS, 2 * D, D), jnp.float32) * s, 'b2': jnp.zeros((NUM_EXPERTS, D), jnp.float32), 'edge_index': jax.random.randint(ks[6], (2, N_EDGES), 0, B * N, jnp.int32)}
    _L0_ffn_all = _L0_ffn_setup()
    _L0_ffn_in = {k: v for k, v in _L0_ffn_all.items() if k in ('W_gat', 'att_src', 'att_dst', 'b_gat', 'ln_gamma', 'ln_beta', 'W1', 'b1', 'W2', 'b2', 'edge_index')}
    del _L0_ffn_all
    return {'x': x, 'src': src, 'dst': dst, 'L0_gnn_W1': _L0_gnn_in['W1'], 'L0_gnn_b1': _L0_gnn_in['b1'], 'L0_gnn_W2': _L0_gnn_in['W2'], 'L0_gnn_b2': _L0_gnn_in['b2'], 'L0_gnn_gamma': _L0_gnn_in['gamma'], 'L0_gnn_beta': _L0_gnn_in['beta'], 'L0_ffn_W_gat': _L0_ffn_in['W_gat'], 'L0_ffn_att_src': _L0_ffn_in['att_src'], 'L0_ffn_att_dst': _L0_ffn_in['att_dst'], 'L0_ffn_b_gat': _L0_ffn_in['b_gat'], 'L0_ffn_ln_gamma': _L0_ffn_in['ln_gamma'], 'L0_ffn_ln_beta': _L0_ffn_in['ln_beta'], 'L0_ffn_W1': _L0_ffn_in['W1'], 'L0_ffn_b1': _L0_ffn_in['b1'], 'L0_ffn_W2': _L0_ffn_in['W2'], 'L0_ffn_b2': _L0_ffn_in['b2'], 'L0_ffn_edge_index': _L0_ffn_in['edge_index']}

def reference(x, src, dst, L0_gnn_W1, L0_gnn_b1, L0_gnn_W2, L0_gnn_b2, L0_gnn_gamma, L0_gnn_beta, L0_ffn_W_gat, L0_ffn_att_src, L0_ffn_att_dst, L0_ffn_b_gat, L0_ffn_ln_gamma, L0_ffn_ln_beta, L0_ffn_W1, L0_ffn_b1, L0_ffn_W2, L0_ffn_b2, L0_ffn_edge_index):
    import jax
    import jax.numpy as jnp

    def _L0_gnn_ref(edge_index, emb_weight, W1, b1, W2, b2, gamma, beta):
        import jax, jax.numpy as jnp
        import numpy as np
        N = 12500
        D = 256
        E = 400000
        BN_EPS = 1e-05

        def gcn_conv(x, W, b, src, dst, num_nodes):
            loop = jnp.arange(num_nodes, dtype=src.dtype)
            src = jnp.concatenate([src, loop])
            dst = jnp.concatenate([dst, loop])
            deg = jax.ops.segment_sum(jnp.ones_like(dst, dtype=x.dtype), dst, num_segments=num_nodes)
            dinv = jnp.where(deg > 0, jax.lax.rsqrt(deg), 0.0)
            norm = dinv[src] * dinv[dst]
            xw = x @ W
            msg = xw[src] * norm[:, None]
            out = jax.ops.segment_sum(msg, dst, num_segments=num_nodes)
            return out + b

        def batch_norm(x, gamma, beta):
            mean = jnp.mean(x, axis=0)
            var = jnp.mean((x - mean) ** 2, axis=0)
            return gamma * (x - mean) * jax.lax.rsqrt(var + BN_EPS) + beta
        src, dst = (edge_index[0], edge_index[1])
        h = gcn_conv(emb_weight, W1, b1, src, dst, N)
        h = gcn_conv(h, W2, b2, src, dst, N)
        return batch_norm(h, gamma, beta)

    def _L0_ffn_ref(x, W_gat, att_src, att_dst, b_gat, ln_gamma, ln_beta, W1, b1, W2, b2, edge_index):
        import jax, jax.numpy as jnp
        import numpy as np
        B, N, D = (16, 512, 256)
        NUM_EXPERTS, TOP_K, HEADS = (4, 2, 4)
        N_EDGES = 131072
        LN_EPS = 1e-05

        def _layernorm(x, g, b):
            mu = x.mean(-1, keepdims=True)
            var = ((x - mu) ** 2).mean(-1, keepdims=True)
            return (x - mu) * jax.lax.rsqrt(var + LN_EPS) * g + b

        def _forward(x, edge_index, W_gat, att_src, att_dst, b_gat, ln_gamma, ln_beta, W1, b1, W2, b2):
            Bc, Nc, Dc = x.shape
            M = Bc * Nc
            x_flat = x.reshape(M, Dc)
            h = (x_flat @ W_gat).reshape(M, HEADS, NUM_EXPERTS)
            loops = jnp.arange(M, dtype=edge_index.dtype)
            src = jnp.concatenate([edge_index[0], loops])
            dst = jnp.concatenate([edge_index[1], loops])
            a_src = (h * att_src).sum(-1)
            a_dst = (h * att_dst).sum(-1)
            e = jax.nn.leaky_relu(a_src[src] + a_dst[dst], negative_slope=0.2)
            e_max = jax.ops.segment_max(e, dst, num_segments=M)
            ee = jnp.exp(e - e_max[dst])
            denom = jax.ops.segment_sum(ee, dst, num_segments=M)
            alpha = ee / (denom[dst] + 1e-16)
            msg = h[src] * alpha[:, :, None]
            agg = jax.ops.segment_sum(msg, dst, num_segments=M).reshape(M, HEADS * NUM_EXPERTS) + b_gat
            scores = _layernorm(agg, ln_gamma, ln_beta).reshape(M, HEADS, NUM_EXPERTS).mean(1)
            scores = scores.reshape(Bc, Nc, NUM_EXPERTS)
            topk_s, topk_i = jax.lax.top_k(scores, TOP_K)
            w = jax.nn.softmax(topk_s, axis=-1)
            out = jnp.zeros_like(x)
            for ei in range(NUM_EXPERTS):
                g = jnp.where(topk_i == ei, w, 0.0).sum(-1)
                hh = jax.nn.gelu(x @ W1[ei] + b1[ei], approximate=False)
                out = out + g[..., None] * (hh @ W2[ei] + b2[ei])
            return out
        return _forward(x, edge_index, W_gat, att_src, att_dst, b_gat, ln_gamma, ln_beta, W1, b1, W2, b2)
    edge_index = jnp.stack([src, dst])
    x = x + _L0_gnn_ref(edge_index, _layernorm(x, axis=-1), L0_gnn_W1, L0_gnn_b1, L0_gnn_W2, L0_gnn_b2, L0_gnn_gamma, L0_gnn_beta)
    x = x + _L0_ffn_ref(_layernorm(x, axis=-1)[None], L0_ffn_W_gat, L0_ffn_att_src, L0_ffn_att_dst, L0_ffn_b_gat, L0_ffn_ln_gamma, L0_ffn_ln_beta, L0_ffn_W1, L0_ffn_b1, L0_ffn_W2, L0_ffn_b2, L0_ffn_edge_index)[0]
    return x

_drawn_inputs = setup_inputs


def setup_inputs(seed=0):
    import zlib

    import numpy as np

    out = dict(_drawn_inputs(seed))
    spreads = {'L0_gnn_b1': (0.0, 0.1),
     'L0_gnn_b2': (0.0, 0.1),
     'L0_gnn_gamma': (1.0, 0.2),
     'L0_gnn_beta': (0.0, 0.1),
     'L0_ffn_b_gat': (0.0, 0.1),
     'L0_ffn_ln_gamma': (1.0, 0.2),
     'L0_ffn_ln_beta': (0.0, 0.1),
     'L0_ffn_b1': (0.0, 0.1),
     'L0_ffn_b2': (0.0, 0.1)}
    factors = {}
    for name, (base, spread) in spreads.items():
        noise = np.random.default_rng([zlib.crc32(name.encode()), seed]).standard_normal(out[name].shape)
        drawn = base * np.exp(spread * noise) if base else spread * noise
        out[name] = jnp.asarray(drawn.astype(out[name].dtype))
    for name, factor in factors.items():
        out[name] = (out[name] * factor).astype(out[name].dtype)
    return out
```

```python
import numpy as np
import concourse.bass as bass
from concourse import mybir
from contextlib import ExitStack

F32 = mybir.dt.float32
BF16 = mybir.dt.bfloat16
I32 = mybir.dt.int32
U32 = mybir.dt.uint32
ALU = mybir.AluOpType
ACT = mybir.ActivationFunctionType
AX = mybir.AxisListType

P = 128
N = 12500
D = 256
NW = (N + P - 1) // P
NP = NW * P
LASTROWS = N - (NW - 1) * P
KC = D // P
E_GNN = 200000
E_FFN = 131072
HEADS = 4
NE = 4
HG = HEADS * NE
ROW = HG + HEADS
F = 512
FC = F // P
EPS = 1e-5
B = 5
NB_W = NW + 1
PADLO = 255
BIG = 1e30
GT = 4
BANK = 512


def tiles_bound(edges):
    most = (edges + NW * (P - 1)) // P
    return (most + 7) // 8 * 8


def blocks_bound(edges):
    return (tiles_bound(edges) + P - 1) // P * P


def pairs(eng, n, body):
    body(0, 0, 0, True, False)
    body(1, 0, 1, True, n == 2)
    end = n // 2 if n % 2 else n // 2 - 1
    with eng.Fori(1, end) as i:
        body(i * 2, i, 0, False, False)
        body(i * 2 + 1, i, 1, False, False)
    if n % 2:
        body(n - 1, n // 2, 0, False, True)
    else:
        body(n - 2, n // 2 - 1, 0, False, False)
        body(n - 1, n // 2 - 1, 1, False, True)


class Signals:

    def __init__(self, nc):
        self.nc, self.taken = nc, []

    def enter_context(self, handle):
        self.taken.append(handle)
        return handle

    def give_back(self):
        self.nc.clear_and_free_semaphores(self.taken)
        self.taken = []
        self.nc.all_engine_barrier()


class Steps:

    def __init__(self, eng, sem):
        self.eng, self.sem, self.n = eng, sem, 0

    def did(self, instruction):
        instruction.then_inc(self.sem, 1)
        self.n += 1

    def settle(self):
        self.eng.wait_ge(self.sem, self.n)

    def link(self, instruction):
        self.did(instruction)
        self.settle()


def window_values(nc, row, start, count, engine):
    return nc.values_load_multi_w_load_instructions(
        row[0:1, bass.ds(start, count)], engines=[engine], min_val=0, max_val=NW - 1,
        skip_runtime_bounds_check_because="the table is clamped to the last window")[1]


def inverse_root(nc, dve, me, v, root, inv, s_ask, s_root, n):
    dve.sem_inc(s_ask)
    dve.wait_ge(s_root, n)
    me.link(nc.vector.reciprocal(inv, root))
    me.link(nc.vector.tensor_tensor(root, inv, inv, ALU.mult))
    me.link(nc.vector.tensor_tensor(root, root, v, ALU.mult))
    me.link(nc.vector.tensor_scalar(root, root, -0.5, 1.5, ALU.mult, ALU.add))
    me.link(nc.vector.tensor_tensor(v, root, inv, ALU.mult))


def take_root(nc, act, v, root, s_ask, s_root, n):
    act.wait_ge(s_ask, n)
    nc.scalar.activation(root, v, ACT.Sqrt).then_inc(s_root, 1)


def make_consts(nc, ctx, sems):
    def sb(name, shape, dt):
        return ctx.enter_context(nc.sbuf_tensor(name, shape, dt))
    c = {
        "sems": sems,
        "iota_i": sb("iota_i", [P, P], I32), "iota_f": sb("iota_f", [P, P], F32),
        "iota_b": sb("iota_b", [P, P], BF16),
        "ident": sb("ident", [P, P], F32), "ident_b": sb("ident_b", [P, P], BF16),
        "before": sb("before", [P, P], BF16), "notbefore": sb("notbefore", [P, P], BF16),
        "upto": sb("upto", [P, P], F32), "ones": sb("ones", [P, P], F32),
        "ones_b": sb("ones_b", [P, P], BF16), "zeros_b": sb("zeros_b", [P, P], BF16),
        "pick": sb("pick", [2 * HEADS, HEADS, P], BF16),
    }
    s_io = c["sems"].enter_context(nc.alloc_semaphore("c_iota"))
    s_set = c["sems"].enter_context(nc.alloc_semaphore("c_set"))
    s_sel = c["sems"].enter_context(nc.alloc_semaphore("c_sel"))
    with nc.Block() as block:
        @block.gpsimd
        def _(pool):
            nc.gpsimd.iota(c["iota_i"][:, :], [[1, P]], base=0, channel_multiplier=0).then_inc(s_io, 1)
            pool.wait_ge(s_set, 8)
            nc.gpsimd.affine_select(out=c["ident"][:, :], in_=c["ident"][:, :], compare_op=ALU.not_equal,
                                    fill=1.0, base=0, pattern=[[-1, P]], channel_multiplier=1)
            nc.gpsimd.affine_select(out=c["ident_b"][:, :], in_=c["ident_b"][:, :], compare_op=ALU.not_equal,
                                    fill=1.0, base=0, pattern=[[-1, P]], channel_multiplier=1)
            nc.gpsimd.affine_select(out=c["before"][:, :], in_=c["before"][:, :], compare_op=ALU.is_ge,
                                    fill=1.0, base=0, pattern=[[-1, P]], channel_multiplier=1)
            nc.gpsimd.affine_select(out=c["notbefore"][:, :], in_=c["notbefore"][:, :], compare_op=ALU.is_ge,
                                    fill=0.0, base=0, pattern=[[-1, P]], channel_multiplier=1)
            nc.gpsimd.affine_select(out=c["upto"][:, :], in_=c["upto"][:, :], compare_op=ALU.is_gt,
                                    fill=1.0, base=0, pattern=[[-1, P]], channel_multiplier=1)
            nc.gpsimd.affine_select(out=c["pick"][:, :, :], in_=c["pick"][:, :, :], compare_op=ALU.not_equal,
                                    fill=1.0, base=0, pattern=[[-1, HEADS], [0, P]],
                                    channel_multiplier=1).then_inc(s_sel, 1)
            pool.wait_ge(s_sel, 1)
            nc.gpsimd.affine_select(out=c["pick"][:, :, :], in_=c["pick"][:, :, :], compare_op=ALU.not_equal,
                                    fill=1.0, base=-HEADS, pattern=[[-1, HEADS], [0, P]],
                                    channel_multiplier=1).then_inc(s_sel, 1)

        @block.vector
        def _(dve):
            for name, v in (("ident", 0.0), ("ident_b", 0.0), ("before", 0.0), ("notbefore", 1.0),
                            ("upto", 0.0), ("ones", 1.0), ("ones_b", 1.0)):
                nc.vector.memset(c[name][:, :], v).then_inc(s_set, 1)
            nc.vector.memset(c["pick"][:, :, :], 0.0).then_inc(s_set, 1)
            nc.vector.memset(c["zeros_b"][:, :], 0.0)
            dve.wait_ge(s_io, 1)
            nc.vector.tensor_copy(c["iota_f"][:, :], c["iota_i"][:, :])
            nc.vector.tensor_copy(c["iota_b"][:, :], c["iota_i"][:, :])
    return c


def bin_edges(nc, c, ps, tag, edges, src, dst, listed, idx, lo_f, win_row, deg):
    cols0 = (edges + P - 1) // P
    cols = (cols0 + B - 1) // B * B
    full, rest = edges // cols0, edges % cols0
    nb = cols // B
    nt, ntb = tiles_bound(edges), blocks_bound(edges)
    slots = ntb * P
    with ExitStack() as ctx:
        def sb(name, shape, dt):
            return ctx.enter_context(nc.sbuf_tensor(tag + name, shape, dt))


        def sem(name):
            return c["sems"].enter_context(nc.alloc_semaphore(tag + name))

        dst_i = sb("dst_i", [P, cols], I32)
        src_i = sb("src_i", [P, cols], I32)
        part_i = sb("part_i", [P, cols], I32)
        win_b = sb("win_b", [P, cols], BF16)
        lo_b = sb("lo_b", [P, cols], BF16)
        rec = sb("rec", [P, cols, 2], I32)
        empty = sb("empty", [P, ntb, 2], I32)
        hot_w = sb("hot_w", [P, 2, B, NB_W], BF16)
        hot_lo = sb("hot_lo", [P, 2, B, P], BF16)
        picked = sb("picked", [P, B, NB_W], F32)
        pos_f = sb("pos_f", [P, B], F32)
        pos = sb("pos", [P, 2, B], U32)
        rec_ring = sb("rec_ring", [P, 2, B, 2], I32)
        count_i = sb("count_i", [P, 1], I32)
        tiles_f = sb("tiles_f", [P, 1], F32)
        ends = sb("ends", [P, 1], F32)
        base = sb("base", [P, 1], F32)
        diag = sb("diag", [P, P], F32)
        step_i = sb("step_i", [P, ntb], I32)
        step_f = sb("step_f", [P, ntb], F32)
        after = sb("after", [P, ntb], F32)
        back = sb("back", [P, 2, P, 2], I32)
        back_f = sb("back_f", [P, 2, 2, P], F32)
        hist, small, row = ps[:, 0, :], ps[:, 1, :], ps[:, 3, :]
        place = ps[:, 2, 0:B * NB_W].rearrange("p (j w) -> p j w", w=NB_W)
        turned = ps[:, 4:6, 0:2 * P].rearrange("p s (f q) -> p s f q", q=P)

        s_pad, s_ld, s_ld2, s_empty, s_fill, s_step = (sem(x) for x in ("pad", "ld", "ld2", "empty", "fill", "step"))
        s_keys, s_hot, s_hist, s_hsum = (sem(x) for x in ("keys", "hot", "hist", "hsum"))
        s_deg, s_cnt, s_tl, s_end, s_dg, s_base = (sem(x) for x in ("deg", "cnt", "tl", "end", "dg", "base"))
        s_dve, s_row, s_rowd, s_win = (sem(x) for x in ("dve", "row", "rowd", "win"))
        s_hot2, s_at, s_adv, s_read, s_pos = (sem(x) for x in ("hot2", "at", "adv", "read", "pos"))
        s_red = sem("red")
        s_sc = [sem("sc0"), sem("sc1")]
        s_tick = sem("tick")
        s_back = [sem("back0"), sem("back1")]
        s_bf, s_tr, s_out = (sem(x) for x in ("bf", "tr", "out"))
        s_listed = sem("listed")
        blocks = ntb // P
        chunk = 416 if ntb % 416 == 0 else 384
        chunks = ntb // chunk
        assert chunks * chunk == ntb

        with nc.Block() as block:
            @block.sync
            def _(sp):
                sp.wait_ge(s_pad, 2)
                for t, a in ((dst_i, dst), (src_i, src)):
                    sp.dma_start(t[0:full, 0:cols0],
                                 a[0:full * cols0].rearrange("(p n) -> p n", n=cols0)).then_inc(s_ld, 16)
                if rest:
                    for t, a in ((dst_i, dst), (src_i, src)):
                        sp.dma_start(t[full:full + 1, 0:rest],
                                     a[full * cols0:edges].rearrange("(p n) -> p n", p=1)).then_inc(s_ld2, 16)
                sp.wait_ge(s_empty, 2)
                sp.dma_start(listed.rearrange("(p n) c -> p (n c)", p=P),
                             empty[:, :, :].rearrange("p n c -> p (n c)")).then_inc(s_fill, 16)
                sp.wait_ge(s_listed, 1)
                rows = listed.rearrange("(b s p) c -> b s p c", s=P, p=P)
                for b in range(blocks):
                    if b >= 2:
                        sp.wait_ge(s_bf, b - 1)
                    sp.dma_start(back[:, b % 2, :, :], rows[b]).then_inc(s_back[b % 2], 16)

            @block.gpsimd
            def _(pool):
                nc.gpsimd.iota(step_i[:, :], [[1, ntb]], base=0, channel_multiplier=0).then_inc(s_step, 1)
                pool.wait_ge(s_fill, 16)

                def scatter(k, i, s, first, last):
                    pool.wait_ge(s_pos, k + 1)
                    pool.sem_inc(s_tick)
                    for j in range(B):
                        nc.gpsimd.indirect_dma_start(
                            out=listed, out_offset=bass.IndirectOffsetOnAxis(ap=pos[:, s, j:j + 1], axis=0),
                            in_=rec_ring[:, s, j, :], in_offset=None,
                            bounds_check=slots - 1, oob_is_err=False).then_inc(s_sc[s], 16)
                pairs(pool, nb, scatter)
                pool.wait_ge(s_sc[0], 16 * B * ((nb + 1) // 2))
                pool.wait_ge(s_sc[1], 16 * B * (nb // 2))
                pool.sem_inc(s_listed)

            @block.vector
            def _(dve):
                me = Steps(dve, s_dve)
                nc.vector.memset(dst_i[:, :], NW * P).then_inc(s_pad, 1)
                nc.vector.memset(src_i[:, :], 0).then_inc(s_pad, 1)
                nc.vector.memset(empty[:, :, 0], 0).then_inc(s_empty, 1)
                nc.vector.memset(empty[:, :, 1], PADLO).then_inc(s_empty, 1)
                nc.vector.memset(base[:, :], float(slots))
                nc.vector.memset(ends[:, :], 0.0)
                dve.wait_ge(s_ld, 32)
                if rest:
                    dve.wait_ge(s_ld2, 32)
                me.link(nc.vector.tensor_scalar(part_i[:, :], dst_i[:, :], 7, None, ALU.arith_shift_right))
                nc.vector.tensor_copy(win_b[:, :], part_i[:, :])
                me.link(nc.vector.tensor_scalar(rec[:, :, 1], dst_i[:, :], P - 1, None, ALU.bitwise_and))
                nc.vector.tensor_copy(lo_b[:, :], rec[:, :, 1])
                me.link(nc.vector.tensor_copy(rec[:, :, 0], src_i[:, :]))

                def hot_windows(k, s, to):
                    return nc.vector.tensor_tensor(
                        to[:, s, :, :], c["iota_b"][:, None, 0:NB_W].to_broadcast([P, B, NB_W]),
                        win_b[:, bass.ds(k * B, B), None].to_broadcast([P, B, NB_W]), ALU.is_equal)

                def count(k, i, s, first, last):
                    if not first:
                        dve.wait_ge(s_hist, k - 1)
                    hot_windows(k, s, hot_w)
                    nc.vector.tensor_tensor(
                        hot_lo[:, s, :, :], c["iota_b"][:, None, :].to_broadcast([P, B, P]),
                        lo_b[:, bass.ds(k * B, B), None].to_broadcast([P, B, P]), ALU.is_equal).then_inc(s_hot, 1)
                pairs(dve, nb, count)
                dve.wait_ge(s_hsum, 1)
                nc.vector.tensor_copy(deg[:, :], hist[:, 0:NW]).then_inc(s_deg, 1)
                dve.wait_ge(s_cnt, 1)
                me.link(nc.vector.tensor_copy(count_i[0:NW, :], small[0:NW, 0:1]))
                me.link(nc.vector.tensor_scalar(count_i[0:NW, :], count_i[0:NW, :], P - 1, None, ALU.add))
                me.link(nc.vector.tensor_scalar(count_i[0:NW, :], count_i[0:NW, :], 7, None, ALU.arith_shift_right))
                me.link(nc.vector.tensor_copy(tiles_f[0:NW, :], count_i[0:NW, :]))
                dve.sem_inc(s_tl)
                dve.wait_ge(s_end, 1)
                me.link(nc.vector.tensor_copy(ends[0:NW, :], small[0:NW, 1:2]))
                me.link(nc.vector.tensor_tensor(base[0:NW, :], ends[0:NW, :], tiles_f[0:NW, :], ALU.subtract))
                me.link(nc.vector.tensor_scalar(base[0:NW, :], base[0:NW, :], float(P), None, ALU.mult))
                nc.vector.tensor_scalar(diag[0:NB_W, 0:NB_W], c["ident"][0:NB_W, 0:NB_W], base[0:NB_W, 0:1], None,
                                        ALU.mult).then_inc(s_dg, 1)
                dve.wait_ge(s_step, 1)
                me.link(nc.vector.tensor_copy(step_f[:, :], step_i[:, :]))
                nc.vector.tensor_scalar(after[0:NW, :], step_f[0:NW, :], ends[0:NW, 0:1], None,
                                        ALU.is_ge).then_inc(s_row, 1)
                for q in range(chunks):
                    dve.wait_ge(s_rowd, q + 1)
                    nc.vector.tensor_scalar(win_row[0:1, q * chunk:(q + 1) * chunk], row[0:1, 0:chunk],
                                            float(NW - 1), None, ALU.min).then_inc(s_win, 1)

                def positions(k, i, s, first, last):
                    if not first:
                        dve.wait_ge(s_adv, k - 1)
                    hot_windows(k, s, hot_w).then_inc(s_hot2, 1)
                    dve.wait_ge(s_at, k + 1)
                    nc.vector.tensor_tensor(picked[:, :, :], place[:, :, :], hot_w[:, s, :, :],
                                            ALU.mult).then_inc(s_read, 1)
                    dve.wait_ge(s_read, k + 1)
                    nc.vector.tensor_reduce(pos_f[:, :], picked[:, :, :], AX.X, ALU.add).then_inc(s_red, 1)
                    if not first:
                        dve.wait_ge(s_sc[s], i * (16 * B))
                    dve.wait_ge(s_red, k + 1)
                    nc.vector.tensor_copy(pos[:, s, :], pos_f[:, :])
                    nc.vector.tensor_copy(rec_ring[:, s, :, :], rec[:, bass.ds(k * B, B), :]).then_inc(s_pos, 1)
                pairs(dve, nb, positions)
                for b in range(blocks):
                    dve.wait_ge(s_back[b % 2], 16 * (b // 2 + 1))
                    if b >= 2:
                        dve.wait_ge(s_tr, b - 1)
                    nc.vector.tensor_copy(back_f[:, b % 2, :, :],
                                          back[:, b % 2, :, :].rearrange("s p c -> s c p")).then_inc(s_bf, 1)
                    dve.wait_ge(s_tr, b + 1)
                    nc.vector.tensor_copy(idx[:, b * P:(b + 1) * P], turned[:, b % 2, 0, :])
                    nc.vector.tensor_copy(lo_f[:, b * P:(b + 1) * P], turned[:, b % 2, 1, :]).then_inc(s_out, 1)

            @block.tensor
            def _(pe):
                nc.tensor.matmul(hist[:, 0:NB_W], c["zeros_b"][:, :], c["zeros_b"][:, 0:NB_W], start=True, stop=False)

                def count(k, i, s, first, last):
                    pe.wait_ge(s_hot, k + 1)
                    for j in range(B):
                        m = nc.tensor.matmul(hist[:, 0:NB_W], hot_lo[:, s, j, :], hot_w[:, s, j, :],
                                             start=False, stop=False)
                    m.then_inc(s_hist, 1)
                pairs(pe, nb, count)
                nc.tensor.matmul(hist[:, 0:NB_W], c["zeros_b"][:, :], c["zeros_b"][:, 0:NB_W],
                                 start=False, stop=True).then_inc(s_hsum, 1)
                pe.wait_ge(s_deg, 1)
                nc.tensor.matmul(small[0:NW, 0:1], deg[:, :], c["ones"][:, 0:1], start=True, stop=True).then_inc(s_cnt, 1)
                pe.wait_ge(s_tl, 1)
                nc.tensor.matmul(small[0:NW, 1:2], c["upto"][0:NW, 0:NW], tiles_f[0:NW, :],
                                 start=True, stop=True).then_inc(s_end, 1)
                pe.wait_ge(s_dg, 1)
                nc.tensor.matmul(place[:, :, :], c["ones"][0:NB_W, :],
                                 diag[0:NB_W, None, 0:NB_W].to_broadcast([NB_W, B, NB_W]), start=True, stop=True)
                pe.wait_ge(s_row, 1)
                for q in range(chunks):
                    if q:
                        pe.wait_ge(s_win, q)
                    nc.tensor.matmul(row[0:1, 0:chunk], c["ones"][0:NW, 0:1], after[0:NW, q * chunk:(q + 1) * chunk],
                                     start=True, stop=True).then_inc(s_rowd, 1)

                def positions(k, i, s, first, last):
                    def add(to, n, lhs, j):
                        return nc.tensor.matmul(place[:, to:to + n, :], lhs,
                                                hot_w[:, s, j:j + 1, :].to_broadcast([P, n, NB_W]) if n > 1
                                                else hot_w[:, s, j:j + 1, :], start=False, stop=True,
                                                skip_group_check=True)
                    pe.wait_ge(s_hot2, k + 1)
                    m = nc.tensor.matmul(place[:, :, :], c["before"][:, :], hot_w[:, s, :, :], start=False,
                                         stop=True, skip_group_check=True)
                    for j in range(B - 1):
                        m = add(j + 1, B - 1 - j, c["ones_b"][:, :], j)
                    m.then_inc(s_at, 1)
                    pe.wait_ge(s_read, k + 1)
                    m = nc.tensor.matmul(place[:, :, :], c["notbefore"][:, :], hot_w[:, s, :, :], start=False,
                                         stop=True, skip_group_check=True)
                    for j in range(1, B):
                        m = add(0, j, c["ones_b"][:, :], j)
                    m.then_inc(s_adv, 1)
                pairs(pe, nb, positions)
                for b in range(blocks):
                    pe.wait_ge(s_bf, b + 1)
                    if b >= 2:
                        pe.wait_ge(s_out, b - 1)
                    for f in range(2):
                        m = nc.tensor.transpose(turned[:, b % 2, f, :], back_f[:, b % 2, f, :], c["ident"][:, :])
                    m.then_inc(s_tr, 1)


def normalize_all(nc, dve, me, Z, stat, rstd, s_sub, s_sq, ask, mean_scale=1.0 / D):
    me.link(nc.vector.tensor_reduce(stat[:, :], Z[:, :, :], AX.X, ALU.add))
    me.link(nc.vector.tensor_scalar(stat[:, :], stat[:, :], mean_scale, None, ALU.mult))
    nc.vector.tensor_tensor(Z[:, :, :], Z[:, :, :], stat[:, :, None].to_broadcast([P, NW, D]),
                            ALU.subtract).then_inc(s_sub, 1)
    dve.wait_ge(s_sq, 1)
    me.link(nc.vector.tensor_scalar(rstd[:, :], rstd[:, :], mean_scale, EPS, ALU.mult, ALU.add))
    inverse_root(nc, dve, me, rstd[:, :], *ask)


def square_rows(nc, act, Z, junk, rstd, s_sub, s_each, s_sq):
    act.wait_ge(s_sub, 1)

    def rows(k, i, s, first, last):
        if not first:
            act.wait_ge(s_each, k - 1)
        nc.scalar.activation(junk[:, s, :], Z[:, bass.ds(k, 1), :].rearrange("p a d -> p (a d)"), ACT.Square,
                             accum_out=rstd[:, bass.ds(k, 1)]).then_inc(s_each, 1)
    pairs(act, NW, rows)
    act.wait_ge(s_each, NW)
    act.sem_inc(s_sq)


def node_rows(dram, w0, n):
    return dram[w0 * P:(w0 + n) * P, :].rearrange("(w p) d -> p w d", p=P)


def first_norm(nc, c, x, Z, deg, dinv, table):
    with ExitStack() as ctx:
        def sem(name):
            return c["sems"].enter_context(nc.alloc_semaphore("n1_" + name))
        stat = ctx.enter_context(nc.sbuf_tensor("n1_stat", [P, NW], F32))
        rstd = ctx.enter_context(nc.sbuf_tensor("n1_rstd", [P, NW], F32))
        root = ctx.enter_context(nc.sbuf_tensor("n1_root", [P, NW], F32))
        inv = ctx.enter_context(nc.sbuf_tensor("n1_inv", [P, NW], F32))
        junk = ctx.enter_context(nc.sbuf_tensor("n1_junk", [P, 2, D], F32))
        s_ask, s_root = sem("ask"), sem("root")
        s_pad, s_x, s_dve, s_sub, s_each, s_sq, s_z, s_t = (
            sem(n) for n in ("pad", "x", "dve", "sub", "each", "sq", "z", "t"))
        with nc.Block() as block:
            @block.sync
            def _(sp):
                sp.dma_start(Z[:, 0:NW - 1, :], node_rows(x, 0, NW - 1)).then_inc(s_x, 16)
                sp.wait_ge(s_pad, 1)
                sp.dma_start(Z[0:LASTROWS, NW - 1, :], x[(NW - 1) * P:N, :]).then_inc(s_x, 16)
                sp.wait_ge(s_z, 1)
                sp.dma_start(node_rows(table, 0, NW), Z[:, :, :]).then_inc(s_t, 16)
                sp.wait_ge(s_t, 16)

            @block.vector
            def _(dve):
                me = Steps(dve, s_dve)
                nc.vector.memset(Z[:, NW - 1, :], 0.0).then_inc(s_pad, 1)
                me.link(nc.vector.tensor_scalar(dinv[:, :], deg[:, :], 1.0, None, ALU.add))
                inverse_root(nc, dve, me, dinv[:, :], root[:, :], inv[:, :], s_ask, s_root, 1)
                dve.wait_ge(s_x, 32)
                normalize_all(nc, dve, me, Z, stat, rstd, s_sub, s_sq, (root[:, :], inv[:, :], s_ask, s_root, 2))
                me.link(nc.vector.tensor_tensor(rstd[:, :], rstd[:, :], dinv[:, :], ALU.mult))
                nc.vector.tensor_tensor(Z[:, :, :], Z[:, :, :], rstd[:, :, None].to_broadcast([P, NW, D]),
                                        ALU.mult).then_inc(s_z, 1)

            @block.scalar
            def _(act):
                take_root(nc, act, dinv[:, :], root[:, :], s_ask, s_root, 1)
                square_rows(nc, act, Z, junk, rstd, s_sub, s_each, s_sq)
                take_root(nc, act, rstd[:, :], root[:, :], s_ask, s_root, 2)


def convolve(nc, c, ps, tag, table, Z, idx, lo_f, win_row):
    batches = tiles_bound(E_GNN) // GT
    with ExitStack() as ctx:
        def sem(name):
            return c["sems"].enter_context(nc.alloc_semaphore(tag + name))
        ring = ctx.enter_context(nc.sbuf_tensor(tag + "ring", [P, 2, GT], U32))
        got = ctx.enter_context(nc.sbuf_tensor(tag + "got", [P, 2, GT, D], F32))
        hot = ctx.enter_context(nc.sbuf_tensor(tag + "hot", [P, 2, GT, P], F32))
        part = ps[:, 0:4, :].rearrange("p (s b) (j d) -> p s (b j) d", s=2, d=D)
        s_idx, s_hot, s_mm, s_add, s_tick = (sem(n) for n in ("idx", "hot", "mm", "add", "tick"))
        s_got = [sem("got0"), sem("got1")]
        with nc.Block() as block:
            @block.scalar
            def _(act):
                def indices(k, i, s, first, last):
                    if not first:
                        act.wait_ge(s_got[s], i * (16 * GT))
                    nc.scalar.copy(ring[:, s, :], idx[:, bass.ds(k * GT, GT)]).then_inc(s_idx, 1)
                pairs(act, batches, indices)

            @block.gpsimd
            def _(pool):
                def gather(k, i, s, first, last):
                    pool.wait_ge(s_idx, k + 1)
                    pool.sem_inc(s_tick)
                    if not first:
                        pool.wait_ge(s_mm, k - 1)
                        pool.sem_inc(s_tick)
                    for j in range(GT):
                        nc.gpsimd.indirect_dma_start(
                            out=got[:, s, j, :], out_offset=None, in_=table,
                            in_offset=bass.IndirectOffsetOnAxis(ap=ring[:, s, j:j + 1], axis=0),
                            bounds_check=NP - 1, oob_is_err=False).then_inc(s_got[s], 16)
                pairs(pool, batches, gather)

            @block.vector
            def _(dve):
                def one_hot(k, s, first):
                    if not first:
                        dve.wait_ge(s_mm, k - 1)
                    nc.vector.tensor_tensor(hot[:, s, :, :], c["iota_f"][:, None, :].to_broadcast([P, GT, P]),
                                            lo_f[:, bass.ds(k * GT, GT), None].to_broadcast([P, GT, P]),
                                            ALU.is_equal).then_inc(s_hot, 1)

                def add(k, i, s, first, last):
                    if not last:
                        one_hot(k + 1, 1 - s, first and s == 0)
                    wins = window_values(nc, win_row, k * GT, GT, mybir.EngineType.DVE)
                    dve.wait_ge(s_mm, k + 1)
                    for j in range(GT):
                        if not (first and s == 0 and j == 0):
                            dve.wait_ge(s_add, k * GT + j)
                        z = Z[:, bass.ds(wins[j], 1), :]
                        nc.vector.tensor_tensor(z, z, part[:, s, j:j + 1, :], ALU.add).then_inc(s_add, 1)
                one_hot(0, 0, True)
                pairs(dve, batches, add)

            @block.tensor
            def _(pe):
                def product(k, i, s, first, last):
                    pe.wait_ge(s_hot, k + 1)
                    pe.wait_ge(s_got[s], i * (16 * GT) + 16 * GT)
                    if not first:
                        pe.wait_ge(s_add, k * GT - GT)
                    for j in range(GT):
                        m = nc.tensor.matmul(part[:, s, j, :], hot[:, s, j, :], got[:, s, j, :],
                                             start=True, stop=True)
                    m.then_inc(s_mm, 1)
                pairs(pe, batches, product)


def between(nc, c, ps, W1, b1, W2, Z, dinv, table):
    with ExitStack() as ctx:
        def sb(name, shape):
            return ctx.enter_context(nc.sbuf_tensor("m_" + name, shape, F32))


        def sem(name):
            return c["sems"].enter_context(nc.alloc_semaphore("m_" + name))
        w1 = sb("w1", [P, KC, F])
        w1t = sb("w1t", [P, FC, D])
        w2 = sb("w2", [P, FC, D])
        w12 = sb("w12", [P, KC, D])
        b1c = sb("b1c", [P, FC])
        b12 = sb("b12", [1, D])
        zs = sb("zs", [P, 2, D])
        zt = sb("zt", [P, 2, KC, P])
        tp = ps[:, 0:2, 0:D].rearrange("p s (k q) -> p s k q", q=P)
        hp = ps[:, 2:4, :]
        wp, bp = ps[:, 4, :], ps[:, 5, :]
        s_w, s_b, s_wt, s_wc, s_wp, s_w12, s_zs, s_tp, s_zt, s_hp, s_h = (
            sem(n) for n in ("w", "b", "wt", "wc", "wp", "w12", "zs", "tp", "zt", "hp", "h"))
        s_st = [sem("st0"), sem("st1")]
        with nc.Block() as block:
            @block.sync
            def _(sp):
                sp.dma_start(w1[:, :, :], W1.rearrange("(k p) f -> p k f", p=P)).then_inc(s_w, 16)
                sp.dma_start(w2[:, :, :], W2.rearrange("(k p) f -> p k f", p=P)).then_inc(s_w, 16)
                with nc.allow_non_contiguous_dma(reason="one bias vector onto partitions"):
                    sp.dma_start(b1c[:, :], b1.rearrange("(k p) -> p k", p=P)).then_inc(s_b, 16)

                def store(k, i, s, first, last):
                    sp.wait_ge(s_h, k + 1)
                    sp.dma_start(table[bass.ds(k * P, P), :],
                                 Z[:, bass.ds(k, 1), :].rearrange("p a d -> p (a d)")).then_inc(s_st[s], 16)
                pairs(sp, NW, store)
                for s in range(2):
                    sp.wait_ge(s_st[s], 16 * (NW // 2))

            @block.tensor
            def _(pe):
                pe.wait_ge(s_w, 32)
                pe.wait_ge(s_b, 16)
                for f in range(FC):
                    for k in range(KC):
                        n = f * KC + k
                        if n >= 1:
                            pe.wait_ge(s_wc, n)
                        nc.tensor.transpose(wp[:, 0:P], w1[:, k, f * P:(f + 1) * P], c["ident"][:, :]).then_inc(s_wt, 1)
                pe.wait_ge(s_wc, FC * KC)
                for k in range(KC):
                    if k:
                        pe.wait_ge(s_w12, k)
                    for f in range(FC):
                        m = nc.tensor.matmul(wp[:, 0:D], w1t[:, f, k * P:(k + 1) * P], w2[:, f, :],
                                             start=(f == 0), stop=(f == FC - 1))
                    m.then_inc(s_wp, 1)
                for f in range(FC):
                    m = nc.tensor.matmul(bp[0:1, 0:D], b1c[:, f:f + 1], w2[:, f, :], start=(f == 0), stop=(f == FC - 1))
                m.then_inc(s_wp, 1)
                pe.wait_ge(s_w12, KC + 1)

                def turn(k, s, first):
                    pe.wait_ge(s_zs, k + 1)
                    if not first:
                        pe.wait_ge(s_zt, k - 1)
                    for q in range(KC):
                        m = nc.tensor.transpose(tp[:, s, q, :], zs[:, s, q * P:(q + 1) * P], c["ident"][:, :])
                    m.then_inc(s_tp, 1)

                def product(k, i, s, first, last):
                    if not last:
                        turn(k + 1, 1 - s, first and s == 0)
                    pe.wait_ge(s_zt, k + 1)
                    if not first:
                        pe.wait_ge(s_h, k - 1)
                    nc.tensor.matmul(hp[:, s, 0:D], c["ones"][0:1, :], b12[0:1, :], start=True, stop=False)
                    for q in range(KC):
                        m = nc.tensor.matmul(hp[:, s, 0:D], zt[:, s, q, :], w12[:, q, :], start=False, stop=(q == KC - 1))
                    m.then_inc(s_hp, 1)
                turn(0, 0, True)
                pairs(pe, NW, product)

            @block.scalar
            def _(act):
                def copy(k, i, s, first, last):
                    act.wait_ge(s_tp, k + 1)
                    if not first:
                        act.wait_ge(s_hp, k - 1)
                    nc.scalar.copy(zt[:, s, :, :], tp[:, s, :, :]).then_inc(s_zt, 1)
                pairs(act, NW, copy)

            @block.vector
            def _(dve):
                for n in range(FC * KC):
                    f, k = n // KC, n % KC
                    dve.wait_ge(s_wt, n + 1)
                    nc.vector.tensor_copy(w1t[:, f, k * P:(k + 1) * P], wp[:, 0:P]).then_inc(s_wc, 1)
                for k in range(KC):
                    dve.wait_ge(s_wp, k + 1)
                    nc.vector.tensor_copy(w12[:, k, :], wp[:, 0:D]).then_inc(s_w12, 1)
                dve.wait_ge(s_wp, KC + 1)
                nc.vector.tensor_copy(b12[0:1, :], bp[0:1, 0:D]).then_inc(s_w12, 1)

                def scale(k, s, first):
                    if not first:
                        dve.wait_ge(s_tp, k - 1)
                    nc.vector.tensor_tensor(zs[:, s, :], Z[:, bass.ds(k, 1), :].rearrange("p a d -> p (a d)"),
                                            dinv[:, bass.ds(k, 1)].to_broadcast([P, D]), ALU.mult).then_inc(s_zs, 1)

                def finish(k, i, s, first, last):
                    if not last:
                        scale(k + 1, 1 - s, first and s == 0)
                    dve.wait_ge(s_hp, k + 1)
                    nc.vector.tensor_tensor(Z[:, bass.ds(k, 1), :].rearrange("p a d -> p (a d)"), hp[:, s, 0:D],
                                            dinv[:, bass.ds(k, 1)].to_broadcast([P, D]), ALU.mult).then_inc(s_h, 1)
                scale(0, 0, True)
                pairs(dve, NW, finish)


def batch_norm(nc, c, ps, x, b2, gamma, beta, wgat, att_src, att_dst, Z, dinv, x2, xn, heads, adst, table):
    GW = 14
    groups = NW // GW
    with ExitStack() as ctx:
        def sb(name, shape):
            return ctx.enter_context(nc.sbuf_tensor("b_" + name, shape, F32))


        def sem(name):
            return c["sems"].enter_context(nc.alloc_semaphore("b_" + name))
        rows = sb("rows", [P, 3, D])
        atts = sb("atts", [P, 2, HG])
        mean = sb("mean", [P, D])
        scale = sb("scale", [P, D])
        sq = sb("sq", [P, 2, D])
        xg = sb("xg", [P, 2, GW, D])
        stat = sb("stat", [P, NW])
        rstd = sb("rstd", [P, NW])
        wg = sb("wg", [P, KC, HG])
        stage = sb("stage", [P, 2, D])
        root = sb("root", [P, D])
        inv = sb("inv", [P, D])
        s_ask, s_root = sem("ask"), sem("root")
        zt = sb("zt", [P, 2, KC, P])
        prod = sb("prod", [P, NW, HG])
        tp = ps[:, 0:2, 0:D].rearrange("p s (k q) -> p s k q", q=P)
        hp = ps[:, 2:4, :]
        total = ps[:, 4:6, :]
        (s_w, s_dve, s_y, s_cs, s_d, s_sq, s_cs2, s_x2, s_st2, s_xpad, s_sub, s_each, s_all, s_n, s_stn,
         s_tp, s_zt, s_hp, s_h, s_tab, s_stt, s_hsq, s_stage) = (sem(n) for n in (
             "w", "dve", "y", "cs", "d", "sq", "cs2", "x2", "st2", "xpad", "sub", "each", "all", "n", "stn",
             "tp", "zt", "hp", "h", "tab", "stt", "hsq", "stage"))
        s_x = [sem("x0"), sem("x1")]
        with nc.Block() as block:
            @block.sync
            def _(sp):
                for n, v in enumerate((b2, gamma, beta)):
                    sp.dma_start(rows[:, n, :], v.rearrange("(a d) -> a d", a=1).to_broadcast([P, D])).then_inc(s_w, 16)
                for n, v in enumerate((att_src, att_dst)):
                    sp.dma_start(atts[:, n, :], v.rearrange("(a h) e -> a (h e)", a=1).to_broadcast([P, HG])).then_inc(s_w, 16)
                sp.dma_start(wg[:, :, :], wgat.rearrange("(k p) f -> p k f", p=P)).then_inc(s_w, 16)

                sp.wait_ge(s_xpad, 1)

                def load(g):
                    n = GW if g < groups - 1 else GW - 1
                    sp.dma_start(xg[:, g % 2, 0:n, :], node_rows(x, g * GW, n)).then_inc(s_x[g % 2], 16)
                    if g == groups - 1:
                        sp.dma_start(xg[0:LASTROWS, g % 2, n, :], x[(NW - 1) * P:N, :]).then_inc(s_x[g % 2], 16)
                load(0)
                load(1)
                for g in range(groups):
                    sp.wait_ge(s_x2, g + 1)
                    sp.dma_start(node_rows(x2, g * GW, GW), Z[:, g * GW:(g + 1) * GW, :]).then_inc(s_st2, 16)
                    if g + 2 < groups:
                        load(g + 2)
                sp.wait_ge(s_n, 1)
                sp.dma_start(node_rows(xn, 0, NW), Z[:, :, :]).then_inc(s_stn, 16)
                sp.wait_ge(s_tab, 1)
                sp.dma_start(node_rows(table, 0, NW), heads[:, :, :]).then_inc(s_stt, 16)
                sp.wait_ge(s_st2, 16 * groups)
                sp.wait_ge(s_stn, 16)
                sp.wait_ge(s_stt, 16)

            @block.vector
            def _(dve):
                me = Steps(dve, s_dve)

                def spread(v):
                    return v[:, None, :].to_broadcast([P, NW, D])
                nc.vector.memset(xg[:, (groups - 1) % 2, GW - 1, :], 0.0).then_inc(s_xpad, 1)
                dve.wait_ge(s_w, 16 * 6)
                me.link(nc.vector.tensor_tensor(Z[:, :, :], Z[:, :, :], dinv[:, :, None].to_broadcast([P, NW, D]), ALU.mult))
                nc.vector.tensor_tensor(Z[:, :, :], Z[:, :, :], spread(rows[:, 0, :]), ALU.add).then_inc(s_y, 1)
                dve.wait_ge(s_cs, 1)
                me.link(nc.vector.tensor_scalar(mean[:, :], total[:, 0, 0:D], 1.0 / N, None, ALU.mult))
                dve.wait_ge(s_y, 1)
                nc.vector.tensor_tensor(Z[:, :, :], Z[:, :, :], spread(mean), ALU.subtract).then_inc(s_d, 1)
                dve.wait_ge(s_cs2, 1)
                me.link(nc.vector.tensor_scalar(scale[:, :], total[:, 1, 0:D], 1.0 / N, EPS, ALU.mult, ALU.add))
                inverse_root(nc, dve, me, scale[:, :], root[:, :], inv[:, :], s_ask, s_root, 1)
                me.link(nc.vector.tensor_tensor(scale[:, :], scale[:, :], rows[:, 1, :], ALU.mult))
                for g in range(groups):
                    z = Z[:, g * GW:(g + 1) * GW, :]
                    me.link(nc.vector.tensor_tensor(z, z, scale[:, None, :].to_broadcast([P, GW, D]), ALU.mult))
                    me.link(nc.vector.tensor_tensor(z, z, rows[:, 2:3, :].to_broadcast([P, GW, D]), ALU.add))
                    dve.wait_ge(s_x[g % 2], 16 * (g // 2 + 1 + (g == groups - 1)))
                    nc.vector.tensor_tensor(z, z, xg[:, g % 2, :, :], ALU.add).then_inc(s_x2, 1)
                dve.wait_ge(s_x2, groups)
                me.link(nc.vector.tensor_reduce(stat[:, :], Z[:, :, :], AX.X, ALU.add))
                me.link(nc.vector.tensor_scalar(stat[:, :], stat[:, :], 1.0 / D, None, ALU.mult))
                dve.wait_ge(s_st2, 16 * groups)
                nc.vector.tensor_tensor(Z[:, :, :], Z[:, :, :], stat[:, :, None].to_broadcast([P, NW, D]),
                                        ALU.subtract).then_inc(s_sub, 1)
                dve.wait_ge(s_all, 1)
                me.link(nc.vector.tensor_scalar(rstd[:, :], rstd[:, :], 1.0 / D, EPS, ALU.mult, ALU.add))
                inverse_root(nc, dve, me, rstd[:, :], root[:, 0:NW], inv[:, 0:NW], s_ask, s_root, 2)
                nc.vector.tensor_tensor(Z[:, :, :], Z[:, :, :], rstd[:, :, None].to_broadcast([P, NW, D]),
                                        ALU.mult).then_inc(s_n, 1)

                dve.wait_ge(s_n, 1)

                def put(k, s, first):
                    if not first:
                        dve.wait_ge(s_tp, k - 1)
                    nc.vector.tensor_copy(stage[:, s, None, :], Z[:, bass.ds(k, 1), :]).then_inc(s_stage, 1)

                def keep(k, i, s, first, last):
                    if not last:
                        put(k + 1, 1 - s, first and s == 0)
                    dve.wait_ge(s_hp, k + 1)
                    nc.vector.tensor_copy(heads[:, bass.ds(k, 1), 0:HG], hp[:, s, None, 0:HG]).then_inc(s_h, 1)
                put(0, 0, True)
                pairs(dve, NW, keep)
                dve.wait_ge(s_h, NW)
                for n, to in ((0, heads[:, :, HG:ROW]), (1, adst[:, :, :])):
                    me.link(nc.vector.tensor_tensor(prod[:, :, :], heads[:, :, 0:HG],
                                                    atts[:, n:n + 1, :].to_broadcast([P, NW, HG]), ALU.mult))
                    me.link(nc.vector.tensor_reduce(to, prod[:, :, :].rearrange("p w (h e) -> p w h e", e=NE), AX.X, ALU.add))
                dve.sem_inc(s_tab)

            @block.scalar
            def _(act):
                def square(k, i, s, first, last):
                    if not first:
                        act.wait_ge(s_hsq, k - 1)
                    nc.scalar.activation(sq[:, s, :], Z[:, bass.ds(k, 1), :].rearrange("p a d -> p (a d)"),
                                         ACT.Square).then_inc(s_sq, 1)
                act.wait_ge(s_d, 1)
                pairs(act, NW, square)
                take_root(nc, act, scale[:, :], root[:, :], s_ask, s_root, 1)
                square_rows(nc, act, Z, sq, rstd, s_sub, s_each, s_all)
                take_root(nc, act, rstd[:, :], root[:, 0:NW], s_ask, s_root, 2)

                def copy(k, i, s, first, last):
                    act.wait_ge(s_tp, k + 1)
                    if not first:
                        act.wait_ge(s_hp, k - 1)
                    nc.scalar.copy(zt[:, s, :, :], tp[:, s, :, :]).then_inc(s_zt, 1)
                pairs(act, NW, copy)

            @block.tensor
            def _(pe):
                pe.wait_ge(s_y, 1)
                nc.tensor.matmul(total[:, 0, 0:D], c["ones"][0:LASTROWS, :], Z[0:LASTROWS, NW - 1, :], start=True, stop=False)
                with pe.Fori(0, NW - 2) as k:
                    nc.tensor.matmul(total[:, 0, 0:D], c["ones"][:, :], Z[:, bass.ds(k, 1), :].rearrange("p a d -> p (a d)"),
                                     start=False, stop=False)
                nc.tensor.matmul(total[:, 0, 0:D], c["ones"][:, :], Z[:, NW - 2, :], start=False, stop=True).then_inc(s_cs, 1)

                def squares(k, i, s, first, last):
                    pe.wait_ge(s_sq, k + 1)
                    n = LASTROWS if last else P
                    nc.tensor.matmul(total[:, 1, 0:D], c["ones"][0:n, :], sq[0:n, s, :],
                                     start=first and s == 0, stop=last).then_inc(s_hsq, 1)
                pairs(pe, NW, squares)
                pe.wait_ge(s_hsq, NW)
                pe.sem_inc(s_cs2)

                def turn(k, s, first):
                    pe.wait_ge(s_stage, k + 1)
                    if not first:
                        pe.wait_ge(s_zt, k - 1)
                    for q in range(KC):
                        m = nc.tensor.transpose(tp[:, s, q, :], stage[:, s, q * P:(q + 1) * P], c["ident"][:, :])
                    m.then_inc(s_tp, 1)

                def product(k, i, s, first, last):
                    if not last:
                        turn(k + 1, 1 - s, first and s == 0)
                    pe.wait_ge(s_zt, k + 1)
                    if not first:
                        pe.wait_ge(s_h, k - 1)
                    for q in range(KC):
                        m = nc.tensor.matmul(hp[:, s, 0:HG], zt[:, s, q, :], wg[:, q, :], start=(q == 0), stop=(q == KC - 1))
                    m.then_inc(s_hp, 1)
                turn(0, 0, True)
                pairs(pe, NW, product)


def attention_max(nc, c, ps, table, idx, lo_f, win_row, H, top):
    batches = tiles_bound(E_FFN) // GT
    with ExitStack() as ctx:
        def sb(name, shape, dt):
            return ctx.enter_context(nc.sbuf_tensor("a_" + name, shape, dt))

        def sem(name):
            return c["sems"].enter_context(nc.alloc_semaphore("a_" + name))
        ring = sb("ring", [P, 2, GT], U32)
        got = sb("got", [P, 2, GT, ROW], F32)
        parts = sb("parts", [P, 2, GT, 2, HEADS], BF16)
        turned = sb("turned", [2 * HEADS, 2, GT, P], BF16)
        hot = sb("hot", [P, 2, GT, P], BF16)
        other = sb("other", [P, 2, GT, P], BF16)
        most = sb("most", [P, 2, GT, HEADS], F32)
        term = ps[:, 0:GT, :].rearrange("p j (h q) -> p j h q", q=P)
        tp = ps[0:2 * HEADS, 4:6, :].bitcast(BF16)[:, :, 0:GT * P].rearrange("p s (j q) -> p s j q", q=P)
        s_idx, s_hi, s_parts, s_eq, s_hot, s_tp, s_turned, s_term, s_most, s_top, s_keep, s_tick = (
            sem(n) for n in ("idx", "hi", "parts", "eq", "hot", "tp", "turned", "term", "most", "top", "keep", "tick"))
        s_got = [sem("got0"), sem("got1")]
        with nc.Block() as block:
            @block.scalar
            def _(act):
                def rows(k, i, s, first, last):
                    if not first:
                        act.wait_ge(s_got[s], i * (16 * GT))
                    nc.scalar.copy(ring[:, s, :], idx[:, bass.ds(k * GT, GT)]).then_inc(s_idx, 1)

                def keep(k, i, s, first, last):
                    if not last:
                        rows(k + 1, i + s, 1 - s, first and s == 0, False)
                    act.wait_ge(s_got[s], i * (16 * GT) + 16 * GT)
                    nc.scalar.copy(H[:, bass.ds(k * GT, GT), :], got[:, s, :, :]).then_inc(s_keep, 1)
                    act.wait_ge(s_tp, k + 1)
                    if not first:
                        act.wait_ge(s_term, k * GT - GT)
                    nc.scalar.copy(turned[:, s, :, :], tp[:, s, :, :]).then_inc(s_turned, 1)
                rows(0, 0, 0, True, False)
                pairs(act, batches, keep)

            @block.gpsimd
            def _(pool):
                def gather(k, i, s, first, last):
                    pool.wait_ge(s_idx, k + 1)
                    pool.sem_inc(s_tick)
                    if not first:
                        pool.wait_ge(s_keep, k - 1)
                        pool.sem_inc(s_tick)
                        pool.wait_ge(s_parts, k - 1)
                        pool.sem_inc(s_tick)
                    for j in range(GT):
                        nc.gpsimd.indirect_dma_start(
                            out=got[:, s, j, :], out_offset=None, in_=table,
                            in_offset=bass.IndirectOffsetOnAxis(ap=ring[:, s, j:j + 1], axis=0),
                            bounds_check=NP - 1, oob_is_err=False).then_inc(s_got[s], 16)
                pairs(pool, batches, gather)

            @block.vector
            def _(dve):
                def one_hot(k, s, first):
                    if not first:
                        dve.wait_ge(s_term, k * GT - GT)
                    nc.vector.tensor_tensor(hot[:, s, :, :], c["iota_b"][:, None, :].to_broadcast([P, GT, P]),
                                            lo_f[:, bass.ds(k * GT, GT), None].to_broadcast([P, GT, P]),
                                            ALU.is_equal).then_inc(s_eq, 1)
                    dve.wait_ge(s_eq, k + 1)
                    nc.vector.tensor_scalar(other[:, s, :, :], hot[:, s, :, :], -1.0, BIG, ALU.add,
                                            ALU.mult).then_inc(s_hot, 1)

                def split(k, i, s, first):
                    dve.wait_ge(s_got[s], i * (16 * GT) + 16 * GT)
                    if not first:
                        dve.wait_ge(s_tp, k - 1)
                    nc.vector.tensor_copy(parts[:, s, :, 0, :], got[:, s, :, HG:ROW]).then_inc(s_hi, 1)
                    dve.wait_ge(s_hi, k + 1)
                    nc.vector.tensor_tensor(parts[:, s, :, 1, :], got[:, s, :, HG:ROW], parts[:, s, :, 0, :],
                                            ALU.subtract).then_inc(s_parts, 1)

                def largest(k, i, s, first, last):
                    if not last:
                        one_hot(k + 1, 1 - s, first and s == 0)
                    split(k, i, s, first)
                    wins = window_values(nc, win_row, k * GT, GT, mybir.EngineType.DVE)
                    for j in range(GT):
                        dve.wait_ge(s_term, k * GT + j + 1)
                        nc.vector.tensor_reduce(most[:, s, j, :], term[:, j, :, :], AX.X, ALU.max).then_inc(s_most, 1)
                    for j in range(GT):
                        dve.wait_ge(s_most, k * GT + j + 1)
                        if not (first and s == 0 and j == 0):
                            dve.wait_ge(s_top, k * GT + j)
                        t = top[:, bass.ds(wins[j], 1), :]
                        nc.vector.tensor_tensor(t, t, most[:, s, j:j + 1, :], ALU.max).then_inc(s_top, 1)
                one_hot(0, 0, True)
                pairs(dve, batches, largest)

            @block.tensor
            def _(pe):
                def product(k, i, s, first, last):
                    pe.wait_ge(s_parts, k + 1)
                    if not first:
                        pe.wait_ge(s_turned, k - 1)
                    for j in range(GT):
                        m = nc.tensor.transpose(tp[:, s, j, :], parts[:, s, j, :, :].rearrange("p a h -> p (a h)"),
                                                c["ident_b"][:, :])
                    m.then_inc(s_tp, 1)
                    pe.wait_ge(s_hot, k + 1)
                    pe.wait_ge(s_turned, k + 1)
                    for j in range(GT):
                        if not (first and s == 0):
                            pe.wait_ge(s_most, k * GT - GT + j + 1)
                        nc.tensor.matmul(term[:, j, :, :], other[:, s, j, :],
                                         c["ident_b"][:, None, :].to_broadcast([P, HEADS, P]), start=True, stop=False)
                        for h in range(HEADS):
                            m = nc.tensor.matmul(term[:, j, h, :], c["pick"][:, h, :], turned[:, s, j, :],
                                                 start=False, stop=(h == HEADS - 1))
                        m.then_inc(s_term, 1)
                pairs(pe, batches, product)


def attention_sums(nc, c, ps, H, lo_f, win_row, node, sums):
    batches = tiles_bound(E_FFN) // GT
    with ExitStack() as ctx:
        def sb(name, shape):
            return ctx.enter_context(nc.sbuf_tensor("s_" + name, shape, F32))


        def sem(name):
            return c["sems"].enter_context(nc.alloc_semaphore("s_" + name))
        hot = sb("hot", [P, 2, GT, P])
        turned = sb("turned", [P, 2, GT, P])
        edge = sb("edge", [P, GT, HEADS])
        steep = sb("steep", [P, GT, HEADS])
        expo = sb("expo", [P, 2, GT, HEADS])
        msg = sb("msg", [P, 2, GT, ROW])
        tp = ps[:, 0:2, :].rearrange("p s (j q) -> p s j q", q=P)
        at = ps[:, 2:4, :]
        part = ps[:, 4:6, :]
        s_hot, s_tp, s_turned, s_at, s_e, s_x, s_ee, s_msg, s_part, s_sum = (
            sem(n) for n in ("hot", "tp", "turned", "at", "e", "x", "ee", "msg", "part", "sum"))

        def at_of(s):
            return at[:, s, 0:GT * 2 * HEADS].rearrange("p (j a h) -> p j a h", a=2, h=HEADS)

        def part_of(s):
            return part[:, s, 0:GT * ROW].rearrange("p (j r) -> p j r", r=ROW)
        with nc.Block() as block:
            @block.vector
            def _(dve):
                def one_hot(k, s, first):
                    if not first:
                        dve.wait_ge(s_part, k - 1)
                    nc.vector.tensor_tensor(hot[:, s, :, :], c["iota_f"][:, None, :].to_broadcast([P, GT, P]),
                                            lo_f[:, bass.ds(k * GT, GT), None].to_broadcast([P, GT, P]),
                                            ALU.is_equal).then_inc(s_hot, 1)

                def weigh(k, i, s, first, last):
                    if not last:
                        one_hot(k + 1, 1 - s, first and s == 0)
                    dve.wait_ge(s_at, k + 1)
                    nc.vector.tensor_tensor(edge[:, :, :], H[:, bass.ds(k * GT, GT), HG:ROW], at_of(s)[:, :, 0, :],
                                            ALU.add).then_inc(s_e, 1)
                    dve.wait_ge(s_e, k * 3 + 1)
                    nc.vector.scalar_tensor_tensor(steep[:, :, :], edge[:, :, :], 0.2, edge[:, :, :], ALU.mult,
                                                   ALU.max).then_inc(s_e, 1)
                    dve.wait_ge(s_e, k * 3 + 2)
                    nc.vector.tensor_tensor(edge[:, :, :], steep[:, :, :], at_of(s)[:, :, 1, :],
                                            ALU.subtract).then_inc(s_e, 1)
                    dve.wait_ge(s_e, k * 3 + 3)
                    if not first:
                        dve.wait_ge(s_ee, k - 1)
                    nc.vector.tensor_scalar(expo[:, s, :, :], edge[:, :, :], 60.0, None, ALU.min).then_inc(s_x, 1)
                    dve.wait_ge(s_ee, k + 1)
                    nc.vector.tensor_tensor(
                        msg[:, s, :, 0:HG].rearrange("p j (h e) -> p j h e", e=NE),
                        H[:, bass.ds(k * GT, GT), 0:HG].rearrange("p j (h e) -> p j h e", e=NE),
                        msg[:, s, :, HG:ROW, None].to_broadcast([P, GT, HEADS, NE]), ALU.mult).then_inc(s_msg, 1)
                    wins = window_values(nc, win_row, k * GT, GT, mybir.EngineType.DVE)
                    dve.wait_ge(s_part, k + 1)
                    for j in range(GT):
                        if not (first and s == 0 and j == 0):
                            dve.wait_ge(s_sum, k * GT + j)
                        t = sums[:, bass.ds(wins[j], 1), :]
                        nc.vector.tensor_tensor(t, t, part_of(s)[:, j:j + 1, :], ALU.add).then_inc(s_sum, 1)
                one_hot(0, 0, True)
                pairs(dve, batches, weigh)

            @block.scalar
            def _(act):
                def copy(k, i, s, first, last):
                    act.wait_ge(s_tp, k + 1)
                    if not first:
                        act.wait_ge(s_at, k - 1)
                    nc.scalar.copy(turned[:, s, :, :], tp[:, s, :, :]).then_inc(s_turned, 1)
                    act.wait_ge(s_x, k + 1)
                    if not first:
                        act.wait_ge(s_part, k - 1)
                    nc.scalar.activation(msg[:, s, :, HG:ROW], expo[:, s, :, :], ACT.Exp).then_inc(s_ee, 1)
                pairs(act, batches, copy)

            @block.tensor
            def _(pe):
                def product(k, i, s, first, last):
                    pe.wait_ge(s_hot, k + 1)
                    if not first:
                        pe.wait_ge(s_turned, k - 1)
                    for j in range(GT):
                        m = nc.tensor.transpose(tp[:, s, j, :], hot[:, s, j, :], c["ident"][:, :])
                    m.then_inc(s_tp, 1)
                    wins = window_values(nc, win_row, k * GT, GT, mybir.EngineType.PE)
                    pe.wait_ge(s_turned, k + 1)
                    if not first:
                        pe.wait_ge(s_x, k - 1)
                    for j in range(GT):
                        m = nc.tensor.matmul(at_of(s)[:, j, :, :].rearrange("p a h -> p (a h)"), turned[:, s, j, :],
                                             node[:, bass.ds(wins[j], 1), :].rearrange("p a h -> p (a h)"),
                                             start=True, stop=True)
                    m.then_inc(s_at, 1)
                    pe.wait_ge(s_msg, k + 1)
                    if not first:
                        pe.wait_ge(s_sum, k * GT - GT)
                    for j in range(GT):
                        m = nc.tensor.matmul(part_of(s)[:, j, :], hot[:, s, j, :], msg[:, s, j, :], start=True, stop=True)
                    m.then_inc(s_part, 1)
                pairs(pe, batches, product)


def start_maxima(nc, heads, top):
    with nc.Block() as block:
        @block.vector
        def _(dve):
            nc.vector.tensor_copy(top[:, :, :], heads[:, :, HG:ROW])


def node_maxima(nc, c, top, adst, heads, node, sums):
    with ExitStack() as ctx:
        raw = ctx.enter_context(nc.sbuf_tensor("x_raw", [P, NW, HEADS], F32))
        loop = ctx.enter_context(nc.sbuf_tensor("x_loop", [P, NW, HEADS], F32))
        s_dve = c["sems"].enter_context(nc.alloc_semaphore("x_dve"))
        s_e = c["sems"].enter_context(nc.alloc_semaphore("x_e"))
        s_x = c["sems"].enter_context(nc.alloc_semaphore("x_x"))
        with nc.Block() as block:
            @block.vector
            def _(dve):
                me = Steps(dve, s_dve)
                me.link(nc.vector.tensor_copy(node[:, :, 0:HEADS], adst[:, :, :]))
                me.link(nc.vector.tensor_tensor(raw[:, :, :], top[:, :, :], adst[:, :, :], ALU.add))
                me.link(nc.vector.scalar_tensor_tensor(node[:, :, HEADS:2 * HEADS], raw[:, :, :], 0.2, raw[:, :, :],
                                                       ALU.mult, ALU.max))
                me.link(nc.vector.tensor_tensor(raw[:, :, :], heads[:, :, HG:ROW], adst[:, :, :], ALU.add))
                me.link(nc.vector.scalar_tensor_tensor(loop[:, :, :], raw[:, :, :], 0.2, raw[:, :, :], ALU.mult, ALU.max))
                me.link(nc.vector.tensor_tensor(raw[:, :, :], loop[:, :, :], node[:, :, HEADS:2 * HEADS], ALU.subtract))
                dve.sem_inc(s_e)
                dve.wait_ge(s_x, 1)
                nc.vector.tensor_tensor(sums[:, :, 0:HG].rearrange("p w (h e) -> p w h e", e=NE),
                                        heads[:, :, 0:HG].rearrange("p w (h e) -> p w h e", e=NE),
                                        sums[:, :, HG:ROW, None].to_broadcast([P, NW, HEADS, NE]), ALU.mult)

            @block.scalar
            def _(act):
                act.wait_ge(s_e, 1)
                nc.scalar.activation(sums[:, :, HG:ROW], raw[:, :, :], ACT.Exp).then_inc(s_x, 1)


def gates_of(nc, c, sums, b_gat, ln_gamma, ln_beta, gates):
    with ExitStack() as ctx:
        def sb(name, shape):
            return ctx.enter_context(nc.sbuf_tensor("g_" + name, shape, F32))
        vecs = sb("vecs", [P, 3, HG])
        den = sb("den", [P, NW, HEADS])
        agg = sb("agg", [P, NW, HG])
        sq = sb("sq", [P, NW, HG])
        one = sb("one", [P, NW])
        two = sb("two", [P, NW])
        root = sb("root", [P, NW])
        inv = sb("inv", [P, NW])
        s_ask = c["sems"].enter_context(nc.alloc_semaphore("g_ask"))
        s_root = c["sems"].enter_context(nc.alloc_semaphore("g_root"))
        score = sb("score", [P, NW, NE])
        rank = sb("rank", [P, NW, NE])
        gap = sb("gap", [P, NW, NE])
        s_w = c["sems"].enter_context(nc.alloc_semaphore("g_w"))
        s_dve = c["sems"].enter_context(nc.alloc_semaphore("g_dve"))
        s_e = c["sems"].enter_context(nc.alloc_semaphore("g_e"))
        s_x = c["sems"].enter_context(nc.alloc_semaphore("g_x"))
        with nc.Block() as block:
            @block.sync
            def _(sp):
                for n, v in enumerate((b_gat, ln_gamma, ln_beta)):
                    sp.dma_start(vecs[:, n, :], v.rearrange("(a h) -> a h", a=1).to_broadcast([P, HG])).then_inc(s_w, 16)

            @block.vector
            def _(dve):
                me = Steps(dve, s_dve)
                v = nc.vector

                def spread(x, n):
                    return x[:, :, None].to_broadcast([P, NW, n])
                me.link(v.tensor_scalar(den[:, :, :], sums[:, :, HG:ROW], 1e-16, None, ALU.add))
                me.link(v.reciprocal(den[:, :, :], den[:, :, :]))
                me.link(v.tensor_tensor(agg[:, :, :].rearrange("p w (h e) -> p w h e", e=NE),
                                        sums[:, :, 0:HG].rearrange("p w (h e) -> p w h e", e=NE),
                                        den[:, :, :, None].to_broadcast([P, NW, HEADS, NE]), ALU.mult))
                dve.wait_ge(s_w, 48)
                me.link(v.tensor_tensor(agg[:, :, :], agg[:, :, :], vecs[:, 0:1, :].to_broadcast([P, NW, HG]), ALU.add))
                me.link(v.tensor_reduce(one[:, :], agg[:, :, :], AX.X, ALU.add))
                me.link(v.tensor_scalar(one[:, :], one[:, :], 1.0 / HG, None, ALU.mult))
                me.link(v.tensor_tensor(agg[:, :, :], agg[:, :, :], spread(one, HG), ALU.subtract))
                me.link(v.tensor_tensor(sq[:, :, :], agg[:, :, :], agg[:, :, :], ALU.mult))
                me.link(v.tensor_reduce(two[:, :], sq[:, :, :], AX.X, ALU.add))
                me.link(v.tensor_scalar(two[:, :], two[:, :], 1.0 / HG, EPS, ALU.mult, ALU.add))
                inverse_root(nc, dve, me, two[:, :], root[:, :], inv[:, :], s_ask, s_root, 1)
                me.link(v.tensor_tensor(agg[:, :, :], agg[:, :, :], spread(two, HG), ALU.mult))
                me.link(v.tensor_tensor(agg[:, :, :], agg[:, :, :], vecs[:, 1:2, :].to_broadcast([P, NW, HG]), ALU.mult))
                me.link(v.tensor_tensor(agg[:, :, :], agg[:, :, :], vecs[:, 2:3, :].to_broadcast([P, NW, HG]), ALU.add))
                me.link(v.tensor_reduce(score[:, :, :], agg[:, :, :].rearrange("p w (h e) -> p w e h", e=NE), AX.X, ALU.add))
                me.link(v.tensor_scalar(score[:, :, :], score[:, :, :], 1.0 / HEADS, None, ALU.mult))
                for e in range(NE):
                    others = [j for j in range(NE) if j != e]
                    for n, j in enumerate(others):
                        op = ALU.is_ge if j < e else ALU.is_gt
                        to = rank[:, :, e] if n == 0 else one[:, :]
                        me.link(v.tensor_tensor(to, score[:, :, j], score[:, :, e], op))
                        if n:
                            me.link(v.tensor_tensor(rank[:, :, e], rank[:, :, e], one[:, :], ALU.add))
                me.link(v.tensor_reduce(two[:, :], score[:, :, :], AX.X, ALU.max))
                me.link(v.tensor_tensor(gap[:, :, :], score[:, :, :], spread(two, NE), ALU.subtract))
                dve.sem_inc(s_e)
                dve.wait_ge(s_x, 1)
                me.link(v.tensor_scalar(rank[:, :, :], rank[:, :, :], 1.5, None, ALU.is_lt))
                me.link(v.tensor_tensor(gates[:, :, :], gates[:, :, :], rank[:, :, :], ALU.mult))
                me.link(v.tensor_reduce(one[:, :], gates[:, :, :], AX.X, ALU.add))
                me.link(v.reciprocal(one[:, :], one[:, :]))
                me.link(v.tensor_tensor(gates[:, :, :], gates[:, :, :], spread(one, NE), ALU.mult))

            @block.scalar
            def _(act):
                take_root(nc, act, two[:, :], root[:, :], s_ask, s_root, 1)
                act.wait_ge(s_e, 1)
                nc.scalar.activation(gates[:, :, :], gap[:, :, :], ACT.Exp).then_inc(s_x, 1)


def experts(nc, c, ps, x2, xn, W1, b1, W2, b2, gates, out):
    T = 2
    groups = NW // T
    with ExitStack() as ctx:
        def sb(name, shape):
            return ctx.enter_context(nc.sbuf_tensor("e_" + name, shape, F32))


        def sem(name):
            return c["sems"].enter_context(nc.alloc_semaphore("e_" + name))
        w1 = sb("w1", [P, NE, KC, F])
        w2 = sb("w2", [P, NE, FC, D])
        b1c = sb("b1c", [P, NE, FC])
        b2r = sb("b2r", [NE, D])
        xin = sb("xin", [P, 2, T, D])
        res = sb("res", [P, 2, T, D])
        xt = sb("xt", [P, 2, KC, T, P])
        gs = sb("gs", [P, 2, T, NE])
        gt = sb("gt", [NE, 2, T, P])
        hid = sb("hid", [P, 2, FC, T, P])
        up = ps[:, 0:2, :].rearrange("p g (a t q) -> p g a t q", a=2, t=T)
        yp = ps[:, 2:4, :].rearrange("p g (t d) -> p g t d", t=T)
        yb = ps[:, 4, :].rearrange("p (t d) -> p t d", t=T)
        tp = ps[:, 5, :].rearrange("p (k t q) -> p k t q", k=KC, t=T)
        gp = ps[0:NE, 6, 0:T * P].rearrange("p (t q) -> p t q", q=P)
        s_w = sem("w")
        s_in = [sem("in0"), sem("in1")]
        s_res = [sem("res0"), sem("res1")]
        s_gs, s_tp, s_xt, s_up, s_hid, s_y, s_acc, s_st = (
            sem(n) for n in ("gs", "tp", "xt", "up", "hid", "y", "acc", "st"))
        s_out = [sem("out0"), sem("out1")]
        NA = NE + 1
        with nc.Block() as block:
            @block.sync
            def _(sp):
                sp.dma_start(w1[:, :, :, :], W1.rearrange("e (k p) f -> p e k f", p=P)).then_inc(s_w, 16)
                sp.dma_start(w2[:, :, :, :], W2.rearrange("e (k p) d -> p e k d", p=P)).then_inc(s_w, 16)
                sp.dma_start(b2r[:, :], b2).then_inc(s_w, 16)
                with nc.allow_non_contiguous_dma(reason="bias vectors onto partitions"):
                    sp.dma_start(b1c[:, :, :], b1.rearrange("e (k p) -> p e k", p=P)).then_inc(s_w, 16)

                def load(k, i, s, first, last):
                    if not first:
                        sp.wait_ge(s_tp, k - 1)
                    rows = bass.ds(k * (T * P), T * P)
                    sp.dma_start(xin[:, s, :, :], xn[rows, :].rearrange("(t p) d -> p t d", p=P)).then_inc(s_in[s], 16)
                    if not first:
                        sp.wait_ge(s_out[s], i * 16)
                    sp.dma_start(res[:, s, :, :], x2[rows, :].rearrange("(t p) d -> p t d", p=P)).then_inc(s_res[s], 16)
                pairs(sp, groups, load)

            @block.gpsimd
            def _(pool):
                def store(k, i, s, first, last):
                    pool.wait_ge(s_acc, k * NA + NA)
                    pool.sem_inc(s_st)
                    if last:
                        pool.dma_start(out[k * T * P:(NW - 1) * P, :], res[:, s, 0, :]).then_inc(s_out[s], 16)
                        pool.dma_start(out[(NW - 1) * P:N, :], res[0:LASTROWS, s, 1, :]).then_inc(s_out[s], 16)
                    else:
                        pool.dma_start(out[bass.ds(k * (T * P), T * P), :].rearrange("(t p) d -> p t d", p=P),
                                       res[:, s, :, :]).then_inc(s_out[s], 16)
                pairs(pool, groups, store)
                pool.wait_ge(s_out[0], 16 * ((groups + 1) // 2) + (16 if groups % 2 else 0))
                pool.wait_ge(s_out[1], 16 * (groups // 2) + (0 if groups % 2 else 16))

            @block.tensor
            def _(pe):
                def product(k, i, s, first, last):
                    pe.wait_ge(s_in[s], i * 16 + 16)
                    pe.wait_ge(s_gs, k + 1)
                    if not (first and s == 0):
                        pe.wait_ge(s_xt, k)
                    for t in range(T):
                        for q in range(KC):
                            nc.tensor.transpose(tp[:, q, t, :], xin[:, s, t, q * P:(q + 1) * P], c["ident"][:, :])
                        m = nc.tensor.transpose(gp[:, t, :], gs[:, s, t, :], c["ident"][:, :])
                    m.then_inc(s_tp, 1)
                    if first and s == 0:
                        pe.wait_ge(s_w, 64)
                    pe.wait_ge(s_xt, k + 1)
                    if not (first and s == 0):
                        pe.wait_ge(s_acc, k * NA - NA + 1)
                    for t in range(T):
                        m = nc.tensor.matmul(yb[:, t, :], gt[:, s, t, :], b2r[:, :], start=True, stop=True)
                    m.then_inc(s_y, 1)

                    def up_of(e):
                        for g in range(2):
                            n = e * 2 + g
                            if not (first and s == 0 and n < 2):
                                pe.wait_ge(s_hid, k * (2 * NE) + n - 1)
                            for a in range(2):
                                f = g * 2 + a
                                for q in range(KC):
                                    m = nc.tensor.matmul(up[:, g, a, :, :], w1[:, e, q, f * P:(f + 1) * P],
                                                         xt[:, s, q, :, :], start=(q == 0), stop=(q == KC - 1))
                            m.then_inc(s_up, 1)

                    def down_of(e):
                        pe.wait_ge(s_hid, k * (2 * NE) + 2 * e + 2)
                        if not (first and s == 0 and e < 2):
                            pe.wait_ge(s_acc, k * NA + e if e >= 2 else k * NA - NA + NE + e)
                        for t in range(T):
                            for f in range(FC):
                                m = nc.tensor.matmul(yp[:, e % 2, t, :], hid[:, e % 2, f, t, :], w2[:, e, f, :],
                                                     start=(f == 0), stop=(f == FC - 1))
                        m.then_inc(s_y, 1)
                    up_of(0)
                    for e in range(NE):
                        if e + 1 < NE:
                            up_of(e + 1)
                        down_of(e)
                pairs(pe, groups, product)

            @block.scalar
            def _(act):
                def act_group(k, i, s, first, last):
                    for e in range(NE):
                        for g in range(2):
                            n = e * 2 + g
                            act.wait_ge(s_up, k * (2 * NE) + n + 1)
                            if not (first and s == 0 and e < 2):
                                act.wait_ge(s_y, k * NA + e if e >= 2 else k * NA - NA + NE + e)
                            for a in range(2):
                                f = g * 2 + a
                                m = nc.scalar.activation(hid[:, e % 2, f, :, :], up[:, g, a, :, :], ACT.Gelu,
                                                         bias=b1c[:, e, f:f + 1])
                            m.then_inc(s_hid, 1)
                pairs(act, groups, act_group)

            @block.vector
            def _(dve):
                def sum_group(k, i, s, first, last):
                    if not first:
                        dve.wait_ge(s_tp, k - 1)
                    nc.vector.tensor_copy(gs[:, s, :, :], gates[:, bass.ds(k * T, T), :]).then_inc(s_gs, 1)
                    dve.wait_ge(s_tp, k + 1)
                    nc.vector.tensor_copy(xt[:, s, :, :, :], tp[:, :, :, :])
                    nc.vector.tensor_copy(gt[:, s, :, :], gp[:, :, :]).then_inc(s_xt, 1)
                    dve.wait_ge(s_res[s], i * 16 + 16)
                    dve.wait_ge(s_y, k * NA + 1)
                    nc.vector.tensor_tensor(res[:, s, :, :], res[:, s, :, :], yb[:, :, :], ALU.add).then_inc(s_acc, 1)
                    for e in range(NE):
                        dve.wait_ge(s_y, k * NA + e + 2)
                        dve.wait_ge(s_acc, k * NA + e + 1)
                        for t in range(T):
                            m = nc.vector.scalar_tensor_tensor(res[:, s, t, :], yp[:, e % 2, t, :], gs[:, s, t, e:e + 1],
                                                               res[:, s, t, :], ALU.mult, ALU.add)
                        m.then_inc(s_acc, 1)
                pairs(dve, groups, sum_group)


def gnn_ffn(nc, x, src, dst, gW1, gb1, gW2, gb2, ggamma, gbeta, wgat, att_src, att_dst, b_gat, ln_gamma, ln_beta,
            fW1, fb1, fW2, fb2, edge_index, out):
    def dram(name, shape, dt=F32):
        return nc.dram_tensor(name, shape, dt, kind="Internal").ap()
    gnn_slots, ffn_slots = blocks_bound(E_GNN), blocks_bound(E_FFN)
    gnn_list = dram("gnn_list", [gnn_slots * P, 2], I32)
    ffn_list = dram("ffn_list", [ffn_slots * P, 2], I32)
    rows1 = dram("rows1", [NP, D])
    rows2 = dram("rows2", [NP, D])
    x2 = dram("x2", [NP, D])
    xn = dram("xn", [NP, D])
    rows3 = dram("rows3", [NP, ROW])
    with ExitStack() as ctx:
        def sb(name, shape, dt=F32):
            return ctx.enter_context(nc.sbuf_tensor(name, shape, dt))
        c = make_consts(nc, ctx, Signals(nc))
        ps = ctx.enter_context(nc.psum_tensor("ps", [P, 8, BANK], F32))
        ffn_idx = sb("ffn_idx", [P, ffn_slots], U32)
        ffn_lo = sb("ffn_lo", [P, ffn_slots])
        ffn_win = sb("ffn_win", [1, ffn_slots], I32)
        heads = sb("heads", [P, NW, ROW])
        adst = sb("adst", [P, NW, HEADS])
        with ExitStack() as gctx:
            def gsb(name, shape, dt=F32):
                return gctx.enter_context(nc.sbuf_tensor(name, shape, dt))
            gnn_idx = gsb("gnn_idx", [P, gnn_slots], U32)
            gnn_lo = gsb("gnn_lo", [P, gnn_slots])
            gnn_win = gsb("gnn_win", [1, gnn_slots], I32)
            deg = gsb("deg", [P, NW])
            deg_ffn = gsb("deg_ffn", [P, NW])
            dinv = gsb("dinv", [P, NW])
            bin_edges(nc, c, ps, "p_", E_GNN, src, dst, gnn_list, gnn_idx, gnn_lo, gnn_win, deg)
            c["sems"].give_back()
            bin_edges(nc, c, ps, "q_", E_FFN, edge_index[0], edge_index[1], ffn_list, ffn_idx, ffn_lo, ffn_win, deg_ffn)
            c["sems"].give_back()
            with nc.sbuf_tensor("Z", [P, NW, D], F32) as Z:
                first_norm(nc, c, x, Z, deg, dinv, rows1)
                c["sems"].give_back()
                convolve(nc, c, ps, "u_", rows1, Z, gnn_idx, gnn_lo, gnn_win)
                c["sems"].give_back()
                between(nc, c, ps, gW1, gb1, gW2, Z, dinv, rows2)
                c["sems"].give_back()
                convolve(nc, c, ps, "v_", rows2, Z, gnn_idx, gnn_lo, gnn_win)
                c["sems"].give_back()
                batch_norm(nc, c, ps, x, gb2, ggamma, gbeta, wgat, att_src, att_dst, Z, dinv, x2, xn, heads, adst, rows3)
                c["sems"].give_back()
        gates = sb("gates", [P, NW, NE])
        with ExitStack() as actx:
            def asb(name, shape, dt=F32):
                return actx.enter_context(nc.sbuf_tensor(name, shape, dt))
            H = asb("H", [P, tiles_bound(E_FFN), ROW])
            top = asb("top", [P, NW, HEADS])
            node = asb("node", [P, NW, 2 * HEADS])
            sums = asb("sums", [P, NW, ROW])
            start_maxima(nc, heads, top)
            attention_max(nc, c, ps, rows3, ffn_idx, ffn_lo, ffn_win, H, top)
            c["sems"].give_back()
            node_maxima(nc, c, top, adst, heads, node, sums)
            attention_sums(nc, c, ps, H, ffn_lo, ffn_win, node, sums)
            c["sems"].give_back()
            gates_of(nc, c, sums, b_gat, ln_gamma, ln_beta, gates)
            c["sems"].give_back()
        experts(nc, c, ps, x2, xn, fW1, fb1, fW2, fb2, gates, out)


_INS = ["x", "src", "dst", "L0_gnn_W1", "L0_gnn_b1", "L0_gnn_W2", "L0_gnn_b2", "L0_gnn_gamma", "L0_gnn_beta",
        "L0_ffn_W_gat", "L0_ffn_att_src", "L0_ffn_att_dst", "L0_ffn_b_gat", "L0_ffn_ln_gamma", "L0_ffn_ln_beta",
        "L0_ffn_W1", "L0_ffn_b1", "L0_ffn_W2", "L0_ffn_b2", "L0_ffn_edge_index"]


def kernel(**inputs):
    import concourse.bacc as bacc
    from concourse.bass_utils import run_bass_kernel_spmd

    nc = bacc.Bacc("TRN2", target_bir_lowering=False, num_devices=1)
    arrays, args = {}, []
    for name in _INS:
        a = np.ascontiguousarray(inputs[name])
        arrays[f"in_{name}"] = a
        args.append(nc.dram_tensor(f"in_{name}", a.shape, mybir.dt.from_np(a.dtype), kind="ExternalInput").ap())
    args.append(nc.dram_tensor("out", (N, D), F32, kind="ExternalOutput").ap())
    gnn_ffn(nc, *args)
    r = run_bass_kernel_spmd(nc, [arrays], core_ids=[0])
    return r.results[0]["out"]
```

```python
import numpy as np
import concourse.bass as bass
from concourse import mybir
from contextlib import ExitStack

F32 = mybir.dt.float32
BF16 = mybir.dt.bfloat16
I32 = mybir.dt.int32
U32 = mybir.dt.uint32
ALU = mybir.AluOpType
ACT = mybir.ActivationFunctionType
AX = mybir.AxisListType

P = 128
N = 12500
D = 256
NW = (N + P - 1) // P
NP = NW * P
LASTROWS = N - (NW - 1) * P
KC = D // P
E_GNN = 200000
E_FFN = 131072
HEADS = 4
NE = 4
HG = HEADS * NE
ROW = HG + HEADS
F = 512
FC = F // P
EPS = 1e-5
B = 5
NB_W = NW + 1
PADLO = 255
BIG = 1e30
GT = 8
BANK = 512


def tiles_bound(edges):
    most = (edges + NW * (P - 1)) // P
    return (most + 7) // 8 * 8


def blocks_bound(edges):
    return (tiles_bound(edges) + P - 1) // P * P


def pairs(eng, n, body):
    body(0, 0, 0, True, False)
    body(1, 0, 1, True, n == 2)
    end = n // 2 if n % 2 else n // 2 - 1
    with eng.Fori(1, end) as i:
        body(i * 2, i, 0, False, False)
        body(i * 2 + 1, i, 1, False, False)
    if n % 2:
        body(n - 1, n // 2, 0, False, True)
    else:
        body(n - 2, n // 2 - 1, 0, False, False)
        body(n - 1, n // 2 - 1, 1, False, True)


def pairs_but_last(eng, n, body):
    body(0, 0, 0, True, False)
    body(1, 0, 1, True, False)
    end = n // 2 - 1
    with eng.Fori(1, end) as i:
        body(i * 2, i, 0, False, False)
        body(i * 2 + 1, i, 1, False, False)
    for k in range(2 * end, n):
        body(k, k // 2, k % 2, False, k == n - 1)


class Signals:

    def __init__(self, nc):
        self.nc, self.taken = nc, []

    def enter_context(self, handle):
        self.taken.append(handle)
        return handle

    def give_back(self):
        self.nc.clear_and_free_semaphores(self.taken)
        self.taken = []
        self.nc.all_engine_barrier()


class Steps:

    def __init__(self, eng, sem):
        self.eng, self.sem, self.n = eng, sem, 0

    def did(self, instruction):
        instruction.then_inc(self.sem, 1)
        self.n += 1

    def settle(self):
        self.eng.wait_ge(self.sem, self.n)

    def link(self, instruction):
        self.did(instruction)
        self.settle()


def window_values(nc, row, start, count, engine):
    return nc.values_load_multi_w_load_instructions(
        row[0:1, bass.ds(start, count)], engines=[engine], min_val=0, max_val=NW - 1,
        skip_runtime_bounds_check_because="the table is clamped to the last window")[1]


def inverse_root(nc, dve, me, v, root, inv, s_ask, s_root, n):
    dve.sem_inc(s_ask)
    dve.wait_ge(s_root, n)
    me.link(nc.vector.reciprocal(inv, root))
    me.link(nc.vector.tensor_tensor(root, inv, inv, ALU.mult))
    me.link(nc.vector.tensor_tensor(root, root, v, ALU.mult))
    me.link(nc.vector.tensor_scalar(root, root, -0.5, 1.5, ALU.mult, ALU.add))
    me.link(nc.vector.tensor_tensor(v, root, inv, ALU.mult))


def take_root(nc, act, v, root, s_ask, s_root, n):
    act.wait_ge(s_ask, n)
    nc.scalar.activation(root, v, ACT.Sqrt).then_inc(s_root, 1)


def make_consts(nc, ctx, sems):
    def sb(name, shape, dt):
        return ctx.enter_context(nc.sbuf_tensor(name, shape, dt))
    c = {
        "sems": sems,
        "iota_i": sb("iota_i", [P, P], I32), "iota_f": sb("iota_f", [P, P], F32),
        "iota_b": sb("iota_b", [P, P], BF16),
        "ident": sb("ident", [P, P], F32), "ident_b": sb("ident_b", [P, P], BF16),
        "before": sb("before", [P, P], BF16), "notbefore": sb("notbefore", [P, P], BF16),
        "upto": sb("upto", [P, P], F32), "ones": sb("ones", [P, P], F32),
        "ones_b": sb("ones_b", [P, P], BF16), "zeros_b": sb("zeros_b", [P, P], BF16),
        "pick": sb("pick", [2 * HEADS, HEADS, P], BF16),
    }
    s_io = c["sems"].enter_context(nc.alloc_semaphore("c_iota"))
    s_set = c["sems"].enter_context(nc.alloc_semaphore("c_set"))
    s_sel = c["sems"].enter_context(nc.alloc_semaphore("c_sel"))
    with nc.Block() as block:
        @block.gpsimd
        def _(pool):
            nc.gpsimd.iota(c["iota_i"][:, :], [[1, P]], base=0, channel_multiplier=0).then_inc(s_io, 1)
            pool.wait_ge(s_set, 8)
            nc.gpsimd.affine_select(out=c["ident"][:, :], in_=c["ident"][:, :], compare_op=ALU.not_equal,
                                    fill=1.0, base=0, pattern=[[-1, P]], channel_multiplier=1)
            nc.gpsimd.affine_select(out=c["ident_b"][:, :], in_=c["ident_b"][:, :], compare_op=ALU.not_equal,
                                    fill=1.0, base=0, pattern=[[-1, P]], channel_multiplier=1)
            nc.gpsimd.affine_select(out=c["before"][:, :], in_=c["before"][:, :], compare_op=ALU.is_ge,
                                    fill=1.0, base=0, pattern=[[-1, P]], channel_multiplier=1)
            nc.gpsimd.affine_select(out=c["notbefore"][:, :], in_=c["notbefore"][:, :], compare_op=ALU.is_ge,
                                    fill=0.0, base=0, pattern=[[-1, P]], channel_multiplier=1)
            nc.gpsimd.affine_select(out=c["upto"][:, :], in_=c["upto"][:, :], compare_op=ALU.is_gt,
                                    fill=1.0, base=0, pattern=[[-1, P]], channel_multiplier=1)
            nc.gpsimd.affine_select(out=c["pick"][:, :, :], in_=c["pick"][:, :, :], compare_op=ALU.not_equal,
                                    fill=1.0, base=0, pattern=[[-1, HEADS], [0, P]],
                                    channel_multiplier=1).then_inc(s_sel, 1)
            pool.wait_ge(s_sel, 1)
            nc.gpsimd.affine_select(out=c["pick"][:, :, :], in_=c["pick"][:, :, :], compare_op=ALU.not_equal,
                                    fill=1.0, base=-HEADS, pattern=[[-1, HEADS], [0, P]],
                                    channel_multiplier=1).then_inc(s_sel, 1)

        @block.vector
        def _(dve):
            for name, v in (("ident", 0.0), ("ident_b", 0.0), ("before", 0.0), ("notbefore", 1.0),
                            ("upto", 0.0), ("ones", 1.0), ("ones_b", 1.0)):
                nc.vector.memset(c[name][:, :], v).then_inc(s_set, 1)
            nc.vector.memset(c["pick"][:, :, :], 0.0).then_inc(s_set, 1)
            nc.vector.memset(c["zeros_b"][:, :], 0.0)
            dve.wait_ge(s_io, 1)
            nc.vector.tensor_copy(c["iota_f"][:, :], c["iota_i"][:, :])
            nc.vector.tensor_copy(c["iota_b"][:, :], c["iota_i"][:, :])
    return c


def bin_edges(nc, c, ps, tag, edges, src, dst, listed, idx, lo_f, win_row, deg, runs=None):
    cols0 = (edges + P - 1) // P
    cols = (cols0 + B - 1) // B * B
    full, rest = edges // cols0, edges % cols0
    nb = cols // B
    nt, ntb = tiles_bound(edges), blocks_bound(edges)
    slots = ntb * P
    with ExitStack() as ctx:
        def sb(name, shape, dt):
            return ctx.enter_context(nc.sbuf_tensor(tag + name, shape, dt))


        def sem(name):
            return c["sems"].enter_context(nc.alloc_semaphore(tag + name))

        dst_i = sb("dst_i", [P, cols], I32)
        src_i = sb("src_i", [P, cols], I32)
        part_i = sb("part_i", [P, cols], I32)
        win_b = sb("win_b", [P, cols], BF16)
        lo_b = sb("lo_b", [P, cols], BF16)
        rec = sb("rec", [P, cols, 2], I32)
        empty = sb("empty", [P, ntb, 2], I32)
        hot_w = sb("hot_w", [P, 2, B, NB_W], BF16)
        hot_lo = sb("hot_lo", [P, 2, B, P], BF16)
        picked = sb("picked", [P, B, NB_W], F32)
        pos_f = sb("pos_f", [P, B], F32)
        pos = sb("pos", [P, 2, B], U32)
        rec_ring = sb("rec_ring", [P, 2, B, 2], I32)
        count_i = sb("count_i", [P, 1], I32)
        tiles_f = sb("tiles_f", [P, 1], F32)
        ends = sb("ends", [P, 1], F32)
        base = sb("base", [P, 1], F32)
        diag = sb("diag", [P, P], F32)
        step_i = sb("step_i", [P, ntb], I32)
        step_f = sb("step_f", [P, ntb], F32)
        after = sb("after", [P, ntb], F32)
        back = sb("back", [P, 2, P, 2], I32)
        back_f = sb("back_f", [P, 2, 2, P], F32)
        hist, small, row = ps[:, 0, :], ps[:, 1, :], ps[:, 3, :]
        place = ps[:, 2, 0:B * NB_W].rearrange("p (j w) -> p j w", w=NB_W)
        turned = ps[:, 4:6, 0:2 * P].rearrange("p s (f q) -> p s f q", q=P)

        s_pad, s_ld, s_ld2, s_empty, s_fill, s_step = (sem(x) for x in ("pad", "ld", "ld2", "empty", "fill", "step"))
        s_keys, s_hot, s_hist, s_hsum = (sem(x) for x in ("keys", "hot", "hist", "hsum"))
        s_deg, s_cnt, s_tl, s_end, s_dg, s_base = (sem(x) for x in ("deg", "cnt", "tl", "end", "dg", "base"))
        s_dve, s_row, s_rowd, s_win = (sem(x) for x in ("dve", "row", "rowd", "win"))
        s_hot2, s_at, s_adv, s_read, s_pos = (sem(x) for x in ("hot2", "at", "adv", "read", "pos"))
        s_red = sem("red")
        s_sc = [sem("sc0"), sem("sc1")]
        s_tick = sem("tick")
        s_back = [sem("back0"), sem("back1")]
        s_bf, s_tr, s_out = (sem(x) for x in ("bf", "tr", "out"))
        s_listed = sem("listed")
        if runs:
            same, last_tile, filled = runs
            diag2 = sb("diag2", [P, P], F32)
            win_all = sb("win_all", [P, ntb], F32)
            last_f = sb("last_f", [1, NW], F32)
            s_dg2, s_wide = sem("dg2"), sem("wide")
        blocks = ntb // P
        chunk = 416 if ntb % 416 == 0 else 384
        chunks = ntb // chunk
        assert chunks * chunk == ntb

        with nc.Block() as block:
            @block.sync
            def _(sp):
                sp.wait_ge(s_pad, 2)
                for t, a in ((dst_i, dst), (src_i, src)):
                    sp.dma_start(t[0:full, 0:cols0],
                                 a[0:full * cols0].rearrange("(p n) -> p n", n=cols0)).then_inc(s_ld, 16)
                if rest:
                    for t, a in ((dst_i, dst), (src_i, src)):
                        sp.dma_start(t[full:full + 1, 0:rest],
                                     a[full * cols0:edges].rearrange("(p n) -> p n", p=1)).then_inc(s_ld2, 16)
                sp.wait_ge(s_empty, 2)
                sp.dma_start(listed.rearrange("(p n) c -> p (n c)", p=P),
                             empty[:, :, :].rearrange("p n c -> p (n c)")).then_inc(s_fill, 16)
                sp.wait_ge(s_listed, 1)
                rows = listed.rearrange("(b s p) c -> b s p c", s=P, p=P)
                for b in range(blocks):
                    if b >= 2:
                        sp.wait_ge(s_bf, b - 1)
                    sp.dma_start(back[:, b % 2, :, :], rows[b]).then_inc(s_back[b % 2], 16)

            @block.gpsimd
            def _(pool):
                nc.gpsimd.iota(step_i[:, :], [[1, ntb]], base=0, channel_multiplier=0).then_inc(s_step, 1)
                pool.wait_ge(s_fill, 16)

                def scatter(k, i, s, first, last):
                    pool.wait_ge(s_pos, k + 1)
                    pool.sem_inc(s_tick)
                    for j in range(B):
                        nc.gpsimd.indirect_dma_start(
                            out=listed, out_offset=bass.IndirectOffsetOnAxis(ap=pos[:, s, j:j + 1], axis=0),
                            in_=rec_ring[:, s, j, :], in_offset=None,
                            bounds_check=slots - 1, oob_is_err=False).then_inc(s_sc[s], 16)
                pairs(pool, nb, scatter)
                pool.wait_ge(s_sc[0], 16 * B * ((nb + 1) // 2))
                pool.wait_ge(s_sc[1], 16 * B * (nb // 2))
                pool.sem_inc(s_listed)

            @block.vector
            def _(dve):
                me = Steps(dve, s_dve)
                nc.vector.memset(dst_i[:, :], NW * P).then_inc(s_pad, 1)
                nc.vector.memset(src_i[:, :], 0).then_inc(s_pad, 1)
                nc.vector.memset(empty[:, :, 0], 0).then_inc(s_empty, 1)
                nc.vector.memset(empty[:, :, 1], PADLO).then_inc(s_empty, 1)
                nc.vector.memset(base[:, :], float(slots))
                nc.vector.memset(ends[:, :], 0.0)
                dve.wait_ge(s_ld, 32)
                if rest:
                    dve.wait_ge(s_ld2, 32)
                me.link(nc.vector.tensor_scalar(part_i[:, :], dst_i[:, :], 7, None, ALU.arith_shift_right))
                nc.vector.tensor_copy(win_b[:, :], part_i[:, :])
                me.link(nc.vector.tensor_scalar(rec[:, :, 1], dst_i[:, :], P - 1, None, ALU.bitwise_and))
                nc.vector.tensor_copy(lo_b[:, :], rec[:, :, 1])
                me.link(nc.vector.tensor_copy(rec[:, :, 0], src_i[:, :]))

                def hot_windows(k, s, to):
                    return nc.vector.tensor_tensor(
                        to[:, s, :, :], c["iota_b"][:, None, 0:NB_W].to_broadcast([P, B, NB_W]),
                        win_b[:, bass.ds(k * B, B), None].to_broadcast([P, B, NB_W]), ALU.is_equal)

                def count(k, i, s, first, last):
                    if not first:
                        dve.wait_ge(s_hist, k - 1)
                    hot_windows(k, s, hot_w)
                    nc.vector.tensor_tensor(
                        hot_lo[:, s, :, :], c["iota_b"][:, None, :].to_broadcast([P, B, P]),
                        lo_b[:, bass.ds(k * B, B), None].to_broadcast([P, B, P]), ALU.is_equal).then_inc(s_hot, 1)
                pairs(dve, nb, count)
                dve.wait_ge(s_hsum, 1)
                nc.vector.tensor_copy(deg[:, :], hist[:, 0:NW]).then_inc(s_deg, 1)
                dve.wait_ge(s_cnt, 1)
                me.link(nc.vector.tensor_copy(count_i[0:NW, :], small[0:NW, 0:1]))
                me.link(nc.vector.tensor_scalar(count_i[0:NW, :], count_i[0:NW, :], P - 1, None, ALU.add))
                me.link(nc.vector.tensor_scalar(count_i[0:NW, :], count_i[0:NW, :], 7, None, ALU.arith_shift_right))
                me.link(nc.vector.tensor_copy(tiles_f[0:NW, :], count_i[0:NW, :]))
                dve.sem_inc(s_tl)
                dve.wait_ge(s_end, 1)
                me.link(nc.vector.tensor_copy(ends[0:NW, :], small[0:NW, 1:2]))
                me.link(nc.vector.tensor_tensor(base[0:NW, :], ends[0:NW, :], tiles_f[0:NW, :], ALU.subtract))
                me.link(nc.vector.tensor_scalar(base[0:NW, :], base[0:NW, :], float(P), None, ALU.mult))
                nc.vector.tensor_scalar(diag[0:NB_W, 0:NB_W], c["ident"][0:NB_W, 0:NB_W], base[0:NB_W, 0:1], None,
                                        ALU.mult).then_inc(s_dg, 1)
                dve.wait_ge(s_step, 1)
                me.link(nc.vector.tensor_copy(step_f[:, :], step_i[:, :]))
                nc.vector.tensor_scalar(after[0:NW, :], step_f[0:NW, :], ends[0:NW, 0:1], None,
                                        ALU.is_ge).then_inc(s_row, 1)
                for q in range(chunks):
                    dve.wait_ge(s_rowd, q + 1)
                    if runs:
                        me.link(nc.vector.tensor_scalar(win_all[:, q * chunk:(q + 1) * chunk], row[:, 0:chunk],
                                                        float(NW - 1), None, ALU.min))
                    nc.vector.tensor_scalar(win_row[0:1, q * chunk:(q + 1) * chunk], row[0:1, 0:chunk],
                                            float(NW - 1), None, ALU.min).then_inc(s_win, 1)
                if runs:
                    nc.vector.tensor_scalar(diag2[0:NW, 0:NW], c["ident"][0:NW, 0:NW], ends[0:NW, 0:1], None, ALU.mult)
                    nc.vector.tensor_scalar(diag[0:NW, 0:NW], c["ident"][0:NW, 0:NW], tiles_f[0:NW, 0:1], None,
                                            ALU.mult).then_inc(s_dg2, 1)
                    me.link(nc.vector.memset(same[:, 0:1], 0.0))
                    me.link(nc.vector.tensor_tensor(same[:, 1:ntb], win_all[:, 1:ntb], win_all[:, 0:ntb - 1], ALU.is_equal))
                    dve.wait_ge(s_wide, 1)
                    me.link(nc.vector.tensor_scalar(last_f[0:1, :], small[0:1, 0:NW], -1.0, 0.0, ALU.add, ALU.max))
                    me.link(nc.vector.tensor_copy(last_tile[0:1, :], last_f[0:1, :]))
                    me.link(nc.vector.tensor_scalar(filled[:, :], small[:, P:P + NW], 0.5, None, ALU.is_gt))

                def positions(k, i, s, first, last):
                    if not first:
                        dve.wait_ge(s_adv, k - 1)
                    hot_windows(k, s, hot_w).then_inc(s_hot2, 1)
                    dve.wait_ge(s_at, k + 1)
                    nc.vector.tensor_tensor(picked[:, :, :], place[:, :, :], hot_w[:, s, :, :],
                                            ALU.mult).then_inc(s_read, 1)
                    dve.wait_ge(s_read, k + 1)
                    nc.vector.tensor_reduce(pos_f[:, :], picked[:, :, :], AX.X, ALU.add).then_inc(s_red, 1)
                    if not first:
                        dve.wait_ge(s_sc[s], i * (16 * B))
                    dve.wait_ge(s_red, k + 1)
                    nc.vector.tensor_copy(pos[:, s, :], pos_f[:, :])
                    nc.vector.tensor_copy(rec_ring[:, s, :, :], rec[:, bass.ds(k * B, B), :]).then_inc(s_pos, 1)
                pairs(dve, nb, positions)
                for b in range(blocks):
                    dve.wait_ge(s_back[b % 2], 16 * (b // 2 + 1))
                    if b >= 2:
                        dve.wait_ge(s_tr, b - 1)
                    nc.vector.tensor_copy(back_f[:, b % 2, :, :],
                                          back[:, b % 2, :, :].rearrange("s p c -> s c p")).then_inc(s_bf, 1)
                    dve.wait_ge(s_tr, b + 1)
                    nc.vector.tensor_copy(idx[:, b * P:(b + 1) * P], turned[:, b % 2, 0, :])
                    nc.vector.tensor_copy(lo_f[:, b * P:(b + 1) * P], turned[:, b % 2, 1, :]).then_inc(s_out, 1)

            @block.tensor
            def _(pe):
                nc.tensor.matmul(hist[:, 0:NB_W], c["zeros_b"][:, :], c["zeros_b"][:, 0:NB_W], start=True, stop=False)

                def count(k, i, s, first, last):
                    pe.wait_ge(s_hot, k + 1)
                    for j in range(B):
                        m = nc.tensor.matmul(hist[:, 0:NB_W], hot_lo[:, s, j, :], hot_w[:, s, j, :],
                                             start=False, stop=False)
                    m.then_inc(s_hist, 1)
                pairs(pe, nb, count)
                nc.tensor.matmul(hist[:, 0:NB_W], c["zeros_b"][:, :], c["zeros_b"][:, 0:NB_W],
                                 start=False, stop=True).then_inc(s_hsum, 1)
                pe.wait_ge(s_deg, 1)
                nc.tensor.matmul(small[0:NW, 0:1], deg[:, :], c["ones"][:, 0:1], start=True, stop=True).then_inc(s_cnt, 1)
                pe.wait_ge(s_tl, 1)
                nc.tensor.matmul(small[0:NW, 1:2], c["upto"][0:NW, 0:NW], tiles_f[0:NW, :],
                                 start=True, stop=True).then_inc(s_end, 1)
                pe.wait_ge(s_dg, 1)
                nc.tensor.matmul(place[:, :, :], c["ones"][0:NB_W, :],
                                 diag[0:NB_W, None, 0:NB_W].to_broadcast([NB_W, B, NB_W]), start=True, stop=True)
                pe.wait_ge(s_row, 1)
                for q in range(chunks):
                    if q:
                        pe.wait_ge(s_win, q)
                    nc.tensor.matmul(row[:, 0:chunk], c["ones"][0:NW, :], after[0:NW, q * chunk:(q + 1) * chunk],
                                     start=True, stop=True).then_inc(s_rowd, 1)
                if runs:
                    pe.wait_ge(s_dg2, 1)
                    nc.tensor.matmul(small[:, 0:NW], c["ones"][0:NW, :], diag2[0:NW, 0:NW], start=True, stop=True)
                    nc.tensor.matmul(small[:, P:P + NW], c["ones"][0:NW, :], diag[0:NW, 0:NW], start=True,
                                     stop=True).then_inc(s_wide, 1)

                def positions(k, i, s, first, last):
                    def add(to, n, lhs, j):
                        return nc.tensor.matmul(place[:, to:to + n, :], lhs,
                                                hot_w[:, s, j:j + 1, :].to_broadcast([P, n, NB_W]) if n > 1
                                                else hot_w[:, s, j:j + 1, :], start=False, stop=True,
                                                skip_group_check=True)
                    pe.wait_ge(s_hot2, k + 1)
                    m = nc.tensor.matmul(place[:, :, :], c["before"][:, :], hot_w[:, s, :, :], start=False,
                                         stop=True, skip_group_check=True)
                    for j in range(B - 1):
                        m = add(j + 1, B - 1 - j, c["ones_b"][:, :], j)
                    m.then_inc(s_at, 1)
                    pe.wait_ge(s_read, k + 1)
                    m = nc.tensor.matmul(place[:, :, :], c["notbefore"][:, :], hot_w[:, s, :, :], start=False,
                                         stop=True, skip_group_check=True)
                    for j in range(1, B):
                        m = add(0, j, c["ones_b"][:, :], j)
                    m.then_inc(s_adv, 1)
                pairs(pe, nb, positions)
                for b in range(blocks):
                    pe.wait_ge(s_bf, b + 1)
                    if b >= 2:
                        pe.wait_ge(s_out, b - 1)
                    for f in range(2):
                        m = nc.tensor.transpose(turned[:, b % 2, f, :], back_f[:, b % 2, f, :], c["ident"][:, :])
                    m.then_inc(s_tr, 1)


def normalize_all(nc, dve, me, Z, stat, rstd, s_sub, s_sq, ask, mean_scale=1.0 / D):
    me.link(nc.vector.tensor_reduce(stat[:, :], Z[:, :, :], AX.X, ALU.add))
    me.link(nc.vector.tensor_scalar(stat[:, :], stat[:, :], mean_scale, None, ALU.mult))
    nc.vector.tensor_tensor(Z[:, :, :], Z[:, :, :], stat[:, :, None].to_broadcast([P, NW, D]),
                            ALU.subtract).then_inc(s_sub, 1)
    dve.wait_ge(s_sq, 1)
    me.link(nc.vector.tensor_scalar(rstd[:, :], rstd[:, :], mean_scale, EPS, ALU.mult, ALU.add))
    inverse_root(nc, dve, me, rstd[:, :], *ask)


def square_rows(nc, act, Z, junk, rstd, s_sub, s_each, s_sq):
    act.wait_ge(s_sub, 1)

    def rows(k, i, s, first, last):
        if not first:
            act.wait_ge(s_each, k - 1)
        nc.scalar.activation(junk[:, s, :], Z[:, bass.ds(k, 1), :].rearrange("p a d -> p (a d)"), ACT.Square,
                             accum_out=rstd[:, bass.ds(k, 1)]).then_inc(s_each, 1)
    pairs(act, NW, rows)
    act.wait_ge(s_each, NW)
    act.sem_inc(s_sq)


def node_rows(dram, w0, n):
    return dram[w0 * P:(w0 + n) * P, :].rearrange("(w p) d -> p w d", p=P)


def first_norm(nc, c, x, Z, deg, dinv, table):
    with ExitStack() as ctx:
        def sem(name):
            return c["sems"].enter_context(nc.alloc_semaphore("n1_" + name))
        stat = ctx.enter_context(nc.sbuf_tensor("n1_stat", [P, NW], F32))
        rstd = ctx.enter_context(nc.sbuf_tensor("n1_rstd", [P, NW], F32))
        root = ctx.enter_context(nc.sbuf_tensor("n1_root", [P, NW], F32))
        inv = ctx.enter_context(nc.sbuf_tensor("n1_inv", [P, NW], F32))
        junk = ctx.enter_context(nc.sbuf_tensor("n1_junk", [P, 2, D], F32))
        s_ask, s_root = sem("ask"), sem("root")
        s_pad, s_x, s_dve, s_sub, s_each, s_sq, s_z, s_t = (
            sem(n) for n in ("pad", "x", "dve", "sub", "each", "sq", "z", "t"))
        with nc.Block() as block:
            @block.sync
            def _(sp):
                sp.dma_start(Z[:, 0:NW - 1, :], node_rows(x, 0, NW - 1)).then_inc(s_x, 16)
                sp.wait_ge(s_pad, 1)
                sp.dma_start(Z[0:LASTROWS, NW - 1, :], x[(NW - 1) * P:N, :]).then_inc(s_x, 16)
                sp.wait_ge(s_z, 1)
                sp.dma_start(node_rows(table, 0, NW), Z[:, :, :]).then_inc(s_t, 16)
                sp.wait_ge(s_t, 16)

            @block.vector
            def _(dve):
                me = Steps(dve, s_dve)
                nc.vector.memset(Z[:, NW - 1, :], 0.0).then_inc(s_pad, 1)
                me.link(nc.vector.tensor_scalar(dinv[:, :], deg[:, :], 1.0, None, ALU.add))
                inverse_root(nc, dve, me, dinv[:, :], root[:, :], inv[:, :], s_ask, s_root, 1)
                dve.wait_ge(s_x, 32)
                normalize_all(nc, dve, me, Z, stat, rstd, s_sub, s_sq, (root[:, :], inv[:, :], s_ask, s_root, 2))
                me.link(nc.vector.tensor_tensor(rstd[:, :], rstd[:, :], dinv[:, :], ALU.mult))
                nc.vector.tensor_tensor(Z[:, :, :], Z[:, :, :], rstd[:, :, None].to_broadcast([P, NW, D]),
                                        ALU.mult).then_inc(s_z, 1)

            @block.scalar
            def _(act):
                take_root(nc, act, dinv[:, :], root[:, :], s_ask, s_root, 1)
                square_rows(nc, act, Z, junk, rstd, s_sub, s_each, s_sq)
                take_root(nc, act, rstd[:, :], root[:, :], s_ask, s_root, 2)


def convolve(nc, c, ps, tag, table, Z, idx, lo_f, win_row):
    batches = tiles_bound(E_GNN) // GT
    with ExitStack() as ctx:
        def sem(name):
            return c["sems"].enter_context(nc.alloc_semaphore(tag + name))
        ring = ctx.enter_context(nc.sbuf_tensor(tag + "ring", [P, 2, GT], U32))
        got = ctx.enter_context(nc.sbuf_tensor(tag + "got", [P, 2, GT, D], F32))
        hot = ctx.enter_context(nc.sbuf_tensor(tag + "hot", [P, 2, GT, P], F32))
        part = ps[:, 0:8, :].rearrange("p (s b) (j d) -> p s (b j) d", s=2, d=D)
        s_idx, s_hot, s_mm, s_add, s_tick = (sem(n) for n in ("idx", "hot", "mm", "add", "tick"))
        s_got = [sem("got0"), sem("got1")]
        with nc.Block() as block:
            @block.scalar
            def _(act):
                def indices(k, i, s, first, last):
                    if not first:
                        act.wait_ge(s_got[s], i * (16 * GT))
                    nc.scalar.copy(ring[:, s, :], idx[:, bass.ds(k * GT, GT)]).then_inc(s_idx, 1)
                pairs(act, batches, indices)

            @block.gpsimd
            def _(pool):
                def gather(k, i, s, first, last):
                    pool.wait_ge(s_idx, k + 1)
                    pool.sem_inc(s_tick)
                    if not first:
                        pool.wait_ge(s_mm, k - 1)
                        pool.sem_inc(s_tick)
                    for j in range(GT):
                        nc.gpsimd.indirect_dma_start(
                            out=got[:, s, j, :], out_offset=None, in_=table,
                            in_offset=bass.IndirectOffsetOnAxis(ap=ring[:, s, j:j + 1], axis=0),
                            bounds_check=NP - 1, oob_is_err=False).then_inc(s_got[s], 16)
                pairs(pool, batches, gather)

            @block.vector
            def _(dve):
                def one_hot(k, s, first):
                    if not first:
                        dve.wait_ge(s_mm, k - 1)
                    nc.vector.tensor_tensor(hot[:, s, :, :], c["iota_f"][:, None, :].to_broadcast([P, GT, P]),
                                            lo_f[:, bass.ds(k * GT, GT), None].to_broadcast([P, GT, P]),
                                            ALU.is_equal).then_inc(s_hot, 1)

                def add(k, i, s, first, last):
                    if not last:
                        one_hot(k + 1, 1 - s, first and s == 0)
                    wins = window_values(nc, win_row, k * GT, GT, mybir.EngineType.DVE)
                    dve.wait_ge(s_mm, k + 1)
                    for j in range(GT):
                        if not (first and s == 0 and j == 0):
                            dve.wait_ge(s_add, k * GT + j)
                        z = Z[:, bass.ds(wins[j], 1), :]
                        nc.vector.tensor_tensor(z, z, part[:, s, j:j + 1, :], ALU.add).then_inc(s_add, 1)
                one_hot(0, 0, True)
                pairs(dve, batches, add)

            @block.tensor
            def _(pe):
                def product(k, i, s, first, last):
                    pe.wait_ge(s_hot, k + 1)
                    pe.wait_ge(s_got[s], i * (16 * GT) + 16 * GT)
                    if not first:
                        pe.wait_ge(s_add, k * GT - GT)
                    for j in range(GT):
                        m = nc.tensor.matmul(part[:, s, j, :], hot[:, s, j, :], got[:, s, j, :],
                                             start=True, stop=True)
                    m.then_inc(s_mm, 1)
                pairs(pe, batches, product)


def between(nc, c, ps, W1, b1, W2, Z, dinv, table):
    with ExitStack() as ctx:
        def sb(name, shape):
            return ctx.enter_context(nc.sbuf_tensor("m_" + name, shape, F32))


        def sem(name):
            return c["sems"].enter_context(nc.alloc_semaphore("m_" + name))
        w1 = sb("w1", [P, KC, F])
        w1t = sb("w1t", [P, FC, D])
        w2 = sb("w2", [P, FC, D])
        w12 = sb("w12", [P, KC, D])
        b1c = sb("b1c", [P, FC])
        b12 = sb("b12", [1, D])
        zs = sb("zs", [P, 2, D])
        zt = sb("zt", [P, 2, KC, P])
        tp = ps[:, 0:2, 0:D].rearrange("p s (k q) -> p s k q", q=P)
        hp = ps[:, 2:4, :]
        wp, bp = ps[:, 4, :], ps[:, 5, :]
        s_w, s_b, s_wt, s_wc, s_wp, s_w12, s_zs, s_tp, s_zt, s_hp, s_h = (
            sem(n) for n in ("w", "b", "wt", "wc", "wp", "w12", "zs", "tp", "zt", "hp", "h"))
        s_st = [sem("st0"), sem("st1")]
        with nc.Block() as block:
            @block.sync
            def _(sp):
                sp.dma_start(w1[:, :, :], W1.rearrange("(k p) f -> p k f", p=P)).then_inc(s_w, 16)
                sp.dma_start(w2[:, :, :], W2.rearrange("(k p) f -> p k f", p=P)).then_inc(s_w, 16)
                with nc.allow_non_contiguous_dma(reason="one bias vector onto partitions"):
                    sp.dma_start(b1c[:, :], b1.rearrange("(k p) -> p k", p=P)).then_inc(s_b, 16)

                def store(k, i, s, first, last):
                    sp.wait_ge(s_h, k + 1)
                    sp.dma_start(table[bass.ds(k * P, P), :],
                                 Z[:, bass.ds(k, 1), :].rearrange("p a d -> p (a d)")).then_inc(s_st[s], 16)
                pairs(sp, NW, store)
                for s in range(2):
                    sp.wait_ge(s_st[s], 16 * (NW // 2))

            @block.tensor
            def _(pe):
                pe.wait_ge(s_w, 32)
                pe.wait_ge(s_b, 16)
                for f in range(FC):
                    for k in range(KC):
                        n = f * KC + k
                        if n >= 1:
                            pe.wait_ge(s_wc, n)
                        nc.tensor.transpose(wp[:, 0:P], w1[:, k, f * P:(f + 1) * P], c["ident"][:, :]).then_inc(s_wt, 1)
                pe.wait_ge(s_wc, FC * KC)
                for k in range(KC):
                    if k:
                        pe.wait_ge(s_w12, k)
                    for f in range(FC):
                        m = nc.tensor.matmul(wp[:, 0:D], w1t[:, f, k * P:(k + 1) * P], w2[:, f, :],
                                             start=(f == 0), stop=(f == FC - 1))
                    m.then_inc(s_wp, 1)
                for f in range(FC):
                    m = nc.tensor.matmul(bp[0:1, 0:D], b1c[:, f:f + 1], w2[:, f, :], start=(f == 0), stop=(f == FC - 1))
                m.then_inc(s_wp, 1)
                pe.wait_ge(s_w12, KC + 1)

                def turn(k, s, first):
                    pe.wait_ge(s_zs, k + 1)
                    if not first:
                        pe.wait_ge(s_zt, k - 1)
                    for q in range(KC):
                        m = nc.tensor.transpose(tp[:, s, q, :], zs[:, s, q * P:(q + 1) * P], c["ident"][:, :])
                    m.then_inc(s_tp, 1)

                def product(k, i, s, first, last):
                    if not last:
                        turn(k + 1, 1 - s, first and s == 0)
                    pe.wait_ge(s_zt, k + 1)
                    if not first:
                        pe.wait_ge(s_h, k - 1)
                    nc.tensor.matmul(hp[:, s, 0:D], c["ones"][0:1, :], b12[0:1, :], start=True, stop=False)
                    for q in range(KC):
                        m = nc.tensor.matmul(hp[:, s, 0:D], zt[:, s, q, :], w12[:, q, :], start=False, stop=(q == KC - 1))
                    m.then_inc(s_hp, 1)
                turn(0, 0, True)
                pairs(pe, NW, product)

            @block.scalar
            def _(act):
                def copy(k, i, s, first, last):
                    act.wait_ge(s_tp, k + 1)
                    if not first:
                        act.wait_ge(s_hp, k - 1)
                    nc.scalar.copy(zt[:, s, :, :], tp[:, s, :, :]).then_inc(s_zt, 1)
                pairs(act, NW, copy)

            @block.vector
            def _(dve):
                for n in range(FC * KC):
                    f, k = n // KC, n % KC
                    dve.wait_ge(s_wt, n + 1)
                    nc.vector.tensor_copy(w1t[:, f, k * P:(k + 1) * P], wp[:, 0:P]).then_inc(s_wc, 1)
                for k in range(KC):
                    dve.wait_ge(s_wp, k + 1)
                    nc.vector.tensor_copy(w12[:, k, :], wp[:, 0:D]).then_inc(s_w12, 1)
                dve.wait_ge(s_wp, KC + 1)
                nc.vector.tensor_copy(b12[0:1, :], bp[0:1, 0:D]).then_inc(s_w12, 1)

                def scale(k, s, first):
                    if not first:
                        dve.wait_ge(s_tp, k - 1)
                    nc.vector.tensor_tensor(zs[:, s, :], Z[:, bass.ds(k, 1), :].rearrange("p a d -> p (a d)"),
                                            dinv[:, bass.ds(k, 1)].to_broadcast([P, D]), ALU.mult).then_inc(s_zs, 1)

                def finish(k, i, s, first, last):
                    if not last:
                        scale(k + 1, 1 - s, first and s == 0)
                    dve.wait_ge(s_hp, k + 1)
                    nc.vector.tensor_tensor(Z[:, bass.ds(k, 1), :].rearrange("p a d -> p (a d)"), hp[:, s, 0:D],
                                            dinv[:, bass.ds(k, 1)].to_broadcast([P, D]), ALU.mult).then_inc(s_h, 1)
                scale(0, 0, True)
                pairs(dve, NW, finish)


def batch_norm(nc, c, ps, x, b2, gamma, beta, wgat, att_src, att_dst, Z, dinv, x2, xn, heads, adst, table):
    GW = 14
    groups = NW // GW
    with ExitStack() as ctx:
        def sb(name, shape):
            return ctx.enter_context(nc.sbuf_tensor("b_" + name, shape, F32))


        def sem(name):
            return c["sems"].enter_context(nc.alloc_semaphore("b_" + name))
        rows = sb("rows", [P, 3, D])
        atts = sb("atts", [P, 2, HG])
        mean = sb("mean", [P, D])
        scale = sb("scale", [P, D])
        sq = sb("sq", [P, 2, D])
        xg = sb("xg", [P, 2, GW, D])
        stat = sb("stat", [P, NW])
        rstd = sb("rstd", [P, NW])
        wg = sb("wg", [P, KC, HG])
        stage = sb("stage", [P, 2, D])
        root = sb("root", [P, D])
        inv = sb("inv", [P, D])
        s_ask, s_root = sem("ask"), sem("root")
        zt = sb("zt", [P, 2, KC, P])
        prod = sb("prod", [P, NW, HG])
        tp = ps[:, 0:2, 0:D].rearrange("p s (k q) -> p s k q", q=P)
        hp = ps[:, 2:4, :]
        total = ps[:, 4:6, :]
        (s_w, s_dve, s_y, s_cs, s_d, s_sq, s_cs2, s_x2, s_st2, s_xpad, s_sub, s_each, s_all, s_n, s_stn,
         s_tp, s_zt, s_hp, s_h, s_tab, s_stt, s_hsq, s_stage) = (sem(n) for n in (
             "w", "dve", "y", "cs", "d", "sq", "cs2", "x2", "st2", "xpad", "sub", "each", "all", "n", "stn",
             "tp", "zt", "hp", "h", "tab", "stt", "hsq", "stage"))
        s_x = [sem("x0"), sem("x1")]
        with nc.Block() as block:
            @block.sync
            def _(sp):
                for n, v in enumerate((b2, gamma, beta)):
                    sp.dma_start(rows[:, n, :], v.rearrange("(a d) -> a d", a=1).to_broadcast([P, D])).then_inc(s_w, 16)
                for n, v in enumerate((att_src, att_dst)):
                    sp.dma_start(atts[:, n, :], v.rearrange("(a h) e -> a (h e)", a=1).to_broadcast([P, HG])).then_inc(s_w, 16)
                sp.dma_start(wg[:, :, :], wgat.rearrange("(k p) f -> p k f", p=P)).then_inc(s_w, 16)

                sp.wait_ge(s_xpad, 1)

                def load(g):
                    n = GW if g < groups - 1 else GW - 1
                    sp.dma_start(xg[:, g % 2, 0:n, :], node_rows(x, g * GW, n)).then_inc(s_x[g % 2], 16)
                    if g == groups - 1:
                        sp.dma_start(xg[0:LASTROWS, g % 2, n, :], x[(NW - 1) * P:N, :]).then_inc(s_x[g % 2], 16)
                load(0)
                load(1)
                for g in range(groups):
                    sp.wait_ge(s_x2, g + 1)
                    sp.dma_start(node_rows(x2, g * GW, GW), Z[:, g * GW:(g + 1) * GW, :]).then_inc(s_st2, 16)
                    if g + 2 < groups:
                        load(g + 2)
                sp.wait_ge(s_n, 1)
                sp.dma_start(node_rows(xn, 0, NW), Z[:, :, :]).then_inc(s_stn, 16)
                sp.wait_ge(s_tab, 1)
                sp.dma_start(node_rows(table, 0, NW), heads[:, :, :]).then_inc(s_stt, 16)
                sp.wait_ge(s_st2, 16 * groups)
                sp.wait_ge(s_stn, 16)
                sp.wait_ge(s_stt, 16)

            @block.vector
            def _(dve):
                me = Steps(dve, s_dve)

                def spread(v):
                    return v[:, None, :].to_broadcast([P, NW, D])
                nc.vector.memset(xg[:, (groups - 1) % 2, GW - 1, :], 0.0).then_inc(s_xpad, 1)
                dve.wait_ge(s_w, 16 * 6)
                me.link(nc.vector.tensor_tensor(Z[:, :, :], Z[:, :, :], dinv[:, :, None].to_broadcast([P, NW, D]), ALU.mult))
                nc.vector.tensor_tensor(Z[:, :, :], Z[:, :, :], spread(rows[:, 0, :]), ALU.add).then_inc(s_y, 1)
                dve.wait_ge(s_cs, 1)
                me.link(nc.vector.tensor_scalar(mean[:, :], total[:, 0, 0:D], 1.0 / N, None, ALU.mult))
                dve.wait_ge(s_y, 1)
                nc.vector.tensor_tensor(Z[:, :, :], Z[:, :, :], spread(mean), ALU.subtract).then_inc(s_d, 1)
                dve.wait_ge(s_cs2, 1)
                me.link(nc.vector.tensor_scalar(scale[:, :], total[:, 1, 0:D], 1.0 / N, EPS, ALU.mult, ALU.add))
                inverse_root(nc, dve, me, scale[:, :], root[:, :], inv[:, :], s_ask, s_root, 1)
                me.link(nc.vector.tensor_tensor(scale[:, :], scale[:, :], rows[:, 1, :], ALU.mult))
                for g in range(groups):
                    z = Z[:, g * GW:(g + 1) * GW, :]
                    me.link(nc.vector.tensor_tensor(z, z, scale[:, None, :].to_broadcast([P, GW, D]), ALU.mult))
                    me.link(nc.vector.tensor_tensor(z, z, rows[:, 2:3, :].to_broadcast([P, GW, D]), ALU.add))
                    dve.wait_ge(s_x[g % 2], 16 * (g // 2 + 1 + (g == groups - 1)))
                    nc.vector.tensor_tensor(z, z, xg[:, g % 2, :, :], ALU.add).then_inc(s_x2, 1)
                dve.wait_ge(s_x2, groups)
                me.link(nc.vector.tensor_reduce(stat[:, :], Z[:, :, :], AX.X, ALU.add))
                me.link(nc.vector.tensor_scalar(stat[:, :], stat[:, :], 1.0 / D, None, ALU.mult))
                dve.wait_ge(s_st2, 16 * groups)
                nc.vector.tensor_tensor(Z[:, :, :], Z[:, :, :], stat[:, :, None].to_broadcast([P, NW, D]),
                                        ALU.subtract).then_inc(s_sub, 1)
                dve.wait_ge(s_all, 1)
                me.link(nc.vector.tensor_scalar(rstd[:, :], rstd[:, :], 1.0 / D, EPS, ALU.mult, ALU.add))
                inverse_root(nc, dve, me, rstd[:, :], root[:, 0:NW], inv[:, 0:NW], s_ask, s_root, 2)
                nc.vector.tensor_tensor(Z[:, :, :], Z[:, :, :], rstd[:, :, None].to_broadcast([P, NW, D]),
                                        ALU.mult).then_inc(s_n, 1)

                dve.wait_ge(s_n, 1)

                def put(k, s, first):
                    if not first:
                        dve.wait_ge(s_tp, k - 1)
                    nc.vector.tensor_copy(stage[:, s, None, :], Z[:, bass.ds(k, 1), :]).then_inc(s_stage, 1)

                def keep(k, i, s, first, last):
                    if not last:
                        put(k + 1, 1 - s, first and s == 0)
                    dve.wait_ge(s_hp, k + 1)
                    nc.vector.tensor_copy(heads[:, bass.ds(k, 1), 0:HG], hp[:, s, None, 0:HG]).then_inc(s_h, 1)
                put(0, 0, True)
                pairs(dve, NW, keep)
                dve.wait_ge(s_h, NW)
                for n, to in ((0, heads[:, :, HG:ROW]), (1, adst[:, :, :])):
                    me.link(nc.vector.tensor_tensor(prod[:, :, :], heads[:, :, 0:HG],
                                                    atts[:, n:n + 1, :].to_broadcast([P, NW, HG]), ALU.mult))
                    me.link(nc.vector.tensor_reduce(to, prod[:, :, :].rearrange("p w (h e) -> p w h e", e=NE), AX.X, ALU.add))
                dve.sem_inc(s_tab)

            @block.scalar
            def _(act):
                def square(k, i, s, first, last):
                    if not first:
                        act.wait_ge(s_hsq, k - 1)
                    nc.scalar.activation(sq[:, s, :], Z[:, bass.ds(k, 1), :].rearrange("p a d -> p (a d)"),
                                         ACT.Square).then_inc(s_sq, 1)
                act.wait_ge(s_d, 1)
                pairs(act, NW, square)
                take_root(nc, act, scale[:, :], root[:, :], s_ask, s_root, 1)
                square_rows(nc, act, Z, sq, rstd, s_sub, s_each, s_all)
                take_root(nc, act, rstd[:, :], root[:, 0:NW], s_ask, s_root, 2)

                def copy(k, i, s, first, last):
                    act.wait_ge(s_tp, k + 1)
                    if not first:
                        act.wait_ge(s_hp, k - 1)
                    nc.scalar.copy(zt[:, s, :, :], tp[:, s, :, :]).then_inc(s_zt, 1)
                pairs(act, NW, copy)

            @block.tensor
            def _(pe):
                pe.wait_ge(s_y, 1)
                nc.tensor.matmul(total[:, 0, 0:D], c["ones"][0:LASTROWS, :], Z[0:LASTROWS, NW - 1, :], start=True, stop=False)
                with pe.Fori(0, NW - 2) as k:
                    nc.tensor.matmul(total[:, 0, 0:D], c["ones"][:, :], Z[:, bass.ds(k, 1), :].rearrange("p a d -> p (a d)"),
                                     start=False, stop=False)
                nc.tensor.matmul(total[:, 0, 0:D], c["ones"][:, :], Z[:, NW - 2, :], start=False, stop=True).then_inc(s_cs, 1)

                def squares(k, i, s, first, last):
                    pe.wait_ge(s_sq, k + 1)
                    n = LASTROWS if last else P
                    nc.tensor.matmul(total[:, 1, 0:D], c["ones"][0:n, :], sq[0:n, s, :],
                                     start=first and s == 0, stop=last).then_inc(s_hsq, 1)
                pairs(pe, NW, squares)
                pe.wait_ge(s_hsq, NW)
                pe.sem_inc(s_cs2)

                def turn(k, s, first):
                    pe.wait_ge(s_stage, k + 1)
                    if not first:
                        pe.wait_ge(s_zt, k - 1)
                    for q in range(KC):
                        m = nc.tensor.transpose(tp[:, s, q, :], stage[:, s, q * P:(q + 1) * P], c["ident"][:, :])
                    m.then_inc(s_tp, 1)

                def product(k, i, s, first, last):
                    if not last:
                        turn(k + 1, 1 - s, first and s == 0)
                    pe.wait_ge(s_zt, k + 1)
                    if not first:
                        pe.wait_ge(s_h, k - 1)
                    for q in range(KC):
                        m = nc.tensor.matmul(hp[:, s, 0:HG], zt[:, s, q, :], wg[:, q, :], start=(q == 0), stop=(q == KC - 1))
                    m.then_inc(s_hp, 1)
                turn(0, 0, True)
                pairs(pe, NW, product)


TB = 4


def attention_max(nc, c, ps, table, idx, lo_f, H, most):
    batches = tiles_bound(E_FFN) // GT
    with ExitStack() as ctx:
        def sb(name, shape, dt):
            return ctx.enter_context(nc.sbuf_tensor("a_" + name, shape, dt))

        def sem(name):
            return c["sems"].enter_context(nc.alloc_semaphore("a_" + name))
        ring = sb("ring", [P, 2, GT], U32)
        got = sb("got", [P, 2, GT, ROW], F32)
        parts = sb("parts", [P, 2, GT, 2, HEADS], BF16)
        turned = sb("turned", [2 * HEADS, 2, GT, P], BF16)
        hot = sb("hot", [P, 2, GT, P], BF16)
        other = sb("other", [P, 2, GT, P], BF16)
        term = ps[:, 0:TB, :].rearrange("p j (h q) -> p j h q", q=P)
        tp = ps[0:2 * HEADS, 4:6, :].bitcast(BF16)[:, :, 0:GT * P].rearrange("p s (j q) -> p s j q", q=P)
        s_idx, s_hi, s_parts, s_eq, s_hot, s_tp, s_turned, s_term, s_most, s_keep, s_tick = (
            sem(n) for n in ("idx", "hi", "parts", "eq", "hot", "tp", "turned", "term", "most", "keep", "tick"))
        s_got = [sem("got0"), sem("got1")]
        with nc.Block() as block:
            @block.scalar
            def _(act):
                def mask(k, s, first):
                    act.wait_ge(s_eq, k + 1)
                    if not first:
                        act.wait_ge(s_term, k * GT - GT)
                    nc.scalar.activation(other[:, s, :, :], hot[:, s, :, :], ACT.Copy, bias=-BIG,
                                         scale=BIG).then_inc(s_hot, 1)

                def rows(k, i, s, first, last):
                    if not first:
                        act.wait_ge(s_got[s], i * (16 * GT))
                    nc.scalar.copy(ring[:, s, :], idx[:, bass.ds(k * GT, GT)]).then_inc(s_idx, 1)

                def keep(k, i, s, first, last):
                    mask(k, s, first)
                    act.wait_ge(s_got[s], i * (16 * GT) + 16 * GT)
                    nc.scalar.copy(H[:, bass.ds(k * GT, GT), :], got[:, s, :, :]).then_inc(s_keep, 1)
                    act.wait_ge(s_tp, k + 1)
                    nc.scalar.copy(turned[:, s, :, :], tp[:, s, :, :]).then_inc(s_turned, 1)
                    if type(k) is not int or k + 2 < batches:
                        rows(k + 2, i + 1, s, False, False)
                rows(0, 0, 0, True, False)
                rows(1, 0, 1, True, False)
                pairs_but_last(act, batches, keep)

            @block.gpsimd
            def _(pool):
                def gather(k, i, s, first, last):
                    pool.wait_ge(s_idx, k + 1)
                    pool.sem_inc(s_tick)
                    if not first:
                        pool.wait_ge(s_keep, k - 1)
                        pool.sem_inc(s_tick)
                        pool.wait_ge(s_parts, k - 1)
                        pool.sem_inc(s_tick)
                    for j in range(GT):
                        nc.gpsimd.indirect_dma_start(
                            out=got[:, s, j, :], out_offset=None, in_=table,
                            in_offset=bass.IndirectOffsetOnAxis(ap=ring[:, s, j:j + 1], axis=0),
                            bounds_check=NP - 1, oob_is_err=False).then_inc(s_got[s], 16)
                pairs(pool, batches, gather)

            @block.vector
            def _(dve):
                def one_hot(k, s, first):
                    if not first:
                        dve.wait_ge(s_hot, k - 1)
                        dve.wait_ge(s_term, k * GT - GT)
                    nc.vector.tensor_tensor(hot[:, s, :, :], c["iota_b"][:, None, :].to_broadcast([P, GT, P]),
                                            lo_f[:, bass.ds(k * GT, GT), None].to_broadcast([P, GT, P]),
                                            ALU.is_equal).then_inc(s_eq, 1)

                def split(k, i, s, first):
                    dve.wait_ge(s_got[s], i * (16 * GT) + 16 * GT)
                    if not first:
                        dve.wait_ge(s_tp, k - 1)
                    nc.vector.tensor_copy(parts[:, s, :, 0, :], got[:, s, :, HG:ROW]).then_inc(s_hi, 1)
                    dve.wait_ge(s_hi, k + 1)
                    nc.vector.tensor_tensor(parts[:, s, :, 1, :], got[:, s, :, HG:ROW], parts[:, s, :, 0, :],
                                            ALU.subtract).then_inc(s_parts, 1)

                def largest(k, i, s, first, last):
                    if not last:
                        one_hot(k + 1, 1 - s, first and s == 0)
                        split(k + 1, i + s, 1 - s, first and s == 0)
                    for j in range(GT):
                        dve.wait_ge(s_term, k * GT + j + 1)
                        nc.vector.tensor_reduce(most[:, bass.ds(k * GT + j, 1), :].rearrange("p a h -> p (a h)"),
                                                term[:, j % TB, :, :], AX.X, ALU.max).then_inc(s_most, 1)
                one_hot(0, 0, True)
                split(0, 0, 0, True)
                pairs(dve, batches, largest)

            @block.tensor
            def _(pe):
                def turn(k, s, first):
                    pe.wait_ge(s_parts, k + 1)
                    if not first:
                        pe.wait_ge(s_turned, k - 1)
                    for j in range(GT):
                        m = nc.tensor.transpose(tp[:, s, j, :], parts[:, s, j, :, :].rearrange("p a h -> p (a h)"),
                                                c["ident_b"][:, :])
                    m.then_inc(s_tp, 1)

                def product(k, i, s, first, last):
                    if not last:
                        turn(k + 1, 1 - s, first and s == 0)
                    pe.wait_ge(s_hot, k + 1)
                    pe.wait_ge(s_turned, k + 1)
                    for j in range(GT):
                        if not (first and s == 0 and j < TB):
                            pe.wait_ge(s_most, k * GT + j - TB + 1)
                        nc.tensor.matmul(term[:, j % TB, :, :], other[:, s, j, :],
                                         c["ident_b"][:, None, :].to_broadcast([P, HEADS, P]), start=True, stop=False)
                        for h in range(HEADS):
                            m = nc.tensor.matmul(term[:, j % TB, h, :], c["pick"][:, h, :], turned[:, s, j, :],
                                                 start=False, stop=(h == HEADS - 1))
                        m.then_inc(s_term, 1)
                turn(0, 0, True)
                pairs(pe, batches, product)


ST = 8


def three_parts(nc, me_did, me_settle, parts, rest, value):
    me_did(nc.vector.tensor_copy(parts[0], value))
    me_settle()
    me_did(nc.vector.tensor_tensor(rest, value, parts[0], ALU.subtract))
    me_settle()
    me_did(nc.vector.tensor_copy(parts[1], rest))
    me_settle()
    me_did(nc.vector.tensor_tensor(parts[2], rest, parts[1], ALU.subtract))


def attention_sums(nc, c, ps, H, lo_f, win_row, node):
    batches = tiles_bound(E_FFN) // ST
    with ExitStack() as ctx:
        def sb(name, shape, dt=F32):
            return ctx.enter_context(nc.sbuf_tensor("s_" + name, shape, dt))

        def sem(name):
            return c["sems"].enter_context(nc.alloc_semaphore("s_" + name))
        hot = sb("hot", [P, 2, ST, P], BF16)
        turned = sb("turned", [P, 2, ST, P], BF16)
        thirds = sb("thirds", [P, 2, 3, ST, ROW], BF16)
        rest = sb("rest", [P, ST, ROW])
        edge = sb("edge", [P, ST, HEADS])
        steep = sb("steep", [P, ST, HEADS])
        expo = sb("expo", [P, 2, ST, HEADS])
        msg = sb("msg", [P, 2, ST, ROW])
        tp = ps[:, 0:2, :].bitcast(BF16).rearrange("p s (j q) -> p s j q", q=P)
        at = ps[:, 4:6, :]
        part = ps[:, 6:8, :]
        s_third = sem("third")
        s_hot, s_tp, s_turned, s_at, s_e, s_x, s_ee, s_msg, s_part, s_sum = (
            sem(n) for n in ("hot", "tp", "turned", "at", "e", "x", "ee", "msg", "part", "sum"))

        def at_of(s):
            return at[:, s, 0:ST * 2 * HEADS].rearrange("p (j a h) -> p j a h", a=2, h=HEADS)

        def part_of(s):
            return part[:, s, 0:ST * ROW].rearrange("p (j r) -> p j r", r=ROW)
        with nc.Block() as block:
            @block.vector
            def _(dve):
                def one_hot(k, s, first):
                    if not first:
                        dve.wait_ge(s_part, k - 1)
                    nc.vector.tensor_tensor(hot[:, s, :, :], c["iota_b"][:, None, :].to_broadcast([P, ST, P]),
                                            lo_f[:, bass.ds(k * ST, ST), None].to_broadcast([P, ST, P]),
                                            ALU.is_equal).then_inc(s_hot, 1)

                def exponents(k, s, first):
                    dve.wait_ge(s_at, k + 1)
                    nc.vector.tensor_tensor(edge[:, :, :], H[:, bass.ds(k * ST, ST), HG:ROW], at_of(s)[:, :, 0, :],
                                            ALU.add).then_inc(s_e, 1)
                    dve.wait_ge(s_e, k * 3 + 1)
                    nc.vector.scalar_tensor_tensor(steep[:, :, :], edge[:, :, :], 0.2, edge[:, :, :], ALU.mult,
                                                   ALU.max).then_inc(s_e, 1)
                    dve.wait_ge(s_e, k * 3 + 2)
                    nc.vector.tensor_tensor(edge[:, :, :], steep[:, :, :], at_of(s)[:, :, 1, :],
                                            ALU.subtract).then_inc(s_e, 1)
                    dve.wait_ge(s_e, k * 3 + 3)
                    if not first:
                        dve.wait_ge(s_ee, k - 1)
                    nc.vector.tensor_scalar(expo[:, s, :, :], edge[:, :, :], 60.0, None, ALU.min).then_inc(s_x, 1)

                def weigh(k, i, s, first, last):
                    dve.wait_ge(s_ee, k + 1)
                    nc.vector.tensor_tensor(
                        msg[:, s, :, 0:HG].rearrange("p j (h e) -> p j h e", e=NE),
                        H[:, bass.ds(k * ST, ST), 0:HG].rearrange("p j (h e) -> p j h e", e=NE),
                        msg[:, s, :, HG:ROW, None].to_broadcast([P, ST, HEADS, NE]), ALU.mult).then_inc(s_third, 1)
                    dve.wait_ge(s_third, k * 4 + 1)
                    nc.vector.tensor_copy(thirds[:, s, 0, :, :], msg[:, s, :, :]).then_inc(s_third, 1)
                    dve.wait_ge(s_third, k * 4 + 2)
                    nc.vector.tensor_tensor(rest[:, :, :], msg[:, s, :, :], thirds[:, s, 0, :, :],
                                            ALU.subtract).then_inc(s_third, 1)
                    dve.wait_ge(s_third, k * 4 + 3)
                    nc.vector.tensor_copy(thirds[:, s, 1, :, :], rest[:, :, :]).then_inc(s_third, 1)
                    dve.wait_ge(s_third, k * 4 + 4)
                    nc.vector.tensor_tensor(thirds[:, s, 2, :, :], rest[:, :, :], thirds[:, s, 1, :, :],
                                            ALU.subtract).then_inc(s_msg, 1)
                    if not last:
                        exponents(k + 1, 1 - s, first and s == 0)
                    dve.wait_ge(s_part, k + 1)
                    nc.vector.tensor_scalar(H[:, bass.ds(k * ST, ST), :], part_of(s), 1.0, None, ALU.mult).then_inc(s_sum, 1)
                    if type(k) is not int or k + 2 < batches:
                        one_hot(k + 2, s, False)
                one_hot(0, 0, True)
                one_hot(1, 1, True)
                exponents(0, 0, True)
                pairs_but_last(dve, batches, weigh)

            @block.scalar
            def _(act):
                def copy(k, s, first):
                    act.wait_ge(s_tp, k + 1)
                    if not first:
                        act.wait_ge(s_at, k - 1)
                    nc.scalar.copy(turned[:, s, :, :], tp[:, s, :, :]).then_inc(s_turned, 1)

                def weights(k, i, s, first, last):
                    if not last:
                        copy(k + 1, 1 - s, first and s == 0)
                    act.wait_ge(s_x, k + 1)
                    if not first:
                        act.wait_ge(s_part, k - 1)
                    nc.scalar.activation(msg[:, s, :, HG:ROW], expo[:, s, :, :], ACT.Exp).then_inc(s_ee, 1)
                copy(0, 0, True)
                pairs(act, batches, weights)

            @block.tensor
            def _(pe):
                def turn(k, s, first):
                    pe.wait_ge(s_hot, k + 1)
                    if not first:
                        pe.wait_ge(s_turned, k - 1)
                    for j in range(ST):
                        m = nc.tensor.transpose(tp[:, s, j, :], hot[:, s, j, :], c["ident_b"][:, :])
                    m.then_inc(s_tp, 1)

                def bring(k, s, first):
                    wins = window_values(nc, win_row, k * ST, ST, mybir.EngineType.PE)
                    pe.wait_ge(s_turned, k + 1)
                    if not first:
                        pe.wait_ge(s_x, k - 1)
                    for j in range(ST):
                        for q in range(3):
                            m = nc.tensor.matmul(at_of(s)[:, j, :, :].rearrange("p a h -> p (a h)"), turned[:, s, j, :],
                                                 node[:, bass.ds(wins[j], 1), q, :].rearrange("p a h -> p (a h)"),
                                                 start=(q == 0), stop=(q == 2))
                    m.then_inc(s_at, 1)

                def product(k, i, s, first, last):
                    if not last:
                        bring(k + 1, 1 - s, first and s == 0)
                    pe.wait_ge(s_msg, k + 1)
                    if not first:
                        pe.wait_ge(s_sum, k - 1)
                    for j in range(ST):
                        for q in range(3):
                            m = nc.tensor.matmul(part_of(s)[:, j, :], hot[:, s, j, :], thirds[:, s, q, j, :],
                                                 start=(q == 0), stop=(q == 2))
                    m.then_inc(s_part, 1)
                    if type(k) is not int or k + 2 < batches:
                        turn(k + 2, s, False)
                turn(0, 0, True)
                turn(1, 1, True)
                bring(0, 0, True)
                pairs_but_last(pe, batches, product)


def last_of_windows(nc, eng, take, last_tile):
    each = 7
    with eng.Fori(0, NW // each) as i:
        at = nc.values_load_multi_w_load_instructions(
            last_tile[0:1, bass.ds(i * each, each)], engines=[mybir.EngineType.DVE], min_val=0,
            max_val=tiles_bound(E_FFN) - 1, skip_runtime_bounds_check_because="tiles are counted on the chip")[1]
        for n in range(each):
            take(i * each + n, at[n])


def node_maxima(nc, c, most, runs, adst, heads, top, node3, sums):
    same, last_tile, filled = runs
    nt = tiles_bound(E_FFN)
    with ExitStack() as ctx:
        def sb(name, shape):
            return ctx.enter_context(nc.sbuf_tensor("x_" + name, shape, F32))

        def sem(name):
            return c["sems"].enter_context(nc.alloc_semaphore("x_" + name))
        raw = sb("raw", [P, NW, HEADS])
        loop = sb("loop", [P, NW, HEADS])
        fresh = sb("fresh", [P, nt])
        none = sb("none", [P, NW])
        node = sb("node", [P, NW, 2 * HEADS])
        rest = sb("rest", [P, NW, 2 * HEADS])
        s_dve, s_e, s_x, s_top = sem("dve"), sem("e"), sem("x"), sem("top")
        with nc.Block() as block:
            @block.vector
            def _(dve):
                me = Steps(dve, s_dve)
                me.link(nc.vector.tensor_scalar(fresh[:, :], same[:, 0:nt], -1.0, BIG, ALU.add, ALU.mult))
                me.link(nc.vector.tensor_scalar(none[:, :], filled[:, :], -1.0, BIG, ALU.add, ALU.mult))
                for h in range(HEADS):
                    me.did(nc.vector.tensor_tensor_scan(most[:, :, h], fresh[:, :], most[:, :, h], -BIG, ALU.add, ALU.max))
                me.settle()
                last_of_windows(nc, dve, lambda w, t: nc.vector.tensor_copy(
                    top[:, bass.ds(w, 1), :], most[:, bass.ds(t, 1), :]).then_inc(s_top, 1), last_tile)
                dve.wait_ge(s_top, NW)
                me.link(nc.vector.tensor_tensor(top[:, :, :], top[:, :, :], none[:, :, None].to_broadcast([P, NW, HEADS]), ALU.add))
                me.link(nc.vector.tensor_tensor(top[:, :, :], top[:, :, :], heads[:, :, HG:ROW], ALU.max))
                me.link(nc.vector.tensor_copy(node[:, :, 0:HEADS], adst[:, :, :]))
                me.link(nc.vector.tensor_tensor(raw[:, :, :], top[:, :, :], adst[:, :, :], ALU.add))
                me.link(nc.vector.scalar_tensor_tensor(node[:, :, HEADS:2 * HEADS], raw[:, :, :], 0.2, raw[:, :, :],
                                                       ALU.mult, ALU.max))
                three_parts(nc, me.did, me.settle, [node3[:, :, q, :] for q in range(3)], rest[:, :, :], node[:, :, :])
                me.link(nc.vector.tensor_tensor(raw[:, :, :], heads[:, :, HG:ROW], adst[:, :, :], ALU.add))
                me.link(nc.vector.scalar_tensor_tensor(loop[:, :, :], raw[:, :, :], 0.2, raw[:, :, :], ALU.mult, ALU.max))
                me.link(nc.vector.tensor_tensor(raw[:, :, :], loop[:, :, :], node[:, :, HEADS:2 * HEADS], ALU.subtract))
                dve.sem_inc(s_e)
                dve.wait_ge(s_x, 1)
                nc.vector.tensor_tensor(sums[:, :, 0:HG].rearrange("p w (h e) -> p w h e", e=NE),
                                        heads[:, :, 0:HG].rearrange("p w (h e) -> p w h e", e=NE),
                                        sums[:, :, HG:ROW, None].to_broadcast([P, NW, HEADS, NE]), ALU.mult)

            @block.scalar
            def _(act):
                act.wait_ge(s_e, 1)
                nc.scalar.activation(sums[:, :, HG:ROW], raw[:, :, :], ACT.Exp).then_inc(s_x, 1)


def gates_of(nc, c, H, runs, sums, b_gat, ln_gamma, ln_beta, gates):
    same, last_tile, filled = runs
    nt = tiles_bound(E_FFN)
    with ExitStack() as ctx:
        def sb(name, shape):
            return ctx.enter_context(nc.sbuf_tensor("g_" + name, shape, F32))
        vecs = sb("vecs", [P, 3, HG])
        tiled = sb("tiled", [P, NW, ROW])
        s_last = c["sems"].enter_context(nc.alloc_semaphore("g_last"))
        den = sb("den", [P, NW, HEADS])
        agg = sb("agg", [P, NW, HG])
        sq = sb("sq", [P, NW, HG])
        one = sb("one", [P, NW])
        two = sb("two", [P, NW])
        root = sb("root", [P, NW])
        inv = sb("inv", [P, NW])
        s_ask = c["sems"].enter_context(nc.alloc_semaphore("g_ask"))
        s_root = c["sems"].enter_context(nc.alloc_semaphore("g_root"))
        score = sb("score", [P, NW, NE])
        rank = sb("rank", [P, NW, NE])
        gap = sb("gap", [P, NW, NE])
        s_w = c["sems"].enter_context(nc.alloc_semaphore("g_w"))
        s_dve = c["sems"].enter_context(nc.alloc_semaphore("g_dve"))
        s_e = c["sems"].enter_context(nc.alloc_semaphore("g_e"))
        s_x = c["sems"].enter_context(nc.alloc_semaphore("g_x"))
        with nc.Block() as block:
            @block.sync
            def _(sp):
                for n, v in enumerate((b_gat, ln_gamma, ln_beta)):
                    sp.dma_start(vecs[:, n, :], v.rearrange("(a h) -> a h", a=1).to_broadcast([P, HG])).then_inc(s_w, 16)

            @block.vector
            def _(dve):
                me = Steps(dve, s_dve)
                v = nc.vector

                def spread(x, n):
                    return x[:, :, None].to_broadcast([P, NW, n])
                for r in range(ROW):
                    me.did(v.tensor_tensor_scan(H[:, :, r], same[:, 0:nt], H[:, :, r], 0.0, ALU.mult, ALU.add))
                me.settle()
                last_of_windows(nc, dve, lambda w, t: nc.vector.tensor_copy(
                    tiled[:, bass.ds(w, 1), :], H[:, bass.ds(t, 1), :]).then_inc(s_last, 1), last_tile)
                dve.wait_ge(s_last, NW)
                me.link(v.tensor_tensor(tiled[:, :, :], tiled[:, :, :], spread(filled, ROW), ALU.mult))
                me.link(v.tensor_tensor(sums[:, :, :], sums[:, :, :], tiled[:, :, :], ALU.add))
                me.link(v.tensor_scalar(den[:, :, :], sums[:, :, HG:ROW], 1e-16, None, ALU.add))
                me.link(v.reciprocal(den[:, :, :], den[:, :, :]))
                me.link(v.tensor_tensor(agg[:, :, :].rearrange("p w (h e) -> p w h e", e=NE),
                                        sums[:, :, 0:HG].rearrange("p w (h e) -> p w h e", e=NE),
                                        den[:, :, :, None].to_broadcast([P, NW, HEADS, NE]), ALU.mult))
                dve.wait_ge(s_w, 48)
                me.link(v.tensor_tensor(agg[:, :, :], agg[:, :, :], vecs[:, 0:1, :].to_broadcast([P, NW, HG]), ALU.add))
                me.link(v.tensor_reduce(one[:, :], agg[:, :, :], AX.X, ALU.add))
                me.link(v.tensor_scalar(one[:, :], one[:, :], 1.0 / HG, None, ALU.mult))
                me.link(v.tensor_tensor(agg[:, :, :], agg[:, :, :], spread(one, HG), ALU.subtract))
                me.link(v.tensor_tensor(sq[:, :, :], agg[:, :, :], agg[:, :, :], ALU.mult))
                me.link(v.tensor_reduce(two[:, :], sq[:, :, :], AX.X, ALU.add))
                me.link(v.tensor_scalar(two[:, :], two[:, :], 1.0 / HG, EPS, ALU.mult, ALU.add))
                inverse_root(nc, dve, me, two[:, :], root[:, :], inv[:, :], s_ask, s_root, 1)
                me.link(v.tensor_tensor(agg[:, :, :], agg[:, :, :], spread(two, HG), ALU.mult))
                me.link(v.tensor_tensor(agg[:, :, :], agg[:, :, :], vecs[:, 1:2, :].to_broadcast([P, NW, HG]), ALU.mult))
                me.link(v.tensor_tensor(agg[:, :, :], agg[:, :, :], vecs[:, 2:3, :].to_broadcast([P, NW, HG]), ALU.add))
                me.link(v.tensor_reduce(score[:, :, :], agg[:, :, :].rearrange("p w (h e) -> p w e h", e=NE), AX.X, ALU.add))
                me.link(v.tensor_scalar(score[:, :, :], score[:, :, :], 1.0 / HEADS, None, ALU.mult))
                for e in range(NE):
                    others = [j for j in range(NE) if j != e]
                    for n, j in enumerate(others):
                        op = ALU.is_ge if j < e else ALU.is_gt
                        to = rank[:, :, e] if n == 0 else one[:, :]
                        me.link(v.tensor_tensor(to, score[:, :, j], score[:, :, e], op))
                        if n:
                            me.link(v.tensor_tensor(rank[:, :, e], rank[:, :, e], one[:, :], ALU.add))
                me.link(v.tensor_reduce(two[:, :], score[:, :, :], AX.X, ALU.max))
                me.link(v.tensor_tensor(gap[:, :, :], score[:, :, :], spread(two, NE), ALU.subtract))
                dve.sem_inc(s_e)
                dve.wait_ge(s_x, 1)
                me.link(v.tensor_scalar(rank[:, :, :], rank[:, :, :], 1.5, None, ALU.is_lt))
                me.link(v.tensor_tensor(gates[:, :, :], gates[:, :, :], rank[:, :, :], ALU.mult))
                me.link(v.tensor_reduce(one[:, :], gates[:, :, :], AX.X, ALU.add))
                me.link(v.reciprocal(one[:, :], one[:, :]))
                me.link(v.tensor_tensor(gates[:, :, :], gates[:, :, :], spread(one, NE), ALU.mult))

            @block.scalar
            def _(act):
                take_root(nc, act, two[:, :], root[:, :], s_ask, s_root, 1)
                act.wait_ge(s_e, 1)
                nc.scalar.activation(gates[:, :, :], gap[:, :, :], ACT.Exp).then_inc(s_x, 1)


def experts(nc, c, ps, x2, xn, W1, b1, W2, b2, gates, out):
    T = 2
    groups = NW // T
    with ExitStack() as ctx:
        def sb(name, shape):
            return ctx.enter_context(nc.sbuf_tensor("e_" + name, shape, F32))


        def sem(name):
            return c["sems"].enter_context(nc.alloc_semaphore("e_" + name))
        w1 = sb("w1", [P, NE, KC, F])
        w2 = sb("w2", [P, NE, FC, D])
        b1c = sb("b1c", [P, NE, FC])
        b2r = sb("b2r", [NE, D])
        xin = sb("xin", [P, 2, T, D])
        res = sb("res", [P, 2, T, D])
        xt = sb("xt", [P, 2, KC, T, P])
        gs = sb("gs", [P, 2, T, NE])
        gt = sb("gt", [NE, 2, T, P])
        hid = sb("hid", [P, 2, FC, T, P])
        up = ps[:, 0:2, :].rearrange("p g (a t q) -> p g a t q", a=2, t=T)
        yp = ps[:, 2:4, :].rearrange("p g (t d) -> p g t d", t=T)
        yb = ps[:, 4, :].rearrange("p (t d) -> p t d", t=T)
        tp = ps[:, 5, :].rearrange("p (k t q) -> p k t q", k=KC, t=T)
        gp = ps[0:NE, 6, 0:T * P].rearrange("p (t q) -> p t q", q=P)
        s_w = sem("w")
        s_in = [sem("in0"), sem("in1")]
        s_res = [sem("res0"), sem("res1")]
        s_gs, s_tp, s_xt, s_up, s_hid, s_y, s_acc, s_st = (
            sem(n) for n in ("gs", "tp", "xt", "up", "hid", "y", "acc", "st"))
        s_out = [sem("out0"), sem("out1")]
        NA = NE + 1
        with nc.Block() as block:
            @block.sync
            def _(sp):
                sp.dma_start(w1[:, :, :, :], W1.rearrange("e (k p) f -> p e k f", p=P)).then_inc(s_w, 16)
                sp.dma_start(w2[:, :, :, :], W2.rearrange("e (k p) d -> p e k d", p=P)).then_inc(s_w, 16)
                sp.dma_start(b2r[:, :], b2).then_inc(s_w, 16)
                with nc.allow_non_contiguous_dma(reason="bias vectors onto partitions"):
                    sp.dma_start(b1c[:, :, :], b1.rearrange("e (k p) -> p e k", p=P)).then_inc(s_w, 16)

                def load(k, i, s, first, last):
                    if not first:
                        sp.wait_ge(s_tp, k - 1)
                    rows = bass.ds(k * (T * P), T * P)
                    sp.dma_start(xin[:, s, :, :], xn[rows, :].rearrange("(t p) d -> p t d", p=P)).then_inc(s_in[s], 16)
                    if not first:
                        sp.wait_ge(s_out[s], i * 16)
                    sp.dma_start(res[:, s, :, :], x2[rows, :].rearrange("(t p) d -> p t d", p=P)).then_inc(s_res[s], 16)
                pairs(sp, groups, load)

            @block.gpsimd
            def _(pool):
                def store(k, i, s, first, last):
                    pool.wait_ge(s_acc, k * NA + NA)
                    pool.sem_inc(s_st)
                    if last:
                        pool.dma_start(out[k * T * P:(NW - 1) * P, :], res[:, s, 0, :]).then_inc(s_out[s], 16)
                        pool.dma_start(out[(NW - 1) * P:N, :], res[0:LASTROWS, s, 1, :]).then_inc(s_out[s], 16)
                    else:
                        pool.dma_start(out[bass.ds(k * (T * P), T * P), :].rearrange("(t p) d -> p t d", p=P),
                                       res[:, s, :, :]).then_inc(s_out[s], 16)
                pairs(pool, groups, store)
                pool.wait_ge(s_out[0], 16 * ((groups + 1) // 2) + (16 if groups % 2 else 0))
                pool.wait_ge(s_out[1], 16 * (groups // 2) + (0 if groups % 2 else 16))

            @block.tensor
            def _(pe):
                def product(k, i, s, first, last):
                    pe.wait_ge(s_in[s], i * 16 + 16)
                    pe.wait_ge(s_gs, k + 1)
                    if not (first and s == 0):
                        pe.wait_ge(s_xt, k)
                    for t in range(T):
                        for q in range(KC):
                            nc.tensor.transpose(tp[:, q, t, :], xin[:, s, t, q * P:(q + 1) * P], c["ident"][:, :])
                        m = nc.tensor.transpose(gp[:, t, :], gs[:, s, t, :], c["ident"][:, :])
                    m.then_inc(s_tp, 1)
                    if first and s == 0:
                        pe.wait_ge(s_w, 64)
                    pe.wait_ge(s_xt, k + 1)
                    if not (first and s == 0):
                        pe.wait_ge(s_acc, k * NA - NA + 1)
                    for t in range(T):
                        m = nc.tensor.matmul(yb[:, t, :], gt[:, s, t, :], b2r[:, :], start=True, stop=True)
                    m.then_inc(s_y, 1)

                    def up_of(e):
                        for g in range(2):
                            n = e * 2 + g
                            if not (first and s == 0 and n < 2):
                                pe.wait_ge(s_hid, k * (2 * NE) + n - 1)
                            for a in range(2):
                                f = g * 2 + a
                                for q in range(KC):
                                    m = nc.tensor.matmul(up[:, g, a, :, :], w1[:, e, q, f * P:(f + 1) * P],
                                                         xt[:, s, q, :, :], start=(q == 0), stop=(q == KC - 1))
                            m.then_inc(s_up, 1)

                    def down_of(e):
                        pe.wait_ge(s_hid, k * (2 * NE) + 2 * e + 2)
                        if not (first and s == 0 and e < 2):
                            pe.wait_ge(s_acc, k * NA + e if e >= 2 else k * NA - NA + NE + e)
                        for t in range(T):
                            for f in range(FC):
                                m = nc.tensor.matmul(yp[:, e % 2, t, :], hid[:, e % 2, f, t, :], w2[:, e, f, :],
                                                     start=(f == 0), stop=(f == FC - 1))
                        m.then_inc(s_y, 1)
                    up_of(0)
                    for e in range(NE):
                        if e + 1 < NE:
                            up_of(e + 1)
                        down_of(e)
                pairs(pe, groups, product)

            @block.scalar
            def _(act):
                def act_group(k, i, s, first, last):
                    for e in range(NE):
                        for g in range(2):
                            n = e * 2 + g
                            act.wait_ge(s_up, k * (2 * NE) + n + 1)
                            if not (first and s == 0 and e < 2):
                                act.wait_ge(s_y, k * NA + e if e >= 2 else k * NA - NA + NE + e)
                            for a in range(2):
                                f = g * 2 + a
                                m = nc.scalar.activation(hid[:, e % 2, f, :, :], up[:, g, a, :, :], ACT.Gelu,
                                                         bias=b1c[:, e, f:f + 1])
                            m.then_inc(s_hid, 1)
                pairs(act, groups, act_group)

            @block.vector
            def _(dve):
                def sum_group(k, i, s, first, last):
                    if not first:
                        dve.wait_ge(s_tp, k - 1)
                    nc.vector.tensor_copy(gs[:, s, :, :], gates[:, bass.ds(k * T, T), :]).then_inc(s_gs, 1)
                    dve.wait_ge(s_tp, k + 1)
                    nc.vector.tensor_copy(xt[:, s, :, :, :], tp[:, :, :, :])
                    nc.vector.tensor_copy(gt[:, s, :, :], gp[:, :, :]).then_inc(s_xt, 1)
                    dve.wait_ge(s_res[s], i * 16 + 16)
                    dve.wait_ge(s_y, k * NA + 1)
                    nc.vector.tensor_tensor(res[:, s, :, :], res[:, s, :, :], yb[:, :, :], ALU.add).then_inc(s_acc, 1)
                    for e in range(NE):
                        dve.wait_ge(s_y, k * NA + e + 2)
                        dve.wait_ge(s_acc, k * NA + e + 1)
                        for t in range(T):
                            m = nc.vector.scalar_tensor_tensor(res[:, s, t, :], yp[:, e % 2, t, :], gs[:, s, t, e:e + 1],
                                                               res[:, s, t, :], ALU.mult, ALU.add)
                        m.then_inc(s_acc, 1)
                pairs(dve, groups, sum_group)


def gnn_ffn(nc, x, src, dst, gW1, gb1, gW2, gb2, ggamma, gbeta, wgat, att_src, att_dst, b_gat, ln_gamma, ln_beta,
            fW1, fb1, fW2, fb2, edge_index, out):
    def dram(name, shape, dt=F32):
        return nc.dram_tensor(name, shape, dt, kind="Internal").ap()
    gnn_slots, ffn_slots = blocks_bound(E_GNN), blocks_bound(E_FFN)
    gnn_list = dram("gnn_list", [gnn_slots * P, 2], I32)
    ffn_list = dram("ffn_list", [ffn_slots * P, 2], I32)
    rows1 = dram("rows1", [NP, D])
    rows2 = dram("rows2", [NP, D])
    x2 = dram("x2", [NP, D])
    xn = dram("xn", [NP, D])
    rows3 = dram("rows3", [NP, ROW])
    with ExitStack() as ctx:
        def sb(name, shape, dt=F32):
            return ctx.enter_context(nc.sbuf_tensor(name, shape, dt))
        c = make_consts(nc, ctx, Signals(nc))
        ps = ctx.enter_context(nc.psum_tensor("ps", [P, 8, BANK], F32))
        ffn_idx = sb("ffn_idx", [P, ffn_slots], U32)
        ffn_lo = sb("ffn_lo", [P, ffn_slots])
        ffn_win = sb("ffn_win", [1, ffn_slots], I32)
        runs = (sb("same", [P, ffn_slots]), sb("last_tile", [1, NW], I32), sb("filled", [P, NW]))
        heads = sb("heads", [P, NW, ROW])
        adst = sb("adst", [P, NW, HEADS])
        with ExitStack() as gctx:
            def gsb(name, shape, dt=F32):
                return gctx.enter_context(nc.sbuf_tensor(name, shape, dt))
            gnn_idx = gsb("gnn_idx", [P, gnn_slots], U32)
            gnn_lo = gsb("gnn_lo", [P, gnn_slots])
            gnn_win = gsb("gnn_win", [1, gnn_slots], I32)
            deg = gsb("deg", [P, NW])
            deg_ffn = gsb("deg_ffn", [P, NW])
            dinv = gsb("dinv", [P, NW])
            bin_edges(nc, c, ps, "p_", E_GNN, src, dst, gnn_list, gnn_idx, gnn_lo, gnn_win, deg)
            c["sems"].give_back()
            bin_edges(nc, c, ps, "q_", E_FFN, edge_index[0], edge_index[1], ffn_list, ffn_idx, ffn_lo, ffn_win, deg_ffn, runs)
            c["sems"].give_back()
            with nc.sbuf_tensor("Z", [P, NW, D], F32) as Z:
                first_norm(nc, c, x, Z, deg, dinv, rows1)
                c["sems"].give_back()
                convolve(nc, c, ps, "u_", rows1, Z, gnn_idx, gnn_lo, gnn_win)
                c["sems"].give_back()
                between(nc, c, ps, gW1, gb1, gW2, Z, dinv, rows2)
                c["sems"].give_back()
                convolve(nc, c, ps, "v_", rows2, Z, gnn_idx, gnn_lo, gnn_win)
                c["sems"].give_back()
                batch_norm(nc, c, ps, x, gb2, ggamma, gbeta, wgat, att_src, att_dst, Z, dinv, x2, xn, heads, adst, rows3)
                c["sems"].give_back()
        gates = sb("gates", [P, NW, NE])
        with ExitStack() as actx:
            def asb(name, shape, dt=F32):
                return actx.enter_context(nc.sbuf_tensor(name, shape, dt))
            H = asb("H", [P, tiles_bound(E_FFN), ROW])
            top = asb("top", [P, NW, HEADS])
            node = asb("node", [P, NW, 3, 2 * HEADS], BF16)
            sums = asb("sums", [P, NW, ROW])
            with nc.sbuf_tensor("most", [P, tiles_bound(E_FFN), HEADS], F32) as most:
                attention_max(nc, c, ps, rows3, ffn_idx, ffn_lo, H, most)
                c["sems"].give_back()
                node_maxima(nc, c, most, runs, adst, heads, top, node, sums)
            attention_sums(nc, c, ps, H, ffn_lo, ffn_win, node)
            c["sems"].give_back()
            gates_of(nc, c, H, runs, sums, b_gat, ln_gamma, ln_beta, gates)
            c["sems"].give_back()
        experts(nc, c, ps, x2, xn, fW1, fb1, fW2, fb2, gates, out)


_INS = ["x", "src", "dst", "L0_gnn_W1", "L0_gnn_b1", "L0_gnn_W2", "L0_gnn_b2", "L0_gnn_gamma", "L0_gnn_beta",
        "L0_ffn_W_gat", "L0_ffn_att_src", "L0_ffn_att_dst", "L0_ffn_b_gat", "L0_ffn_ln_gamma", "L0_ffn_ln_beta",
        "L0_ffn_W1", "L0_ffn_b1", "L0_ffn_W2", "L0_ffn_b2", "L0_ffn_edge_index"]


def kernel(**inputs):
    import concourse.bacc as bacc
    from concourse.bass_utils import run_bass_kernel_spmd

    nc = bacc.Bacc("TRN2", target_bir_lowering=False, num_devices=1)
    arrays, args = {}, []
    for name in _INS:
        a = np.ascontiguousarray(inputs[name])
        arrays[f"in_{name}"] = a
        args.append(nc.dram_tensor(f"in_{name}", a.shape, mybir.dt.from_np(a.dtype), kind="ExternalInput").ap())
    args.append(nc.dram_tensor("out", (N, D), F32, kind="ExternalOutput").ap())
    gnn_ffn(nc, *args)
    r = run_bass_kernel_spmd(nc, [arrays], core_ids=[0])
    return r.results[0]["out"]
```

```python
import numpy as np
import concourse.bass as bass
from concourse import mybir
from contextlib import ExitStack

F32 = mybir.dt.float32
BF16 = mybir.dt.bfloat16
I32 = mybir.dt.int32
U32 = mybir.dt.uint32
ALU = mybir.AluOpType
ACT = mybir.ActivationFunctionType
AX = mybir.AxisListType

P = 128
N = 12500
D = 256
NW = (N + P - 1) // P
NP = NW * P
LASTROWS = N - (NW - 1) * P
KC = D // P
E_GNN = 200000
E_FFN = 131072
HEADS = 4
NE = 4
HG = HEADS * NE
ROW = HG + HEADS
F = 512
FC = F // P
EPS = 1e-5
B = 5
NB_W = NW + 1
PADLO = 255
BIG = 1e30
GT = 8
BANK = 512


def tiles_bound(edges):
    most = (edges + NW * (P - 1)) // P
    return (most + 7) // 8 * 8


def blocks_bound(edges):
    return (tiles_bound(edges) + P - 1) // P * P


def pairs(eng, n, body):
    body(0, 0, 0, True, False)
    body(1, 0, 1, True, n == 2)
    end = n // 2 if n % 2 else n // 2 - 1
    with eng.Fori(1, end) as i:
        body(i * 2, i, 0, False, False)
        body(i * 2 + 1, i, 1, False, False)
    if n % 2:
        body(n - 1, n // 2, 0, False, True)
    else:
        body(n - 2, n // 2 - 1, 0, False, False)
        body(n - 1, n // 2 - 1, 1, False, True)


def pairs_but_last(eng, n, body):
    body(0, 0, 0, True, False)
    body(1, 0, 1, True, False)
    end = n // 2 - 1
    with eng.Fori(1, end) as i:
        body(i * 2, i, 0, False, False)
        body(i * 2 + 1, i, 1, False, False)
    for k in range(2 * end, n):
        body(k, k // 2, k % 2, False, k == n - 1)


def threes(eng, n, body):
    assert n % 3 == 0 and n > 6
    for k in range(3):
        body(k, k)
    with eng.Fori(1, n // 3 - 1) as i:
        for s in range(3):
            body(i * 3 + s, s)
    for k in range(n - 3, n):
        body(k, k % 3)


def past(k, least):
    return type(k) is not int or k >= least


def more(k, ahead, n):
    return type(k) is not int or k + ahead < n


class Signals:

    def __init__(self, nc):
        self.nc, self.taken = nc, []

    def enter_context(self, handle):
        self.taken.append(handle)
        return handle

    def give_back(self):
        self.nc.clear_and_free_semaphores(self.taken)
        self.taken = []
        self.nc.all_engine_barrier()


class Steps:

    def __init__(self, eng, sem):
        self.eng, self.sem, self.n = eng, sem, 0

    def did(self, instruction):
        instruction.then_inc(self.sem, 1)
        self.n += 1

    def settle(self):
        self.eng.wait_ge(self.sem, self.n)

    def link(self, instruction):
        self.did(instruction)
        self.settle()


def window_values(nc, row, start, count, engine):
    return nc.values_load_multi_w_load_instructions(
        row[0:1, bass.ds(start, count)], engines=[engine], min_val=0, max_val=NW - 1,
        skip_runtime_bounds_check_because="the table is clamped to the last window")[1]


def inverse_root(nc, dve, me, v, root, inv, s_ask, s_root, n):
    dve.sem_inc(s_ask)
    dve.wait_ge(s_root, n)
    me.link(nc.vector.reciprocal(inv, root))
    me.link(nc.vector.tensor_tensor(root, inv, inv, ALU.mult))
    me.link(nc.vector.tensor_tensor(root, root, v, ALU.mult))
    me.link(nc.vector.tensor_scalar(root, root, -0.5, 1.5, ALU.mult, ALU.add))
    me.link(nc.vector.tensor_tensor(v, root, inv, ALU.mult))


def take_root(nc, act, v, root, s_ask, s_root, n):
    act.wait_ge(s_ask, n)
    nc.scalar.activation(root, v, ACT.Sqrt).then_inc(s_root, 1)


def make_consts(nc, ctx, sems):
    def sb(name, shape, dt):
        return ctx.enter_context(nc.sbuf_tensor(name, shape, dt))
    c = {
        "sems": sems,
        "iota_i": sb("iota_i", [P, P], I32), "iota_f": sb("iota_f", [P, P], F32),
        "iota_b": sb("iota_b", [P, P], BF16),
        "ident": sb("ident", [P, P], F32), "ident_b": sb("ident_b", [P, P], BF16),
        "before": sb("before", [P, P], BF16), "notbefore": sb("notbefore", [P, P], BF16),
        "upto": sb("upto", [P, P], F32), "ones": sb("ones", [P, P], F32),
        "ones_b": sb("ones_b", [P, P], BF16), "zeros_b": sb("zeros_b", [P, P], BF16),
        "pick": sb("pick", [2 * HEADS, HEADS, P], BF16),
    }
    s_io = c["sems"].enter_context(nc.alloc_semaphore("c_iota"))
    s_set = c["sems"].enter_context(nc.alloc_semaphore("c_set"))
    s_sel = c["sems"].enter_context(nc.alloc_semaphore("c_sel"))
    with nc.Block() as block:
        @block.gpsimd
        def _(pool):
            nc.gpsimd.iota(c["iota_i"][:, :], [[1, P]], base=0, channel_multiplier=0).then_inc(s_io, 1)
            pool.wait_ge(s_set, 8)
            nc.gpsimd.affine_select(out=c["ident"][:, :], in_=c["ident"][:, :], compare_op=ALU.not_equal,
                                    fill=1.0, base=0, pattern=[[-1, P]], channel_multiplier=1)
            nc.gpsimd.affine_select(out=c["ident_b"][:, :], in_=c["ident_b"][:, :], compare_op=ALU.not_equal,
                                    fill=1.0, base=0, pattern=[[-1, P]], channel_multiplier=1)
            nc.gpsimd.affine_select(out=c["before"][:, :], in_=c["before"][:, :], compare_op=ALU.is_ge,
                                    fill=1.0, base=0, pattern=[[-1, P]], channel_multiplier=1)
            nc.gpsimd.affine_select(out=c["notbefore"][:, :], in_=c["notbefore"][:, :], compare_op=ALU.is_ge,
                                    fill=0.0, base=0, pattern=[[-1, P]], channel_multiplier=1)
            nc.gpsimd.affine_select(out=c["upto"][:, :], in_=c["upto"][:, :], compare_op=ALU.is_gt,
                                    fill=1.0, base=0, pattern=[[-1, P]], channel_multiplier=1)
            nc.gpsimd.affine_select(out=c["pick"][:, :, :], in_=c["pick"][:, :, :], compare_op=ALU.not_equal,
                                    fill=1.0, base=0, pattern=[[-1, HEADS], [0, P]],
                                    channel_multiplier=1).then_inc(s_sel, 1)
            pool.wait_ge(s_sel, 1)
            nc.gpsimd.affine_select(out=c["pick"][:, :, :], in_=c["pick"][:, :, :], compare_op=ALU.not_equal,
                                    fill=1.0, base=-HEADS, pattern=[[-1, HEADS], [0, P]],
                                    channel_multiplier=1).then_inc(s_sel, 1)

        @block.vector
        def _(dve):
            for name, v in (("ident", 0.0), ("ident_b", 0.0), ("before", 0.0), ("notbefore", 1.0),
                            ("upto", 0.0), ("ones", 1.0), ("ones_b", 1.0)):
                nc.vector.memset(c[name][:, :], v).then_inc(s_set, 1)
            nc.vector.memset(c["pick"][:, :, :], 0.0).then_inc(s_set, 1)
            nc.vector.memset(c["zeros_b"][:, :], 0.0)
            dve.wait_ge(s_io, 1)
            nc.vector.tensor_copy(c["iota_f"][:, :], c["iota_i"][:, :])
            nc.vector.tensor_copy(c["iota_b"][:, :], c["iota_i"][:, :])
    return c


class Placement:

    def __init__(self, nc, c, ps, tag, ctx, cols, listed, win_b, rec):
        self.nc, self.c, self.nb, self.listed, self.win_b, self.rec = nc, c, cols // B, listed, win_b, rec

        def sb(name, shape, dt):
            return ctx.enter_context(nc.sbuf_tensor(tag + name, shape, dt))

        def sem(name):
            return c["sems"].enter_context(nc.alloc_semaphore(tag + name))
        self.place = ps[:, 2, 0:B * NB_W].rearrange("p (j w) -> p j w", w=NB_W)
        self.hot = sb("hot_w", [P, 2, B, NB_W], BF16)
        self.picked = sb("picked", [P, B, NB_W], F32)
        self.pos_f = sb("pos_f", [P, B], F32)
        self.pos = sb("pos", [P, 2, B], U32)
        self.ring = sb("rec_ring", [P, 2, B, 2], I32)
        self.s_hot, self.s_at, self.s_adv, self.s_read, self.s_red, self.s_pos, self.s_tick = (
            sem(x) for x in ("hot2", "at", "adv", "read", "red", "pos", "tick"))
        self.s_sc = [sem("sc0"), sem("sc1")]

    def start(self, base):
        return self.nc.tensor.matmul(self.place, self.c["ident"][:, :],
                                     base[:, None, :].to_broadcast([P, B, NB_W]), start=True, stop=True)

    def hot_windows(self, k, s):
        return self.nc.vector.tensor_tensor(
            self.hot[:, s, :, :], self.c["iota_b"][:, None, 0:NB_W].to_broadcast([P, B, NB_W]),
            self.win_b[:, bass.ds(k * B, B), None].to_broadcast([P, B, NB_W]), ALU.is_equal)

    def vector(self, dve, k, i, s, first):
        v = self.nc.vector
        if not first:
            dve.wait_ge(self.s_adv, k - 1)
        self.hot_windows(k, s).then_inc(self.s_hot, 1)
        dve.wait_ge(self.s_at, k + 1)
        v.tensor_tensor(self.picked[:, :, :], self.place, self.hot[:, s, :, :], ALU.mult).then_inc(self.s_read, 1)
        dve.wait_ge(self.s_read, k + 1)
        v.tensor_reduce(self.pos_f[:, :], self.picked[:, :, :], AX.X, ALU.add).then_inc(self.s_red, 1)
        if not first:
            dve.wait_ge(self.s_sc[s], i * (16 * B))
        dve.wait_ge(self.s_red, k + 1)
        v.tensor_copy(self.pos[:, s, :], self.pos_f[:, :])
        v.tensor_copy(self.ring[:, s, :, :], self.rec[:, bass.ds(k * B, B), :]).then_inc(self.s_pos, 1)

    def tensor(self, pe, k, s):
        mm, hot, c = self.nc.tensor.matmul, self.hot, self.c

        def add(to, n, lhs, j):
            return mm(self.place[:, to:to + n, :], lhs, hot[:, s, j:j + 1, :].to_broadcast([P, n, NB_W]) if n > 1
                      else hot[:, s, j:j + 1, :], start=False, stop=True, skip_group_check=True)
        pe.wait_ge(self.s_hot, k + 1)
        m = mm(self.place, c["before"][:, :], hot[:, s, :, :], start=False, stop=True, skip_group_check=True)
        for j in range(B - 1):
            m = add(j + 1, B - 1 - j, c["ones_b"][:, :], j)
        m.then_inc(self.s_at, 1)
        pe.wait_ge(self.s_read, k + 1)
        m = mm(self.place, c["notbefore"][:, :], hot[:, s, :, :], start=False, stop=True, skip_group_check=True)
        for j in range(1, B):
            m = add(0, j, c["ones_b"][:, :], j)
        m.then_inc(self.s_adv, 1)

    def gpsimd(self, pool, k, s):
        pool.wait_ge(self.s_pos, k + 1)
        pool.sem_inc(self.s_tick)
        for j in range(B):
            self.nc.gpsimd.indirect_dma_start(
                out=self.listed, out_offset=bass.IndirectOffsetOnAxis(ap=self.pos[:, s, j:j + 1], axis=0),
                in_=self.ring[:, s, j, :], in_offset=None,
                bounds_check=self.listed.shape[0] - 1, oob_is_err=False).then_inc(self.s_sc[s], 16)

    def settle(self, pool):
        pool.wait_ge(self.s_sc[0], 16 * B * ((self.nb + 1) // 2))
        pool.wait_ge(self.s_sc[1], 16 * B * (self.nb // 2))


def columns_of(edges):
    return (edges + P - 1) // P


def load_edges(sp, t, a, edges, s_ld):
    cols = columns_of(edges)
    full, rest = edges // cols, edges % cols
    sp.dma_start(t[0:full, 0:cols], a[0:full * cols].rearrange("(p n) -> p n", n=cols)).then_inc(s_ld, 16)
    if rest:
        sp.dma_start(t[full:full + 1, 0:rest], a[full * cols:edges].rearrange("(p n) -> p n", p=1)).then_inc(s_ld, 16)
    return 32 if rest else 16


def window_row(nc, c, dve, pe, ps, ntb, after, s_row, s_rowd, s_win, win_row, win_all, me):
    chunk = 416 if ntb % 416 == 0 else 384
    row = ps[:, 3, :]
    assert ntb % chunk == 0
    if pe:
        pe.wait_ge(s_row, 1)
    for q in range(ntb // chunk):
        at = slice(q * chunk, (q + 1) * chunk)
        if pe:
            if q:
                pe.wait_ge(s_win, q)
            nc.tensor.matmul(row[:, 0:chunk], c["ones"][0:NW, :], after[0:NW, at], start=True, stop=True).then_inc(s_rowd, 1)
        else:
            dve.wait_ge(s_rowd, q + 1)
            if win_all is not None:
                me.link(nc.vector.tensor_scalar(win_all[:, at], row[:, 0:chunk], float(NW - 1), None, ALU.min))
            nc.vector.tensor_scalar(win_row[0:1, at], row[0:1, 0:chunk], float(NW - 1), None, ALU.min).then_inc(s_win, 1)


def bin_edges(nc, c, ps, src, dst, listed, idx, lo_f, win_row, runs, gnn_dst, deg, windows_fall):
    edges = E_FFN
    cols = (columns_of(edges) + B - 1) // B * B
    nb = cols // B
    nt, ntb = tiles_bound(edges), blocks_bound(edges)
    slots = ntb * P
    same, last_tile, filled = runs
    gcols0 = columns_of(E_GNN)
    CB = (gcols0 + nb - 1) // nb
    gcols = CB * nb
    with ExitStack() as ctx:
        def sb(name, shape, dt):
            return ctx.enter_context(nc.sbuf_tensor("q_" + name, shape, dt))

        def sem(name):
            return c["sems"].enter_context(nc.alloc_semaphore("q_" + name))

        dst_i = sb("dst_i", [P, cols], I32)
        src_i = sb("src_i", [P, cols], I32)
        part_i = sb("part_i", [P, cols], I32)
        win_b = sb("win_b", [P, cols], BF16)
        rec = sb("rec", [P, cols, 2], I32)
        g_dst = sb("g_dst", [P, gcols], I32)
        g_part = sb("g_part", [P, gcols], I32)
        g_next = sb("g_next", [P, 1], I32)
        g_win = sb("g_win", [P, gcols], BF16)
        g_lo = sb("g_lo", [P, gcols], BF16)
        g_fall = sb("g_fall", [P, gcols], BF16)
        g_hot_w = sb("g_hot_w", [P, 2, CB, NW], BF16)
        g_hot_lo = sb("g_hot_lo", [P, 2, CB, P], BF16)
        falls = sb("falls", [P, 2], F32)
        fall_b = sb("fall_b", [P, 2], BF16)
        empty = sb("empty", [P, ntb, 2], I32)
        count_r = sb("count_r", [P, NB_W], F32)
        count_i = sb("count_i", [P, NB_W], I32)
        tiles_r = sb("tiles_r", [P, NB_W], F32)
        ends_r = sb("ends_r", [P, NB_W], F32)
        base_r = sb("base_r", [P, NB_W], F32)
        zero_r = sb("zero_r", [P, NB_W], F32)
        ends = sb("ends", [P, 1], F32)
        step_i = sb("step_i", [P, ntb], I32)
        step_f = sb("step_f", [P, ntb], F32)
        after = sb("after", [P, ntb], F32)
        win_all = sb("win_all", [P, ntb], F32)
        last_f = sb("last_f", [1, NW], F32)
        back = sb("back", [P, 2, P, 2], I32)
        back_f = sb("back_f", [P, 2, 2, P], F32)
        pl = Placement(nc, c, ps, "q_", ctx, cols, listed, win_b, rec)
        hist, small, counts = ps[:, 0, :], ps[:, 1, :], ps[:, 6, 0:B * NB_W]
        turned = ps[:, 4:6, 0:2 * P].rearrange("p s (f q) -> p s f q", q=P)

        s_pad, s_ld, s_gld, s_empty, s_fill, s_step, s_dve, s_cnt, s_csum, s_ends, s_endc = (
            sem(x) for x in ("pad", "ld", "gld", "empty", "fill", "step", "dve", "cnt", "csum", "ends", "endc"))
        s_chot, s_ghot, s_ghist, s_base, s_row, s_rowd, s_win, s_gsum = (
            sem(x) for x in ("chot", "ghot", "ghist", "base", "row", "rowd", "win", "gsum"))
        s_back = [sem("back0"), sem("back1")]
        s_bf, s_tr, s_out, s_listed, s_fall, s_falls = (sem(x) for x in ("bf", "tr", "out", "listed", "fall", "falls"))
        blocks = ntb // P

        with nc.Block() as block:
            @block.sync
            def _(sp):
                sp.wait_ge(s_pad, 1)
                load_edges(sp, dst_i, dst, edges, s_ld)
                load_edges(sp, src_i, src, edges, s_ld)
                load_edges(sp, g_dst, gnn_dst, E_GNN, s_gld)
                with nc.allow_non_contiguous_dma(reason="one edge of each partition"):
                    sp.dma_start(g_next[0:P - 1, :], gnn_dst[gcols0:gcols0 * P].rearrange("(p n) -> p n", n=gcols0)[:, 0:1]
                                 if gcols0 * P <= E_GNN else
                                 bass.AP(tensor=gnn_dst.tensor, offset=gcols0, ap=[[gcols0, P - 1], [1, 1]])).then_inc(s_gld, 16)
                sp.wait_ge(s_empty, 2)
                sp.dma_start(listed.rearrange("(p n) c -> p (n c)", p=P),
                             empty[:, :, :].rearrange("p n c -> p (n c)")).then_inc(s_fill, 16)
                sp.wait_ge(s_listed, 1)
                rows = listed.rearrange("(b s p) c -> b s p c", s=P, p=P)
                for b in range(blocks):
                    if b >= 2:
                        sp.wait_ge(s_bf, b - 1)
                    sp.dma_start(back[:, b % 2, :, :], rows[b]).then_inc(s_back[b % 2], 16)

            @block.gpsimd
            def _(pool):
                nc.gpsimd.iota(step_i[:, :], [[1, ntb]], base=0, channel_multiplier=0).then_inc(s_step, 1)
                pool.wait_ge(s_fill, 16)
                pairs(pool, nb, lambda k, i, s, first, last: pl.gpsimd(pool, k, s))
                pl.settle(pool)
                pool.sem_inc(s_listed)

            @block.vector
            def _(dve):
                me = Steps(dve, s_dve)
                v = nc.vector
                me.link(v.memset(dst_i[:, :], NW * P))
                me.link(v.memset(g_dst[:, :], NW * P))
                me.link(v.memset(g_next[:, :], NW * P))
                dve.sem_inc(s_pad)
                v.memset(empty[:, :, 0], 0).then_inc(s_empty, 1)
                v.memset(empty[:, :, 1], PADLO).then_inc(s_empty, 1)
                v.memset(zero_r[:, :], 0.0)
                v.memset(src_i[:, columns_of(edges):cols], 0)
                dve.wait_ge(s_ld, 32)
                me.link(v.tensor_scalar(part_i[:, :], dst_i[:, :], 7, None, ALU.arith_shift_right))
                me.link(v.tensor_copy(win_b[:, :], part_i[:, :]))

                def count(k, i, s, first, last):
                    if not first:
                        dve.wait_ge(s_cnt, k - 1)
                    pl.hot_windows(k, s).then_inc(s_chot, 1)
                pairs(dve, nb, count)
                me.did(v.tensor_scalar(rec[:, :, 1], dst_i[:, :], P - 1, None, ALU.bitwise_and))
                me.link(v.tensor_copy(rec[:, :, 0], src_i[:, :]))
                dve.wait_ge(s_csum, 1)
                me.link(v.tensor_reduce(count_r[:, :], counts.rearrange("p (j w) -> p w j", w=NB_W), AX.X, ALU.add))
                me.link(v.tensor_copy(count_i[:, :], count_r[:, :]))
                me.link(v.tensor_scalar(count_i[:, :], count_i[:, :], P - 1, None, ALU.add))
                me.link(v.tensor_scalar(count_i[:, :], count_i[:, :], 7, None, ALU.arith_shift_right))
                me.link(v.tensor_copy(tiles_r[:, :], count_i[:, :]))
                me.link(v.tensor_tensor_scan(ends_r[:, :], tiles_r[:, :], zero_r[:, :], 0.0, ALU.add, ALU.add))
                me.link(v.tensor_tensor(base_r[:, :], ends_r[:, :], tiles_r[:, :], ALU.subtract))
                me.link(v.tensor_scalar(base_r[:, :], base_r[:, :], float(P), None, ALU.mult))
                me.link(v.memset(base_r[:, NW:NB_W], float(slots)))
                dve.sem_inc(s_base)
                me.link(v.tensor_scalar(last_f[0:1, :], ends_r[0:1, 0:NW], -1.0, 0.0, ALU.add, ALU.max))
                me.did(v.tensor_copy(last_tile[0:1, :], last_f[0:1, :]))
                me.did(v.tensor_scalar(filled[:, :], tiles_r[:, 0:NW], 0.5, None, ALU.is_gt))
                dve.wait_ge(s_gld, 48)
                me.link(v.tensor_scalar(g_part[:, :], g_dst[:, :], 7, None, ALU.arith_shift_right))
                me.link(v.tensor_copy(g_win[:, :], g_part[:, :]))
                me.link(v.tensor_scalar(g_part[:, :], g_dst[:, :], P - 1, None, ALU.bitwise_and))
                me.link(v.tensor_copy(g_lo[:, :], g_part[:, :]))
                me.link(v.tensor_tensor(g_fall[:, 0:gcols0 - 1], g_win[:, 0:gcols0 - 1], g_win[:, 1:gcols0], ALU.is_gt))
                me.did(v.tensor_reduce(falls[:, 0:1], g_fall[:, 0:gcols0 - 1], AX.X, ALU.max))
                me.link(v.tensor_scalar(g_next[:, :], g_next[:, :], 7, None, ALU.arith_shift_right))
                me.link(v.tensor_copy(fall_b[:, 0:1], g_next[:, :]))
                me.link(v.tensor_tensor(falls[:, 1:2], g_win[:, gcols0 - 1:gcols0], fall_b[:, 0:1], ALU.is_gt))
                me.link(v.tensor_copy(fall_b[:, :], falls[:, :]))
                dve.sem_inc(s_fall)

                def both(k, i, s, first, last):
                    if not first:
                        dve.wait_ge(s_ghist, k - 1)
                    v.tensor_tensor(g_hot_w[:, s, :, :], c["iota_b"][:, None, 0:NW].to_broadcast([P, CB, NW]),
                                    g_win[:, bass.ds(k * CB, CB), None].to_broadcast([P, CB, NW]), ALU.is_equal)
                    v.tensor_tensor(g_hot_lo[:, s, :, :], c["iota_b"][:, None, :].to_broadcast([P, CB, P]),
                                    g_lo[:, bass.ds(k * CB, CB), None].to_broadcast([P, CB, P]),
                                    ALU.is_equal).then_inc(s_ghot, 1)
                    pl.vector(dve, k, i, s, first)
                pairs(dve, nb, both)
                dve.wait_ge(s_gsum, 1)
                v.tensor_copy(deg[:, :], hist[:, 0:NW])
                dve.wait_ge(s_falls, 1)
                v.tensor_scalar(windows_fall[0:1, 0:1], small[0:1, 4:5], small[0:1, 5:6], None, ALU.add)
                dve.wait_ge(s_endc, 1)
                me.link(v.tensor_copy(ends[0:NW, :], small[0:NW, 1:2]))
                dve.wait_ge(s_step, 1)
                me.link(v.tensor_copy(step_f[:, :], step_i[:, :]))
                v.tensor_scalar(after[0:NW, :], step_f[0:NW, :], ends[0:NW, 0:1], None, ALU.is_ge).then_inc(s_row, 1)
                window_row(nc, c, dve, None, ps, ntb, after, s_row, s_rowd, s_win, win_row, win_all, me)
                me.link(v.memset(same[:, 0:1], 0.0))
                me.link(v.tensor_tensor(same[:, 1:ntb], win_all[:, 1:ntb], win_all[:, 0:ntb - 1], ALU.is_equal))
                for b in range(blocks):
                    dve.wait_ge(s_back[b % 2], 16 * (b // 2 + 1))
                    if b >= 2:
                        dve.wait_ge(s_tr, b - 1)
                    v.tensor_copy(back_f[:, b % 2, :, :], back[:, b % 2, :, :].rearrange("s p c -> s c p")).then_inc(s_bf, 1)
                    dve.wait_ge(s_tr, b + 1)
                    v.tensor_copy(idx[:, b * P:(b + 1) * P], turned[:, b % 2, 0, :])
                    v.tensor_copy(lo_f[:, b * P:(b + 1) * P], turned[:, b % 2, 1, :]).then_inc(s_out, 1)

            @block.tensor
            def _(pe):
                nc.tensor.matmul(counts, c["zeros_b"][:, :], c["ones_b"][:, None, 0:NB_W].to_broadcast([P, B, NB_W]),
                                 start=True, stop=False)

                def count(k, i, s, first, last):
                    pe.wait_ge(s_chot, k + 1)
                    nc.tensor.matmul(counts, c["ones_b"][:, :], pl.hot[:, s, :, :], start=False, stop=last).then_inc(s_cnt, 1)
                pairs(pe, nb, count)
                pe.wait_ge(s_cnt, nb)
                pe.sem_inc(s_csum)
                pe.wait_ge(s_base, 1)
                nc.tensor.matmul(small[0:NW, 1:2], ends_r[0:1, 0:NW], c["ones"][0:1, 0:1], start=True, stop=True).then_inc(s_endc, 1)
                pl.start(base_r)
                pe.wait_ge(s_fall, 1)
                nc.tensor.matmul(small[:, 4:6], c["ones_b"][:, :], fall_b[:, :], start=True, stop=True).then_inc(s_falls, 1)
                nc.tensor.matmul(hist[:, 0:NW], c["zeros_b"][:, :], c["zeros_b"][:, 0:NW], start=True, stop=False)

                def both(k, i, s, first, last):
                    pe.wait_ge(s_ghot, k + 1)
                    for j in range(CB):
                        m = nc.tensor.matmul(hist[:, 0:NW], g_hot_lo[:, s, j, :], g_hot_w[:, s, j, :], start=False,
                                             stop=last and j == CB - 1)
                    m.then_inc(s_ghist, 1)
                    pl.tensor(pe, k, s)
                pairs(pe, nb, both)
                pe.wait_ge(s_ghist, nb)
                pe.sem_inc(s_gsum)
                window_row(nc, c, None, pe, ps, ntb, after, s_row, s_rowd, s_win, win_row, win_all, None)
                for b in range(blocks):
                    pe.wait_ge(s_bf, b + 1)
                    if b >= 2:
                        pe.wait_ge(s_out, b - 1)
                    for f in range(2):
                        m = nc.tensor.transpose(turned[:, b % 2, f, :], back_f[:, b % 2, f, :], c["ident"][:, :])
                    m.then_inc(s_tr, 1)


def group_edges(nc, c, ps, deg, src, dst, pairs_list, src_rows, dst_rows):
    edges = E_GNN
    cols0 = columns_of(edges)
    cols = (cols0 + B - 1) // B * B
    with ExitStack() as ctx:
        def sb(name, shape, dt):
            return ctx.enter_context(nc.sbuf_tensor("r_" + name, shape, dt))

        def sem(name):
            return c["sems"].enter_context(nc.alloc_semaphore("r_" + name))
        dst_i = sb("dst_i", [P, cols], I32)
        src_i = sb("src_i", [P, cols], I32)
        part_i = sb("part_i", [P, cols], I32)
        win_b = sb("win_b", [P, cols], BF16)
        rec = sb("rec", [P, cols, 2], I32)
        base_r = sb("base_r", [P, NB_W], F32)
        count_r = sb("count_r", [P, NW], F32)
        ends_r = sb("ends_r", [P, NW], F32)
        zero_r = sb("zero_r", [P, NW], F32)
        tail = sb("tail", [1, P, 2], I32)
        back = sb("back", [P, cols0, 2], I32)
        split = sb("split", [P, 2, cols0], I32)
        pl = Placement(nc, c, ps, "r_", ctx, cols, pairs_list, win_b, rec)
        s_pad, s_ld, s_tail, s_dve, s_cnt, s_base, s_listed, s_back, s_split, s_rows = (
            sem(x) for x in ("pad", "ld", "tail", "dve", "cnt", "base", "listed", "back", "split", "rows"))
        with nc.Block() as block:
            @block.sync
            def _(sp):
                sp.wait_ge(s_pad, 1)
                load_edges(sp, dst_i, dst, edges, s_ld)
                sp.dma_start(pairs_list[edges:cols0 * P, :].rearrange("(a n) c -> a (n c)", a=1),
                             tail[:, 0:cols0 * P - edges, :].rearrange("a n c -> a (n c)")).then_inc(s_tail, 16)
                sp.wait_ge(s_listed, 1)
                sp.dma_start(back[:, :, :], pairs_list.rearrange("(p n) c -> p n c", p=P)).then_inc(s_back, 16)
                sp.wait_ge(s_split, 1)
                sp.dma_start(src_rows.rearrange("r n -> (r n)").rearrange("(p n) -> p n", p=P), split[:, 0, :]).then_inc(s_rows, 16)
                sp.dma_start(dst_rows.rearrange("r n -> (r n)").rearrange("(p n) -> p n", p=P), split[:, 1, :]).then_inc(s_rows, 16)
                sp.wait_ge(s_rows, 32)

            @block.scalar
            def _(act):
                act.wait_ge(s_pad, 1)
                load_edges(act, src_i, src, edges, s_ld)

            @block.gpsimd
            def _(pool):
                pool.wait_ge(s_tail, 16)
                pairs(pool, cols // B, lambda k, i, s, first, last: pl.gpsimd(pool, k, s))
                pl.settle(pool)
                pool.sem_inc(s_listed)

            @block.vector
            def _(dve):
                me = Steps(dve, s_dve)
                v = nc.vector
                me.did(v.memset(tail[:, :, 0], 0))
                me.did(v.memset(tail[:, :, 1], 2 * NW * P))
                me.did(v.memset(src_i[:, :], 0))
                me.did(v.memset(zero_r[:, :], 0.0))
                me.link(v.memset(dst_i[:, :], NW * P))
                dve.sem_inc(s_pad)
                dve.wait_ge(s_ld, 64)
                me.link(v.tensor_scalar(part_i[:, :], dst_i[:, :], 7, None, ALU.arith_shift_right))
                me.link(v.tensor_copy(win_b[:, :], part_i[:, :]))
                me.link(v.tensor_copy(rec[:, :, 0], src_i[:, :]))
                me.link(v.tensor_copy(rec[:, :, 1], dst_i[:, :]))
                dve.wait_ge(s_cnt, 1)
                me.link(v.tensor_copy(count_r[:, :], ps[:, 0, 0:NW]))
                me.link(v.tensor_tensor_scan(ends_r[:, :], count_r[:, :], zero_r[:, :], 0.0, ALU.add, ALU.add))
                me.link(v.tensor_tensor(base_r[:, 0:NW], ends_r[:, :], count_r[:, :], ALU.subtract))
                me.link(v.memset(base_r[:, NW:NB_W], float(cols0 * P)))
                dve.sem_inc(s_base)
                pairs(dve, cols // B, lambda k, i, s, first, last: pl.vector(dve, k, i, s, first))
                dve.wait_ge(s_back, 16)
                v.tensor_copy(split[:, :, :], back[:, :, :].rearrange("p n c -> p c n")).then_inc(s_split, 1)

            @block.tensor
            def _(pe):
                nc.tensor.matmul(ps[:, 0, 0:NW], c["ones"][:, :], deg[:, :], start=True, stop=True).then_inc(s_cnt, 1)
                pe.wait_ge(s_base, 1)
                pl.start(base_r)
                pairs(pe, cols // B, lambda k, i, s, first, last: pl.tensor(pe, k, s))


def copy_rows(nc, c, src, dst, src_rows, dst_rows):
    edges = E_GNN
    flat = columns_of(edges) * P
    with nc.sbuf_tensor("w_tail", [1, 2, P], I32) as tail:
        s_tail = c["sems"].enter_context(nc.alloc_semaphore("w_tail"))
        s_rows = c["sems"].enter_context(nc.alloc_semaphore("w_rows"))
        with nc.Block() as block:
            @block.vector
            def _(dve):
                nc.vector.memset(tail[:, 0, :], 0).then_inc(s_tail, 1)
                nc.vector.memset(tail[:, 1, :], 2 * NW * P).then_inc(s_tail, 1)

            @block.sync
            def _(sp):
                sp.wait_ge(s_tail, 2)
                for n, (a, rows) in enumerate(((src, src_rows), (dst, dst_rows))):
                    to = rows.rearrange("r n -> (r n)")
                    sp.dma_start(to[0:edges].rearrange("(a n) -> a n", a=16),
                                 a[0:edges].rearrange("(a n) -> a n", a=16)).then_inc(s_rows, 16)
                    sp.dma_start(to[edges:flat].rearrange("(a n) -> a n", a=1), tail[:, n, 0:flat - edges]).then_inc(s_rows, 16)
                sp.wait_ge(s_rows, 64)


def take_tiles(nc, c, ps, deg, src_rows, dst_rows, idx, lo_f, win_row):
    ntb = blocks_bound(E_GNN)
    blocks = ntb // P
    with ExitStack() as ctx:
        def sb(name, shape, dt=F32):
            return ctx.enter_context(nc.sbuf_tensor("t_" + name, shape, dt))

        def sem(name):
            return c["sems"].enter_context(nc.alloc_semaphore("t_" + name))
        count_r = sb("count_r", [P, NW])
        some = sb("some", [P, NW])
        ends_e = sb("ends_e", [P, NW])
        whole = sb("whole", [P, NW], I32)
        first_r = sb("first_r", [P, NW])
        last_r = sb("last_r", [P, NW])
        rows_r = sb("rows_r", [P, NW])
        ends_r = sb("ends_r", [P, NW])
        shift = sb("shift", [P, NW])
        zero_r = sb("zero_r", [P, NW])
        ends = sb("ends", [P, 1])
        own_i = sb("own_i", [P, blocks], I32)
        own = sb("own", [P, blocks])
        wide = sb("wide", [P, blocks, NW])
        wide2 = sb("wide2", [P, blocks, NW])
        win_c = sb("win_c", [P, blocks])
        node_c = sb("node_c", [P, blocks])
        row_c = sb("row_c", [P, blocks])
        row_i = sb("row_i", [P, blocks], U32)
        step_i = sb("step_i", [P, ntb], I32)
        step_f = sb("step_f", [P, ntb])
        after = sb("after", [P, ntb])
        got = sb("got", [P, 2, blocks, P], I32)
        back_f = sb("back_f", [P, 2, 2, P])
        turned = ps[:, 4:6, 0:2 * P].rearrange("p s (f q) -> p s f q", q=P)
        small = ps[:, 1, :]
        s_dve, s_iota, s_cnt, s_ends, s_endc, s_row, s_rowd, s_win, s_rowi, s_got, s_bf, s_tr, s_out = (
            sem(x) for x in ("dve", "iota", "cnt", "ends", "endc", "row", "rowd", "win", "rowi", "got", "bf", "tr", "out"))
        with nc.Block() as block:
            @block.gpsimd
            def _(pool):
                nc.gpsimd.iota(step_i[:, :], [[1, ntb]], base=0, channel_multiplier=0).then_inc(s_iota, 1)
                nc.gpsimd.iota(own_i[:, :], [[P, blocks]], base=0, channel_multiplier=1).then_inc(s_iota, 1)
                pool.wait_ge(s_rowi, 1)
                for b in range(blocks):
                    for n, rows in enumerate((src_rows, dst_rows)):
                        nc.gpsimd.indirect_dma_start(
                            out=got[:, n, b, :], out_offset=None, in_=rows,
                            in_offset=bass.IndirectOffsetOnAxis(ap=row_i[:, b:b + 1], axis=0),
                            bounds_check=columns_of(E_GNN) - 1, oob_is_err=False).then_inc(s_got, 16)

            @block.vector
            def _(dve):
                me = Steps(dve, s_dve)
                v = nc.vector

                def by_step(x):
                    return x[:, None, :].to_broadcast([P, blocks, NW])

                def by_window(x):
                    return x[:, :, None].to_broadcast([P, blocks, NW])
                me.did(v.memset(zero_r[:, :], 0.0))
                dve.wait_ge(s_cnt, 1)
                me.link(v.tensor_copy(count_r[:, :], ps[:, 0, 0:NW]))
                me.did(v.tensor_scalar(some[:, :], count_r[:, :], 0.5, None, ALU.is_gt))
                me.link(v.tensor_tensor_scan(ends_e[:, :], count_r[:, :], zero_r[:, :], 0.0, ALU.add, ALU.add))
                me.link(v.tensor_tensor(first_r[:, :], ends_e[:, :], count_r[:, :], ALU.subtract))
                for x, y in ((first_r, 0.0), (last_r, -1.0)):
                    me.link(v.tensor_scalar(whole[:, :], (first_r if x is first_r else ends_e)[:, :], y, 0.0, ALU.add, ALU.max))
                    me.link(v.tensor_scalar(whole[:, :], whole[:, :], 7, None, ALU.arith_shift_right))
                    me.link(v.tensor_copy(x[:, :], whole[:, :]))
                me.link(v.scalar_tensor_tensor(rows_r[:, :], last_r[:, :], 1.0, first_r[:, :], ALU.add, ALU.subtract))
                me.link(v.tensor_tensor(rows_r[:, :], rows_r[:, :], some[:, :], ALU.mult))
                me.link(v.tensor_tensor_scan(ends_r[:, :], rows_r[:, :], zero_r[:, :], 0.0, ALU.add, ALU.add))
                me.link(v.tensor_tensor(shift[:, :], first_r[:, :], ends_r[:, :], ALU.subtract))
                me.link(v.tensor_tensor(shift[:, :], shift[:, :], rows_r[:, :], ALU.add))
                dve.sem_inc(s_ends)
                dve.wait_ge(s_iota, 2)
                me.link(v.tensor_copy(own[:, :], own_i[:, :]))
                me.link(v.tensor_tensor(wide[:, :, :], by_window(own), by_step(ends_r), ALU.is_ge))
                me.link(v.tensor_reduce(win_c[:, :], wide[:, :, :], AX.X, ALU.add))
                me.link(v.tensor_tensor(wide[:, :, :], by_window(win_c), by_step(c["iota_f"][:, 0:NW]), ALU.is_equal))
                me.link(v.tensor_tensor(wide2[:, :, :], wide[:, :, :], by_step(shift), ALU.mult))
                me.link(v.tensor_reduce(row_c[:, :], wide2[:, :, :], AX.X, ALU.add))
                me.link(v.tensor_tensor(row_c[:, :], row_c[:, :], own[:, :], ALU.add))
                me.link(v.tensor_scalar(row_c[:, :], row_c[:, :], float(columns_of(E_GNN) - 1), None, ALU.min))
                me.link(v.tensor_copy(row_i[:, :], row_c[:, :]))
                dve.sem_inc(s_rowi)
                me.link(v.tensor_scalar(node_c[:, :], win_c[:, :], float(P), None, ALU.mult))
                me.link(v.tensor_copy(step_f[:, :], step_i[:, :]))
                dve.wait_ge(s_endc, 1)
                me.link(v.tensor_copy(ends[0:NW, :], small[0:NW, 1:2]))
                v.tensor_scalar(after[0:NW, :], step_f[0:NW, :], ends[0:NW, 0:1], None, ALU.is_ge).then_inc(s_row, 1)
                window_row(nc, c, dve, None, ps, ntb, after, s_row, s_rowd, s_win, win_row, None, me)
                dve.wait_ge(s_got, 32 * blocks)
                for b in range(blocks):
                    if b >= 2:
                        dve.wait_ge(s_tr, b - 1)
                    v.tensor_copy(back_f[:, b % 2, 0, :], got[:, 0, b, :])
                    v.tensor_scalar(back_f[:, b % 2, 1, :], got[:, 1, b, :], node_c[:, b:b + 1], None,
                                    ALU.subtract).then_inc(s_bf, 1)
                    dve.wait_ge(s_tr, b + 1)
                    v.tensor_copy(idx[:, b * P:(b + 1) * P], turned[:, b % 2, 0, :])
                    v.tensor_copy(lo_f[:, b * P:(b + 1) * P], turned[:, b % 2, 1, :]).then_inc(s_out, 1)

            @block.tensor
            def _(pe):
                nc.tensor.matmul(ps[:, 0, 0:NW], c["ones"][:, :], deg[:, :], start=True, stop=True).then_inc(s_cnt, 1)
                pe.wait_ge(s_ends, 1)
                nc.tensor.matmul(small[0:NW, 1:2], ends_r[0:1, :], c["ones"][0:1, 0:1], start=True, stop=True).then_inc(s_endc, 1)
                window_row(nc, c, None, pe, ps, ntb, after, s_row, s_rowd, s_win, win_row, None, None)
                for b in range(blocks):
                    pe.wait_ge(s_bf, b + 1)
                    if b >= 2:
                        pe.wait_ge(s_out, b - 1)
                    for f in range(2):
                        m = nc.tensor.transpose(turned[:, b % 2, f, :], back_f[:, b % 2, f, :], c["ident"][:, :])
                    m.then_inc(s_tr, 1)


GW = 14
GROUPS = NW // GW


def group(t, g):
    return t[:, g * GW:(g + 1) * GW]


def row_means(nc, me, Z, stat, g):
    me.link(nc.vector.tensor_reduce(group(stat, g), group(Z, g), AX.X, ALU.add))
    me.link(nc.vector.tensor_scalar(group(stat, g), group(stat, g), 1.0 / D, None, ALU.mult))


def less_means(nc, Z, stat, s_sub, g):
    nc.vector.tensor_tensor(group(Z, g), group(Z, g), group(stat, g)[:, :, None].to_broadcast([P, GW, D]),
                            ALU.subtract).then_inc(s_sub, 1)


def row_scales(nc, dve, me, rstd, s_sq, ask):
    dve.wait_ge(s_sq, 1)
    me.link(nc.vector.tensor_scalar(rstd[:, :], rstd[:, :], 1.0 / D, EPS, ALU.mult, ALU.add))
    inverse_root(nc, dve, me, rstd[:, :], *ask)


def scale_rows(nc, Z, rstd, s_z, g):
    nc.vector.tensor_tensor(group(Z, g), group(Z, g), group(rstd, g)[:, :, None].to_broadcast([P, GW, D]),
                            ALU.mult).then_inc(s_z, 1)


def window_pairs(act, s_ready, body):
    for w in range(2):
        act.wait_ge(s_ready, 1)
        body(w, 0, w, True, False)
    for g in range(GROUPS):
        act.wait_ge(s_ready, g + 1)
        with act.Fori(max(1, g * GW // 2), (g + 1) * GW // 2) as i:
            body(i * 2, i, 0, False, False)
            body(i * 2 + 1, i, 1, False, False)


def square_rows(nc, act, Z, junk, rstd, s_sub, s_each, s_sq):
    def rows(k, i, s, first, last):
        if not first:
            act.wait_ge(s_each, k - 1)
        nc.scalar.activation(junk[:, s, :], Z[:, bass.ds(k, 1), :].rearrange("p a d -> p (a d)"), ACT.Square,
                             accum_out=rstd[:, bass.ds(k, 1)]).then_inc(s_each, 1)
    window_pairs(act, s_sub, rows)
    act.wait_ge(s_each, NW)
    act.sem_inc(s_sq)


def node_rows(dram, w0, n):
    return dram[w0 * P:(w0 + n) * P, :].rearrange("(w p) d -> p w d", p=P)


def first_norm(nc, c, x, Z, deg, dinv, table):
    with ExitStack() as ctx:
        def sem(name):
            return c["sems"].enter_context(nc.alloc_semaphore("n1_" + name))
        stat = ctx.enter_context(nc.sbuf_tensor("n1_stat", [P, NW], F32))
        rstd = ctx.enter_context(nc.sbuf_tensor("n1_rstd", [P, NW], F32))
        root = ctx.enter_context(nc.sbuf_tensor("n1_root", [P, NW], F32))
        inv = ctx.enter_context(nc.sbuf_tensor("n1_inv", [P, NW], F32))
        junk = ctx.enter_context(nc.sbuf_tensor("n1_junk", [P, 2, D], F32))
        s_ask, s_root = sem("ask"), sem("root")
        s_pad, s_dve, s_sub, s_each, s_sq, s_z, s_t = (
            sem(n) for n in ("pad", "dve", "sub", "each", "sq", "z", "t"))
        s_x = [sem(f"x{g}") for g in range(GROUPS)]
        with nc.Block() as block:
            @block.sync
            def _(sp):
                for g in range(GROUPS):
                    n = GW if g < GROUPS - 1 else GW - 1
                    sp.dma_start(Z[:, g * GW:g * GW + n, :], node_rows(x, g * GW, n)).then_inc(s_x[g], 16)
                sp.wait_ge(s_pad, 1)
                sp.dma_start(Z[0:LASTROWS, NW - 1, :], x[(NW - 1) * P:N, :]).then_inc(s_x[GROUPS - 1], 16)
                for g in range(GROUPS):
                    sp.wait_ge(s_z, g + 1)
                    sp.dma_start(node_rows(table, g * GW, GW), group(Z, g)).then_inc(s_t, 16)
                sp.wait_ge(s_t, 16 * GROUPS)

            @block.vector
            def _(dve):
                me = Steps(dve, s_dve)
                nc.vector.memset(Z[:, NW - 1, :], 0.0).then_inc(s_pad, 1)
                me.link(nc.vector.tensor_scalar(dinv[:, :], deg[:, :], 1.0, None, ALU.add))
                inverse_root(nc, dve, me, dinv[:, :], root[:, :], inv[:, :], s_ask, s_root, 1)
                for g in range(GROUPS):
                    dve.wait_ge(s_x[g], 32 if g == GROUPS - 1 else 16)
                    row_means(nc, me, Z, stat, g)
                    less_means(nc, Z, stat, s_sub, g)
                row_scales(nc, dve, me, rstd, s_sq, (root[:, :], inv[:, :], s_ask, s_root, 2))
                me.link(nc.vector.tensor_tensor(rstd[:, :], rstd[:, :], dinv[:, :], ALU.mult))
                for g in range(GROUPS):
                    scale_rows(nc, Z, rstd, s_z, g)

            @block.scalar
            def _(act):
                take_root(nc, act, dinv[:, :], root[:, :], s_ask, s_root, 1)
                square_rows(nc, act, Z, junk, rstd, s_sub, s_each, s_sq)
                take_root(nc, act, rstd[:, :], root[:, :], s_ask, s_root, 2)


def convolve(nc, c, ps, tag, table, Z, idx, lo_f, win_row):
    batches = tiles_bound(E_GNN) // GT
    with ExitStack() as ctx:
        def sem(name):
            return c["sems"].enter_context(nc.alloc_semaphore(tag + name))
        ring = ctx.enter_context(nc.sbuf_tensor(tag + "ring", [P, 2, GT], U32))
        got = ctx.enter_context(nc.sbuf_tensor(tag + "got", [P, 2, GT, D], F32))
        hot = ctx.enter_context(nc.sbuf_tensor(tag + "hot", [P, 2, GT, P], F32))
        part = ps[:, 0:8, :].rearrange("p (s b) (j d) -> p s (b j) d", s=2, d=D)
        s_idx, s_hot, s_mm, s_add, s_tick = (sem(n) for n in ("idx", "hot", "mm", "add", "tick"))
        s_got = [sem("got0"), sem("got1")]
        with nc.Block() as block:
            @block.scalar
            def _(act):
                def indices(k, i, s, first, last):
                    if not first:
                        act.wait_ge(s_got[s], i * (16 * GT))
                    nc.scalar.copy(ring[:, s, :], idx[:, bass.ds(k * GT, GT)]).then_inc(s_idx, 1)
                pairs(act, batches, indices)

            @block.gpsimd
            def _(pool):
                def gather(k, i, s, first, last):
                    pool.wait_ge(s_idx, k + 1)
                    pool.sem_inc(s_tick)
                    if not first:
                        pool.wait_ge(s_mm, k - 1)
                        pool.sem_inc(s_tick)
                    for j in range(GT):
                        nc.gpsimd.indirect_dma_start(
                            out=got[:, s, j, :], out_offset=None, in_=table,
                            in_offset=bass.IndirectOffsetOnAxis(ap=ring[:, s, j:j + 1], axis=0),
                            bounds_check=NP - 1, oob_is_err=False).then_inc(s_got[s], 16)
                pairs(pool, batches, gather)

            @block.vector
            def _(dve):
                def one_hot(k, s, first):
                    if not first:
                        dve.wait_ge(s_mm, k - 1)
                    nc.vector.tensor_tensor(hot[:, s, :, :], c["iota_f"][:, None, :].to_broadcast([P, GT, P]),
                                            lo_f[:, bass.ds(k * GT, GT), None].to_broadcast([P, GT, P]),
                                            ALU.is_equal).then_inc(s_hot, 1)

                def add(k, i, s, first, last):
                    if not last:
                        one_hot(k + 1, 1 - s, first and s == 0)
                    wins = window_values(nc, win_row, k * GT, GT, mybir.EngineType.DVE)
                    dve.wait_ge(s_mm, k + 1)
                    for j in range(GT):
                        if not (first and s == 0 and j == 0):
                            dve.wait_ge(s_add, k * GT + j)
                        z = Z[:, bass.ds(wins[j], 1), :]
                        nc.vector.tensor_tensor(z, z, part[:, s, j:j + 1, :], ALU.add).then_inc(s_add, 1)
                one_hot(0, 0, True)
                pairs(dve, batches, add)

            @block.tensor
            def _(pe):
                def product(k, i, s, first, last):
                    pe.wait_ge(s_hot, k + 1)
                    pe.wait_ge(s_got[s], i * (16 * GT) + 16 * GT)
                    if not first:
                        pe.wait_ge(s_add, k * GT - GT)
                    for j in range(GT):
                        m = nc.tensor.matmul(part[:, s, j, :], hot[:, s, j, :], got[:, s, j, :],
                                             start=True, stop=True)
                    m.then_inc(s_mm, 1)
                pairs(pe, batches, product)


def between(nc, c, ps, W1, b1, W2, Z, dinv, table):
    T = 2
    steps = NW // T
    with ExitStack() as ctx:
        def sb(name, shape):
            return ctx.enter_context(nc.sbuf_tensor("m_" + name, shape, F32))


        def sem(name):
            return c["sems"].enter_context(nc.alloc_semaphore("m_" + name))
        w1 = sb("w1", [P, KC, F])
        w1t = sb("w1t", [P, FC, D])
        w2 = sb("w2", [P, FC, D])
        w12 = sb("w12", [P, KC, D])
        b1c = sb("b1c", [P, FC])
        b12 = sb("b12", [1, D])
        bias = sb("bias", [P, D])
        zs = sb("zs", [P, 2, T, D])
        zt = sb("zt", [P, 2, KC, T, P])
        tp = ps[:, 0:2, :].rearrange("p s (k t q) -> p s k t q", k=KC, q=P)
        hp = ps[:, 2:4, :].rearrange("p s (t d) -> p s t d", d=D)
        wp, bp = ps[:, 4, :], ps[:, 5, :]
        s_w, s_b, s_wt, s_wc, s_wp, s_w12, s_zs, s_tp, s_zt, s_hp, s_add, s_h = (
            sem(n) for n in ("w", "b", "wt", "wc", "wp", "w12", "zs", "tp", "zt", "hp", "add", "h"))
        s_st = [sem("st0"), sem("st1")]
        with nc.Block() as block:
            @block.sync
            def _(sp):
                sp.dma_start(w1[:, :, :], W1.rearrange("(k p) f -> p k f", p=P)).then_inc(s_w, 16)
                sp.dma_start(w2[:, :, :], W2.rearrange("(k p) f -> p k f", p=P)).then_inc(s_w, 16)
                with nc.allow_non_contiguous_dma(reason="one bias vector onto partitions"):
                    sp.dma_start(b1c[:, :], b1.rearrange("(k p) -> p k", p=P)).then_inc(s_b, 16)

                def store(k, i, s, first, last):
                    sp.wait_ge(s_h, k + 1)
                    sp.dma_start(table[bass.ds(k * (T * P), T * P), :].rearrange("(t p) d -> p t d", p=P),
                                 Z[:, bass.ds(k * T, T), :]).then_inc(s_st[s], 16)
                pairs(sp, steps, store)
                for s in range(2):
                    sp.wait_ge(s_st[s], 16 * ((steps + 1 - s) // 2))

            @block.tensor
            def _(pe):
                pe.wait_ge(s_w, 32)
                pe.wait_ge(s_b, 16)
                for f in range(FC):
                    for k in range(KC):
                        n = f * KC + k
                        if n >= 1:
                            pe.wait_ge(s_wc, n)
                        nc.tensor.transpose(wp[:, 0:P], w1[:, k, f * P:(f + 1) * P], c["ident"][:, :]).then_inc(s_wt, 1)
                pe.wait_ge(s_wc, FC * KC)
                for k in range(KC):
                    if k:
                        pe.wait_ge(s_w12, k)
                    for f in range(FC):
                        m = nc.tensor.matmul(wp[:, 0:D], w1t[:, f, k * P:(k + 1) * P], w2[:, f, :],
                                             start=(f == 0), stop=(f == FC - 1))
                    m.then_inc(s_wp, 1)
                for f in range(FC):
                    m = nc.tensor.matmul(bp[0:1, 0:D], b1c[:, f:f + 1], w2[:, f, :], start=(f == 0), stop=(f == FC - 1))
                m.then_inc(s_wp, 1)
                pe.wait_ge(s_w12, KC + 1)
                nc.tensor.matmul(bp[:, 0:D], c["ones"][0:1, :], b12[0:1, :], start=True, stop=True).then_inc(s_wp, 1)

                def turn(k, s, first):
                    pe.wait_ge(s_zs, k + 1)
                    if not first:
                        pe.wait_ge(s_zt, k - 1)
                    for t in range(T):
                        for q in range(KC):
                            m = nc.tensor.transpose(tp[:, s, q, t, :], zs[:, s, t, q * P:(q + 1) * P], c["ident"][:, :])
                    m.then_inc(s_tp, 1)

                def product(k, i, s, first, last):
                    if not last:
                        turn(k + 1, 1 - s, first and s == 0)
                    pe.wait_ge(s_zt, k + 1)
                    if not first:
                        pe.wait_ge(s_add, k - 1)
                    for t in range(T):
                        for q in range(KC):
                            m = nc.tensor.matmul(hp[:, s, t, :], zt[:, s, q, t, :], w12[:, q, :],
                                                 start=(q == 0), stop=(q == KC - 1))
                    m.then_inc(s_hp, 1)
                turn(0, 0, True)
                pairs(pe, steps, product)

            @block.scalar
            def _(act):
                def copy(k, i, s, first, last):
                    act.wait_ge(s_tp, k + 1)
                    if not first:
                        act.wait_ge(s_hp, k - 1)
                    nc.scalar.copy(zt[:, s, :, :, :], tp[:, s, :, :, :]).then_inc(s_zt, 1)
                pairs(act, steps, copy)

            @block.vector
            def _(dve):
                for n in range(FC * KC):
                    f, k = n // KC, n % KC
                    dve.wait_ge(s_wt, n + 1)
                    nc.vector.tensor_copy(w1t[:, f, k * P:(k + 1) * P], wp[:, 0:P]).then_inc(s_wc, 1)
                for k in range(KC):
                    dve.wait_ge(s_wp, k + 1)
                    nc.vector.tensor_copy(w12[:, k, :], wp[:, 0:D]).then_inc(s_w12, 1)
                dve.wait_ge(s_wp, KC + 1)
                nc.vector.tensor_copy(b12[0:1, :], bp[0:1, 0:D]).then_inc(s_w12, 1)

                dve.wait_ge(s_wp, KC + 2)
                nc.vector.tensor_copy(bias[:, :], bp[:, 0:D]).then_inc(s_w12, 1)

                def scale(k, s, first):
                    if not first:
                        dve.wait_ge(s_tp, k - 1)
                    nc.vector.tensor_tensor(zs[:, s, :, :], Z[:, bass.ds(k * T, T), :],
                                            dinv[:, bass.ds(k * T, T), None].to_broadcast([P, T, D]), ALU.mult).then_inc(s_zs, 1)

                def finish(k, i, s, first, last):
                    if type(k) is not int or k + 2 < steps:
                        scale(k + 2, s, False)
                    z = Z[:, bass.ds(k * T, T), :]
                    dve.wait_ge(s_hp, k + 1)
                    nc.vector.tensor_tensor(z, hp[:, s, :, :], bias[:, None, :].to_broadcast([P, T, D]), ALU.add).then_inc(s_add, 1)
                    dve.wait_ge(s_add, k + 1)
                    nc.vector.tensor_tensor(z, z, dinv[:, bass.ds(k * T, T), None].to_broadcast([P, T, D]),
                                            ALU.mult).then_inc(s_h, 1)
                scale(0, 0, True)
                scale(1, 1, True)
                dve.wait_ge(s_w12, KC + 2)
                pairs_but_last(dve, steps, finish)


def batch_norm(nc, c, ps, x, b2, gamma, beta, wgat, att_src, att_dst, Z, dinv, x2, xn, heads, adst, table):
    T = 2
    groups = GROUPS
    with ExitStack() as ctx:
        def sb(name, shape):
            return ctx.enter_context(nc.sbuf_tensor("b_" + name, shape, F32))


        def sem(name):
            return c["sems"].enter_context(nc.alloc_semaphore("b_" + name))
        rows = sb("rows", [P, 3, D])
        atts = sb("atts", [P, 2, HG])
        mean = sb("mean", [P, D])
        scale = sb("scale", [P, D])
        sq = sb("sq", [P, 2, D])
        xg = sb("xg", [P, 2, GW, D])
        stat = sb("stat", [P, NW])
        rstd = sb("rstd", [P, NW])
        wg = sb("wg", [P, KC, HG])
        stage = sb("stage", [P, 2, T, D])
        root = sb("root", [P, D])
        inv = sb("inv", [P, D])
        s_ask, s_root = sem("ask"), sem("root")
        zt = sb("zt", [P, 2, KC, T, P])
        prod = sb("prod", [P, NW, HG])
        tp = ps[:, 0:2, :].rearrange("p s (k t q) -> p s k t q", k=KC, q=P)
        hp = ps[:, 2:4, 0:T * HG].rearrange("p s (t h) -> p s t h", h=HG)
        total = ps[:, 4:6, :]
        (s_w, s_dve, s_y, s_cs, s_d, s_sq, s_cs2, s_x2, s_xpad, s_sub, s_each, s_all, s_n, s_stn,
         s_tp, s_zt, s_hp, s_h, s_tab, s_stt, s_hsq, s_stage) = (sem(n) for n in (
             "w", "dve", "y", "cs", "d", "sq", "cs2", "x2", "xpad", "sub", "each", "all", "n", "stn",
             "tp", "zt", "hp", "h", "tab", "stt", "hsq", "stage"))
        s_x = [sem("x0"), sem("x1")]
        s_st2 = [sem(f"st2_{g}") for g in range(groups)]
        with nc.Block() as block:
            @block.sync
            def _(sp):
                for n, v in enumerate((b2, gamma, beta)):
                    sp.dma_start(rows[:, n, :], v.rearrange("(a d) -> a d", a=1).to_broadcast([P, D])).then_inc(s_w, 16)
                for n, v in enumerate((att_src, att_dst)):
                    sp.dma_start(atts[:, n, :], v.rearrange("(a h) e -> a (h e)", a=1).to_broadcast([P, HG])).then_inc(s_w, 16)
                sp.dma_start(wg[:, :, :], wgat.rearrange("(k p) f -> p k f", p=P)).then_inc(s_w, 16)

                sp.wait_ge(s_xpad, 1)

                def load(g):
                    n = GW if g < groups - 1 else GW - 1
                    sp.dma_start(xg[:, g % 2, 0:n, :], node_rows(x, g * GW, n)).then_inc(s_x[g % 2], 16)
                    if g == groups - 1:
                        sp.dma_start(xg[0:LASTROWS, g % 2, n, :], x[(NW - 1) * P:N, :]).then_inc(s_x[g % 2], 16)
                load(0)
                load(1)
                for g in range(groups):
                    sp.wait_ge(s_x2, g + 1)
                    sp.dma_start(node_rows(x2, g * GW, GW), group(Z, g)).then_inc(s_st2[g], 16)
                    if g + 2 < groups:
                        load(g + 2)
                for g in range(groups):
                    sp.wait_ge(s_n, g + 1)
                    sp.dma_start(node_rows(xn, g * GW, GW), group(Z, g)).then_inc(s_stn, 16)
                sp.wait_ge(s_tab, 1)
                sp.dma_start(node_rows(table, 0, NW), heads[:, :, :]).then_inc(s_stt, 16)
                for g in range(groups):
                    sp.wait_ge(s_st2[g], 16)
                sp.wait_ge(s_stn, 16 * groups)
                sp.wait_ge(s_stt, 16)

            @block.vector
            def _(dve):
                me = Steps(dve, s_dve)
                nc.vector.memset(xg[:, (groups - 1) % 2, GW - 1, :], 0.0).then_inc(s_xpad, 1)
                dve.wait_ge(s_w, 16 * 6)
                for g in range(groups):
                    z = Z[:, g * GW:(g + 1) * GW, :]
                    me.link(nc.vector.tensor_tensor(z, z, dinv[:, g * GW:(g + 1) * GW, None].to_broadcast([P, GW, D]), ALU.mult))
                    nc.vector.tensor_tensor(z, z, rows[:, 0:1, :].to_broadcast([P, GW, D]), ALU.add).then_inc(s_y, 1)
                dve.wait_ge(s_cs, 1)
                me.link(nc.vector.tensor_scalar(mean[:, :], total[:, 0, 0:D], 1.0 / N, None, ALU.mult))
                dve.wait_ge(s_y, groups)
                for g in range(groups):
                    z = Z[:, g * GW:(g + 1) * GW, :]
                    nc.vector.tensor_tensor(z, z, mean[:, None, :].to_broadcast([P, GW, D]), ALU.subtract).then_inc(s_d, 1)
                dve.wait_ge(s_cs2, 1)
                me.link(nc.vector.tensor_scalar(scale[:, :], total[:, 1, 0:D], 1.0 / N, EPS, ALU.mult, ALU.add))
                inverse_root(nc, dve, me, scale[:, :], root[:, :], inv[:, :], s_ask, s_root, 1)
                me.link(nc.vector.tensor_tensor(scale[:, :], scale[:, :], rows[:, 1, :], ALU.mult))
                for g in range(groups):
                    z = Z[:, g * GW:(g + 1) * GW, :]
                    me.link(nc.vector.tensor_tensor(z, z, scale[:, None, :].to_broadcast([P, GW, D]), ALU.mult))
                    me.link(nc.vector.tensor_tensor(z, z, rows[:, 2:3, :].to_broadcast([P, GW, D]), ALU.add))
                    dve.wait_ge(s_x[g % 2], 16 * (g // 2 + 1 + (g == groups - 1)))
                    nc.vector.tensor_tensor(z, z, xg[:, g % 2, :, :], ALU.add).then_inc(s_x2, 1)
                    if g:
                        dve.wait_ge(s_st2[g - 1], 16)
                        less_means(nc, Z, stat, s_sub, g - 1)
                    dve.wait_ge(s_x2, g + 1)
                    row_means(nc, me, Z, stat, g)
                dve.wait_ge(s_st2[groups - 1], 16)
                less_means(nc, Z, stat, s_sub, groups - 1)
                row_scales(nc, dve, me, rstd, s_all, (root[:, 0:NW], inv[:, 0:NW], s_ask, s_root, 2))
                for g in range(groups):
                    scale_rows(nc, Z, rstd, s_n, g)

                dve.wait_ge(s_n, groups)

                def put(k, s, first):
                    if not first:
                        dve.wait_ge(s_tp, k - 1)
                    nc.vector.tensor_copy(stage[:, s, :, :], Z[:, bass.ds(k * T, T), :]).then_inc(s_stage, 1)

                def keep(k, i, s, first, last):
                    if type(k) is not int or k + 2 < NW // T:
                        put(k + 2, s, False)
                    dve.wait_ge(s_hp, k + 1)
                    nc.vector.tensor_copy(heads[:, bass.ds(k * T, T), 0:HG], hp[:, s, :, :]).then_inc(s_h, 1)
                put(0, 0, True)
                put(1, 1, True)
                pairs_but_last(dve, NW // T, keep)
                dve.wait_ge(s_h, NW // T)
                for n, to in ((0, heads[:, :, HG:ROW]), (1, adst[:, :, :])):
                    me.link(nc.vector.tensor_tensor(prod[:, :, :], heads[:, :, 0:HG],
                                                    atts[:, n:n + 1, :].to_broadcast([P, NW, HG]), ALU.mult))
                    me.link(nc.vector.tensor_reduce(to, prod[:, :, :].rearrange("p w (h e) -> p w h e", e=NE), AX.X, ALU.add))
                dve.sem_inc(s_tab)

            @block.scalar
            def _(act):
                def square(k, i, s, first, last):
                    if not first:
                        act.wait_ge(s_hsq, k - 1)
                    nc.scalar.activation(sq[:, s, :], Z[:, bass.ds(k, 1), :].rearrange("p a d -> p (a d)"),
                                         ACT.Square).then_inc(s_sq, 1)
                window_pairs(act, s_d, square)
                take_root(nc, act, scale[:, :], root[:, :], s_ask, s_root, 1)
                square_rows(nc, act, Z, sq, rstd, s_sub, s_each, s_all)
                take_root(nc, act, rstd[:, :], root[:, 0:NW], s_ask, s_root, 2)

                def copy(k, i, s, first, last):
                    act.wait_ge(s_tp, k + 1)
                    if not first:
                        act.wait_ge(s_hp, k - 1)
                    nc.scalar.copy(zt[:, s, :, :, :], tp[:, s, :, :, :]).then_inc(s_zt, 1)
                pairs(act, NW // T, copy)

            @block.tensor
            def _(pe):
                for g in range(groups):
                    pe.wait_ge(s_y, g + 1)
                    for w in range(g * GW, (g + 1) * GW):
                        n = LASTROWS if w == NW - 1 else P
                        m = nc.tensor.matmul(total[:, 0, 0:D], c["ones"][0:n, :], Z[0:n, w, :], start=(w == 0), stop=(w == NW - 1))
                m.then_inc(s_cs, 1)

                def squares(k, i, s, first, last):
                    pe.wait_ge(s_sq, k + 1)
                    n = LASTROWS if last else P
                    nc.tensor.matmul(total[:, 1, 0:D], c["ones"][0:n, :], sq[0:n, s, :],
                                     start=first and s == 0, stop=last).then_inc(s_hsq, 1)
                pairs(pe, NW, squares)
                pe.wait_ge(s_hsq, NW)
                pe.sem_inc(s_cs2)

                def turn(k, s, first):
                    pe.wait_ge(s_stage, k + 1)
                    if not first:
                        pe.wait_ge(s_zt, k - 1)
                    for t in range(T):
                        for q in range(KC):
                            m = nc.tensor.transpose(tp[:, s, q, t, :], stage[:, s, t, q * P:(q + 1) * P], c["ident"][:, :])
                    m.then_inc(s_tp, 1)

                def product(k, i, s, first, last):
                    if not last:
                        turn(k + 1, 1 - s, first and s == 0)
                    pe.wait_ge(s_zt, k + 1)
                    if not first:
                        pe.wait_ge(s_h, k - 1)
                    for t in range(T):
                        for q in range(KC):
                            m = nc.tensor.matmul(hp[:, s, t, :], zt[:, s, q, t, :], wg[:, q, :], start=(q == 0), stop=(q == KC - 1))
                    m.then_inc(s_hp, 1)
                turn(0, 0, True)
                pairs(pe, NW // T, product)


TB = 4


def attention_max(nc, c, ps, table, idx, lo_f, H, most):
    batches = tiles_bound(E_FFN) // GT
    with ExitStack() as ctx:
        def sb(name, shape, dt):
            return ctx.enter_context(nc.sbuf_tensor("a_" + name, shape, dt))

        def sem(name):
            return c["sems"].enter_context(nc.alloc_semaphore("a_" + name))
        ring = sb("ring", [P, 2, GT], U32)
        got = sb("got", [P, 2, GT, ROW], F32)
        parts = sb("parts", [P, 2, GT, 2, HEADS], BF16)
        turned = sb("turned", [2 * HEADS, 2, GT, P], BF16)
        hot = sb("hot", [P, 2, GT, P], BF16)
        other = sb("other", [P, 2, GT, P], BF16)
        term = ps[:, 0:TB, :].rearrange("p j (h q) -> p j h q", q=P)
        tp = ps[0:2 * HEADS, 4:6, :].bitcast(BF16)[:, :, 0:GT * P].rearrange("p s (j q) -> p s j q", q=P)
        s_idx, s_hi, s_parts, s_eq, s_hot, s_tp, s_turned, s_term, s_most, s_keep, s_tick = (
            sem(n) for n in ("idx", "hi", "parts", "eq", "hot", "tp", "turned", "term", "most", "keep", "tick"))
        s_got = [sem("got0"), sem("got1")]
        with nc.Block() as block:
            @block.scalar
            def _(act):
                def mask(k, s, first):
                    act.wait_ge(s_eq, k + 1)
                    if not first:
                        act.wait_ge(s_term, k * GT - GT)
                    nc.scalar.activation(other[:, s, :, :], hot[:, s, :, :], ACT.Copy, bias=-BIG,
                                         scale=BIG).then_inc(s_hot, 1)

                def rows(k, i, s, first, last):
                    if not first:
                        act.wait_ge(s_got[s], i * (16 * GT))
                    nc.scalar.copy(ring[:, s, :], idx[:, bass.ds(k * GT, GT)]).then_inc(s_idx, 1)

                def keep(k, i, s, first, last):
                    mask(k, s, first)
                    act.wait_ge(s_got[s], i * (16 * GT) + 16 * GT)
                    nc.scalar.copy(H[:, bass.ds(k * GT, GT), :], got[:, s, :, :]).then_inc(s_keep, 1)
                    act.wait_ge(s_tp, k + 1)
                    nc.scalar.copy(turned[:, s, :, :], tp[:, s, :, :]).then_inc(s_turned, 1)
                    if type(k) is not int or k + 2 < batches:
                        rows(k + 2, i + 1, s, False, False)
                rows(0, 0, 0, True, False)
                rows(1, 0, 1, True, False)
                pairs_but_last(act, batches, keep)

            @block.gpsimd
            def _(pool):
                def gather(k, i, s, first, last):
                    pool.wait_ge(s_idx, k + 1)
                    pool.sem_inc(s_tick)
                    if not first:
                        pool.wait_ge(s_keep, k - 1)
                        pool.sem_inc(s_tick)
                        pool.wait_ge(s_parts, k - 1)
                        pool.sem_inc(s_tick)
                    for j in range(GT):
                        nc.gpsimd.indirect_dma_start(
                            out=got[:, s, j, :], out_offset=None, in_=table,
                            in_offset=bass.IndirectOffsetOnAxis(ap=ring[:, s, j:j + 1], axis=0),
                            bounds_check=NP - 1, oob_is_err=False).then_inc(s_got[s], 16)
                pairs(pool, batches, gather)

            @block.vector
            def _(dve):
                def one_hot(k, s, first):
                    if not first:
                        dve.wait_ge(s_hot, k - 1)
                        dve.wait_ge(s_term, k * GT - GT)
                    nc.vector.tensor_tensor(hot[:, s, :, :], c["iota_b"][:, None, :].to_broadcast([P, GT, P]),
                                            lo_f[:, bass.ds(k * GT, GT), None].to_broadcast([P, GT, P]),
                                            ALU.is_equal).then_inc(s_eq, 1)

                def split(k, i, s, first):
                    dve.wait_ge(s_got[s], i * (16 * GT) + 16 * GT)
                    if not first:
                        dve.wait_ge(s_tp, k - 1)
                    nc.vector.tensor_copy(parts[:, s, :, 0, :], got[:, s, :, HG:ROW]).then_inc(s_hi, 1)
                    dve.wait_ge(s_hi, k + 1)
                    nc.vector.tensor_tensor(parts[:, s, :, 1, :], got[:, s, :, HG:ROW], parts[:, s, :, 0, :],
                                            ALU.subtract).then_inc(s_parts, 1)

                def largest(k, i, s, first, last):
                    for j in range(GT):
                        if j == 2 and not last:
                            one_hot(k + 1, 1 - s, first and s == 0)
                            split(k + 1, i + s, 1 - s, first and s == 0)
                        dve.wait_ge(s_term, k * GT + j + 1)
                        nc.vector.tensor_reduce(most[:, bass.ds(k * GT + j, 1), :].rearrange("p a h -> p (a h)"),
                                                term[:, j % TB, :, :], AX.X, ALU.max).then_inc(s_most, 1)
                one_hot(0, 0, True)
                split(0, 0, 0, True)
                pairs(dve, batches, largest)

            @block.tensor
            def _(pe):
                def turn(k, s, first):
                    pe.wait_ge(s_parts, k + 1)
                    if not first:
                        pe.wait_ge(s_turned, k - 1)
                    for j in range(GT):
                        m = nc.tensor.transpose(tp[:, s, j, :], parts[:, s, j, :, :].rearrange("p a h -> p (a h)"),
                                                c["ident_b"][:, :])
                    m.then_inc(s_tp, 1)

                def product(k, i, s, first, last):
                    pe.wait_ge(s_hot, k + 1)
                    pe.wait_ge(s_turned, k + 1)
                    for j in range(GT):
                        if j == GT - 2 and not last:
                            turn(k + 1, 1 - s, first and s == 0)
                        if not (first and s == 0 and j < TB):
                            pe.wait_ge(s_most, k * GT + j - TB + 1)
                        nc.tensor.matmul(term[:, j % TB, :, :], other[:, s, j, :],
                                         c["ident_b"][:, None, :].to_broadcast([P, HEADS, P]), start=True, stop=False)
                        for h in range(HEADS):
                            m = nc.tensor.matmul(term[:, j % TB, h, :], c["pick"][:, h, :], turned[:, s, j, :],
                                                 start=False, stop=(h == HEADS - 1))
                        m.then_inc(s_term, 1)
                turn(0, 0, True)
                pairs(pe, batches, product)


ST = 8


def three_parts(nc, me_did, me_settle, parts, rest, value):
    me_did(nc.vector.tensor_copy(parts[0], value))
    me_settle()
    me_did(nc.vector.tensor_tensor(rest, value, parts[0], ALU.subtract))
    me_settle()
    me_did(nc.vector.tensor_copy(parts[1], rest))
    me_settle()
    me_did(nc.vector.tensor_tensor(parts[2], rest, parts[1], ALU.subtract))


def attention_sums(nc, c, ps, H, lo_f, win_row, node):
    batches = tiles_bound(E_FFN) // ST
    with ExitStack() as ctx:
        def sb(name, shape, dt=F32):
            return ctx.enter_context(nc.sbuf_tensor("s_" + name, shape, dt))

        def sem(name):
            return c["sems"].enter_context(nc.alloc_semaphore("s_" + name))
        hot = sb("hot", [P, 3, ST, P], BF16)
        turned = sb("turned", [P, 3, ST, P], BF16)
        thirds = sb("thirds", [P, 3, 3, ST, ROW], BF16)
        rest = sb("rest", [P, ST, ROW])
        brought = sb("brought", [P, ST, 2, HEADS])
        edge = sb("edge", [P, ST, HEADS])
        steep = sb("steep", [P, ST, HEADS])
        expo = sb("expo", [P, 3, ST, HEADS])
        msg = sb("msg", [P, 3, ST, ROW])
        tp = ps[:, 0, :].bitcast(BF16).rearrange("p (j q) -> p j q", q=P)
        s_third = sem("third")
        s_hot, s_tp, s_turned, s_at, s_e, s_x, s_ee, s_msg, s_part, s_sum = (
            sem(n) for n in ("hot", "tp", "turned", "at", "e", "x", "ee", "msg", "part", "sum"))

        def at_of(s):
            return ps[:, 1 + s, 0:ST * 6 * HEADS].rearrange("p (j q h) -> p j q h", q=3, h=2 * HEADS)

        def part_of(s):
            return ps[:, 4 + s, 0:ST * ROW].rearrange("p (j r) -> p j r", r=ROW)
        with nc.Block() as block:
            @block.vector
            def _(dve):
                def one_hot(k, s):
                    if past(k, 3):
                        dve.wait_ge(s_part, k - 2)
                    nc.vector.tensor_tensor(hot[:, s, :, :], c["iota_b"][:, None, :].to_broadcast([P, ST, P]),
                                            lo_f[:, bass.ds(k * ST, ST), None].to_broadcast([P, ST, P]),
                                            ALU.is_equal).then_inc(s_hot, 1)

                def exponents(k, s):
                    dve.wait_ge(s_at, k + 1)
                    nc.vector.tensor_reduce(brought[:, :, :, :].rearrange("p j a h -> p j (a h)"),
                                            at_of(s).rearrange("p j q h -> p j h q"), AX.X, ALU.add).then_inc(s_e, 1)
                    dve.wait_ge(s_e, k * 4 + 1)
                    nc.vector.tensor_tensor(edge[:, :, :], H[:, bass.ds(k * ST, ST), HG:ROW], brought[:, :, 0, :],
                                            ALU.add).then_inc(s_e, 1)
                    dve.wait_ge(s_e, k * 4 + 2)
                    nc.vector.scalar_tensor_tensor(steep[:, :, :], edge[:, :, :], 0.2, edge[:, :, :], ALU.mult,
                                                   ALU.max).then_inc(s_e, 1)
                    dve.wait_ge(s_e, k * 4 + 3)
                    nc.vector.tensor_tensor(edge[:, :, :], steep[:, :, :], brought[:, :, 1, :],
                                            ALU.subtract).then_inc(s_e, 1)
                    dve.wait_ge(s_e, k * 4 + 4)
                    if past(k, 3):
                        dve.wait_ge(s_ee, k - 2)
                    nc.vector.tensor_scalar(expo[:, s, :, :], edge[:, :, :], 60.0, None, ALU.min).then_inc(s_x, 1)

                def weigh(k, s):
                    dve.wait_ge(s_ee, k + 1)
                    nc.vector.tensor_tensor(
                        msg[:, s, :, 0:HG].rearrange("p j (h e) -> p j h e", e=NE),
                        H[:, bass.ds(k * ST, ST), 0:HG].rearrange("p j (h e) -> p j h e", e=NE),
                        msg[:, s, :, HG:ROW, None].to_broadcast([P, ST, HEADS, NE]), ALU.mult).then_inc(s_third, 1)
                    dve.wait_ge(s_third, k * 4 + 1)
                    if past(k, 3):
                        dve.wait_ge(s_part, k - 2)
                    nc.vector.tensor_copy(thirds[:, s, 0, :, :], msg[:, s, :, :]).then_inc(s_third, 1)
                    dve.wait_ge(s_third, k * 4 + 2)
                    nc.vector.tensor_tensor(rest[:, :, :], msg[:, s, :, :], thirds[:, s, 0, :, :],
                                            ALU.subtract).then_inc(s_third, 1)
                    dve.wait_ge(s_third, k * 4 + 3)
                    nc.vector.tensor_copy(thirds[:, s, 1, :, :], rest[:, :, :]).then_inc(s_third, 1)
                    dve.wait_ge(s_third, k * 4 + 4)
                    nc.vector.tensor_tensor(thirds[:, s, 2, :, :], rest[:, :, :], thirds[:, s, 1, :, :],
                                            ALU.subtract).then_inc(s_msg, 1)

                def keep(k, s):
                    dve.wait_ge(s_part, k + 1)
                    nc.vector.tensor_scalar(H[:, bass.ds(k * ST, ST), :], part_of(s), 1.0, None, ALU.mult).then_inc(s_sum, 1)

                def step(k, s):
                    if past(k, 1):
                        keep(k - 1, (s + 2) % 3)
                    if more(k, 2, batches):
                        one_hot(k + 2, (s + 2) % 3)
                    if more(k, 1, batches):
                        exponents(k + 1, (s + 1) % 3)
                        weigh(k + 1, (s + 1) % 3)
                one_hot(0, 0)
                one_hot(1, 1)
                exponents(0, 0)
                weigh(0, 0)
                threes(dve, batches, step)
                keep(batches - 1, (batches - 1) % 3)

            @block.scalar
            def _(act):
                def copy(k, s):
                    act.wait_ge(s_tp, k + 1)
                    if past(k, 3):
                        act.wait_ge(s_at, k - 2)
                    nc.scalar.copy(turned[:, s, :, :], tp[:, :, :]).then_inc(s_turned, 1)

                def weights(k, s):
                    act.wait_ge(s_x, k + 1)
                    if past(k, 3):
                        act.wait_ge(s_msg, k - 2)
                    nc.scalar.activation(msg[:, s, :, HG:ROW], expo[:, s, :, :], ACT.Exp).then_inc(s_ee, 1)

                def step(k, s):
                    if more(k, 1, batches):
                        weights(k + 1, (s + 1) % 3)
                    if more(k, 2, batches):
                        copy(k + 2, (s + 2) % 3)
                copy(0, 0)
                copy(1, 1)
                weights(0, 0)
                threes(act, batches, step)

            @block.tensor
            def _(pe):
                def turn(k, s):
                    pe.wait_ge(s_hot, k + 1)
                    if past(k, 1):
                        pe.wait_ge(s_turned, k)
                    for j in range(ST):
                        m = nc.tensor.transpose(tp[:, j, :], hot[:, s, j, :], c["ident_b"][:, :])
                    m.then_inc(s_tp, 1)

                def bring(k, s):
                    wins = window_values(nc, win_row, k * ST, ST, mybir.EngineType.PE)
                    pe.wait_ge(s_turned, k + 1)
                    if past(k, 3):
                        pe.wait_ge(s_x, k - 2)
                    for j in range(ST):
                        m = nc.tensor.matmul(at_of(s)[:, j, :, :].rearrange("p q h -> p (q h)"), turned[:, s, j, :],
                                             node[:, bass.ds(wins[j], 1), :, :].rearrange("p a q h -> p (a q h)"),
                                             start=True, stop=True)
                    m.then_inc(s_at, 1)

                def product(k, s):
                    pe.wait_ge(s_msg, k + 1)
                    if past(k, 3):
                        pe.wait_ge(s_sum, k - 2)
                    for j in range(ST):
                        for q in range(3):
                            m = nc.tensor.matmul(part_of(s)[:, j, :], hot[:, s, j, :], thirds[:, s, q, j, :],
                                                 start=(q == 0), stop=(q == 2))
                    m.then_inc(s_part, 1)

                def step(k, s):
                    if past(k, 1):
                        product(k - 1, (s + 2) % 3)
                    if more(k, 1, batches):
                        bring(k + 1, (s + 1) % 3)
                    if more(k, 2, batches):
                        turn(k + 2, (s + 2) % 3)
                turn(0, 0)
                turn(1, 1)
                bring(0, 0)
                threes(pe, batches, step)
                product(batches - 1, (batches - 1) % 3)


def last_of_windows(nc, eng, take, last_tile):
    each = 7
    with eng.Fori(0, NW // each) as i:
        at = nc.values_load_multi_w_load_instructions(
            last_tile[0:1, bass.ds(i * each, each)], engines=[mybir.EngineType.DVE], min_val=0,
            max_val=tiles_bound(E_FFN) - 1, skip_runtime_bounds_check_because="tiles are counted on the chip")[1]
        for n in range(each):
            take(i * each + n, at[n])


def node_maxima(nc, c, most, runs, adst, heads, top, node3, sums):
    same, last_tile, filled = runs
    nt = tiles_bound(E_FFN)
    with ExitStack() as ctx:
        def sb(name, shape):
            return ctx.enter_context(nc.sbuf_tensor("x_" + name, shape, F32))

        def sem(name):
            return c["sems"].enter_context(nc.alloc_semaphore("x_" + name))
        raw = sb("raw", [P, NW, HEADS])
        loop = sb("loop", [P, NW, HEADS])
        fresh = sb("fresh", [P, nt])
        none = sb("none", [P, NW])
        node = sb("node", [P, NW, 2 * HEADS])
        rest = sb("rest", [P, NW, 2 * HEADS])
        s_dve, s_e, s_x, s_top = sem("dve"), sem("e"), sem("x"), sem("top")
        with nc.Block() as block:
            @block.vector
            def _(dve):
                me = Steps(dve, s_dve)
                me.link(nc.vector.tensor_scalar(fresh[:, :], same[:, 0:nt], -1.0, BIG, ALU.add, ALU.mult))
                me.link(nc.vector.tensor_scalar(none[:, :], filled[:, :], -1.0, BIG, ALU.add, ALU.mult))
                for h in range(HEADS):
                    me.did(nc.vector.tensor_tensor_scan(most[:, :, h], fresh[:, :], most[:, :, h], -BIG, ALU.add, ALU.max))
                me.settle()
                last_of_windows(nc, dve, lambda w, t: nc.vector.tensor_copy(
                    top[:, bass.ds(w, 1), :], most[:, bass.ds(t, 1), :]).then_inc(s_top, 1), last_tile)
                dve.wait_ge(s_top, NW)
                me.link(nc.vector.tensor_tensor(top[:, :, :], top[:, :, :], none[:, :, None].to_broadcast([P, NW, HEADS]), ALU.add))
                me.link(nc.vector.tensor_tensor(top[:, :, :], top[:, :, :], heads[:, :, HG:ROW], ALU.max))
                me.link(nc.vector.tensor_copy(node[:, :, 0:HEADS], adst[:, :, :]))
                me.link(nc.vector.tensor_tensor(raw[:, :, :], top[:, :, :], adst[:, :, :], ALU.add))
                me.link(nc.vector.scalar_tensor_tensor(node[:, :, HEADS:2 * HEADS], raw[:, :, :], 0.2, raw[:, :, :],
                                                       ALU.mult, ALU.max))
                three_parts(nc, me.did, me.settle, [node3[:, :, q, :] for q in range(3)], rest[:, :, :], node[:, :, :])
                me.link(nc.vector.tensor_tensor(raw[:, :, :], heads[:, :, HG:ROW], adst[:, :, :], ALU.add))
                me.link(nc.vector.scalar_tensor_tensor(loop[:, :, :], raw[:, :, :], 0.2, raw[:, :, :], ALU.mult, ALU.max))
                me.link(nc.vector.tensor_tensor(raw[:, :, :], loop[:, :, :], node[:, :, HEADS:2 * HEADS], ALU.subtract))
                dve.sem_inc(s_e)
                dve.wait_ge(s_x, 1)
                nc.vector.tensor_tensor(sums[:, :, 0:HG].rearrange("p w (h e) -> p w h e", e=NE),
                                        heads[:, :, 0:HG].rearrange("p w (h e) -> p w h e", e=NE),
                                        sums[:, :, HG:ROW, None].to_broadcast([P, NW, HEADS, NE]), ALU.mult)

            @block.scalar
            def _(act):
                act.wait_ge(s_e, 1)
                nc.scalar.activation(sums[:, :, HG:ROW], raw[:, :, :], ACT.Exp).then_inc(s_x, 1)


def gates_of(nc, c, H, runs, sums, b_gat, ln_gamma, ln_beta, gates):
    same, last_tile, filled = runs
    nt = tiles_bound(E_FFN)
    with ExitStack() as ctx:
        def sb(name, shape):
            return ctx.enter_context(nc.sbuf_tensor("g_" + name, shape, F32))
        vecs = sb("vecs", [P, 3, HG])
        tiled = sb("tiled", [P, NW, ROW])
        s_last = c["sems"].enter_context(nc.alloc_semaphore("g_last"))
        den = sb("den", [P, NW, HEADS])
        agg = sb("agg", [P, NW, HG])
        sq = sb("sq", [P, NW, HG])
        one = sb("one", [P, NW])
        two = sb("two", [P, NW])
        root = sb("root", [P, NW])
        inv = sb("inv", [P, NW])
        s_ask = c["sems"].enter_context(nc.alloc_semaphore("g_ask"))
        s_root = c["sems"].enter_context(nc.alloc_semaphore("g_root"))
        score = sb("score", [P, NW, NE])
        rank = sb("rank", [P, NW, NE])
        gap = sb("gap", [P, NW, NE])
        s_w = c["sems"].enter_context(nc.alloc_semaphore("g_w"))
        s_dve = c["sems"].enter_context(nc.alloc_semaphore("g_dve"))
        s_e = c["sems"].enter_context(nc.alloc_semaphore("g_e"))
        s_x = c["sems"].enter_context(nc.alloc_semaphore("g_x"))
        with nc.Block() as block:
            @block.sync
            def _(sp):
                for n, v in enumerate((b_gat, ln_gamma, ln_beta)):
                    sp.dma_start(vecs[:, n, :], v.rearrange("(a h) -> a h", a=1).to_broadcast([P, HG])).then_inc(s_w, 16)

            @block.vector
            def _(dve):
                me = Steps(dve, s_dve)
                v = nc.vector

                def spread(x, n):
                    return x[:, :, None].to_broadcast([P, NW, n])
                for r in range(ROW):
                    me.did(v.tensor_tensor_scan(H[:, :, r], same[:, 0:nt], H[:, :, r], 0.0, ALU.mult, ALU.add))
                me.settle()
                last_of_windows(nc, dve, lambda w, t: nc.vector.tensor_copy(
                    tiled[:, bass.ds(w, 1), :], H[:, bass.ds(t, 1), :]).then_inc(s_last, 1), last_tile)
                dve.wait_ge(s_last, NW)
                me.link(v.tensor_tensor(tiled[:, :, :], tiled[:, :, :], spread(filled, ROW), ALU.mult))
                me.link(v.tensor_tensor(sums[:, :, :], sums[:, :, :], tiled[:, :, :], ALU.add))
                me.link(v.tensor_scalar(den[:, :, :], sums[:, :, HG:ROW], 1e-16, None, ALU.add))
                me.link(v.reciprocal(den[:, :, :], den[:, :, :]))
                me.link(v.tensor_tensor(agg[:, :, :].rearrange("p w (h e) -> p w h e", e=NE),
                                        sums[:, :, 0:HG].rearrange("p w (h e) -> p w h e", e=NE),
                                        den[:, :, :, None].to_broadcast([P, NW, HEADS, NE]), ALU.mult))
                dve.wait_ge(s_w, 48)
                me.link(v.tensor_tensor(agg[:, :, :], agg[:, :, :], vecs[:, 0:1, :].to_broadcast([P, NW, HG]), ALU.add))
                me.link(v.tensor_reduce(one[:, :], agg[:, :, :], AX.X, ALU.add))
                me.link(v.tensor_scalar(one[:, :], one[:, :], 1.0 / HG, None, ALU.mult))
                me.link(v.tensor_tensor(agg[:, :, :], agg[:, :, :], spread(one, HG), ALU.subtract))
                me.link(v.tensor_tensor(sq[:, :, :], agg[:, :, :], agg[:, :, :], ALU.mult))
                me.link(v.tensor_reduce(two[:, :], sq[:, :, :], AX.X, ALU.add))
                me.link(v.tensor_scalar(two[:, :], two[:, :], 1.0 / HG, EPS, ALU.mult, ALU.add))
                inverse_root(nc, dve, me, two[:, :], root[:, :], inv[:, :], s_ask, s_root, 1)
                me.link(v.tensor_tensor(agg[:, :, :], agg[:, :, :], spread(two, HG), ALU.mult))
                me.link(v.tensor_tensor(agg[:, :, :], agg[:, :, :], vecs[:, 1:2, :].to_broadcast([P, NW, HG]), ALU.mult))
                me.link(v.tensor_tensor(agg[:, :, :], agg[:, :, :], vecs[:, 2:3, :].to_broadcast([P, NW, HG]), ALU.add))
                me.link(v.tensor_reduce(score[:, :, :], agg[:, :, :].rearrange("p w (h e) -> p w e h", e=NE), AX.X, ALU.add))
                me.link(v.tensor_scalar(score[:, :, :], score[:, :, :], 1.0 / HEADS, None, ALU.mult))
                for e in range(NE):
                    others = [j for j in range(NE) if j != e]
                    for n, j in enumerate(others):
                        op = ALU.is_ge if j < e else ALU.is_gt
                        to = rank[:, :, e] if n == 0 else one[:, :]
                        me.link(v.tensor_tensor(to, score[:, :, j], score[:, :, e], op))
                        if n:
                            me.link(v.tensor_tensor(rank[:, :, e], rank[:, :, e], one[:, :], ALU.add))
                me.link(v.tensor_reduce(two[:, :], score[:, :, :], AX.X, ALU.max))
                me.link(v.tensor_tensor(gap[:, :, :], score[:, :, :], spread(two, NE), ALU.subtract))
                dve.sem_inc(s_e)
                dve.wait_ge(s_x, 1)
                me.link(v.tensor_scalar(rank[:, :, :], rank[:, :, :], 1.5, None, ALU.is_lt))
                me.link(v.tensor_tensor(gates[:, :, :], gates[:, :, :], rank[:, :, :], ALU.mult))
                me.link(v.tensor_reduce(one[:, :], gates[:, :, :], AX.X, ALU.add))
                me.link(v.reciprocal(one[:, :], one[:, :]))
                me.link(v.tensor_tensor(gates[:, :, :], gates[:, :, :], spread(one, NE), ALU.mult))

            @block.scalar
            def _(act):
                take_root(nc, act, two[:, :], root[:, :], s_ask, s_root, 1)
                act.wait_ge(s_e, 1)
                nc.scalar.activation(gates[:, :, :], gap[:, :, :], ACT.Exp).then_inc(s_x, 1)


def experts(nc, c, ps, x2, xn, W1, b1, W2, b2, gates, out):
    T = 2
    groups = NW // T
    with ExitStack() as ctx:
        def sb(name, shape):
            return ctx.enter_context(nc.sbuf_tensor("e_" + name, shape, F32))


        def sem(name):
            return c["sems"].enter_context(nc.alloc_semaphore("e_" + name))
        w1 = sb("w1", [P, NE, KC, F])
        w2 = sb("w2", [P, NE, FC, D])
        b1c = sb("b1c", [P, NE, FC])
        b2r = sb("b2r", [NE, D])
        xin = sb("xin", [P, 2, T, D])
        res = sb("res", [P, 2, T, D])
        xt = sb("xt", [P, 2, KC, T, P])
        gs = sb("gs", [P, 2, T, NE])
        gt = sb("gt", [NE, 2, T, P])
        hid = sb("hid", [P, 2, FC, T, P])
        up = ps[:, 0:2, :].rearrange("p g (a t q) -> p g a t q", a=2, t=T)
        yp = ps[:, 2:4, :].rearrange("p g (t d) -> p g t d", t=T)
        yb = ps[:, 4, :].rearrange("p (t d) -> p t d", t=T)
        tp = ps[:, 5, :].rearrange("p (k t q) -> p k t q", k=KC, t=T)
        gp = ps[0:NE, 6, 0:T * P].rearrange("p (t q) -> p t q", q=P)
        s_w = sem("w")
        s_in = [sem("in0"), sem("in1")]
        s_res = [sem("res0"), sem("res1")]
        s_gs, s_tp, s_xt, s_up, s_hid, s_y, s_acc, s_st = (
            sem(n) for n in ("gs", "tp", "xt", "up", "hid", "y", "acc", "st"))
        s_out = [sem("out0"), sem("out1")]
        NA = NE + 1
        with nc.Block() as block:
            @block.sync
            def _(sp):
                sp.dma_start(w1[:, :, :, :], W1.rearrange("e (k p) f -> p e k f", p=P)).then_inc(s_w, 16)
                sp.dma_start(w2[:, :, :, :], W2.rearrange("e (k p) d -> p e k d", p=P)).then_inc(s_w, 16)
                sp.dma_start(b2r[:, :], b2).then_inc(s_w, 16)
                with nc.allow_non_contiguous_dma(reason="bias vectors onto partitions"):
                    sp.dma_start(b1c[:, :, :], b1.rearrange("e (k p) -> p e k", p=P)).then_inc(s_w, 16)

                def load(k, i, s, first, last):
                    if not first:
                        sp.wait_ge(s_tp, k - 1)
                    rows = bass.ds(k * (T * P), T * P)
                    sp.dma_start(xin[:, s, :, :], xn[rows, :].rearrange("(t p) d -> p t d", p=P)).then_inc(s_in[s], 16)
                    if not first:
                        sp.wait_ge(s_out[s], i * 16)
                    sp.dma_start(res[:, s, :, :], x2[rows, :].rearrange("(t p) d -> p t d", p=P)).then_inc(s_res[s], 16)
                pairs(sp, groups, load)

            @block.gpsimd
            def _(pool):
                def store(k, i, s, first, last):
                    pool.wait_ge(s_acc, k * NA + NA)
                    pool.sem_inc(s_st)
                    if last:
                        pool.dma_start(out[k * T * P:(NW - 1) * P, :], res[:, s, 0, :]).then_inc(s_out[s], 16)
                        pool.dma_start(out[(NW - 1) * P:N, :], res[0:LASTROWS, s, 1, :]).then_inc(s_out[s], 16)
                    else:
                        pool.dma_start(out[bass.ds(k * (T * P), T * P), :].rearrange("(t p) d -> p t d", p=P),
                                       res[:, s, :, :]).then_inc(s_out[s], 16)
                pairs(pool, groups, store)
                pool.wait_ge(s_out[0], 16 * ((groups + 1) // 2) + (16 if groups % 2 else 0))
                pool.wait_ge(s_out[1], 16 * (groups // 2) + (0 if groups % 2 else 16))

            @block.tensor
            def _(pe):
                def turn(k, i, s, begin):
                    pe.wait_ge(s_in[s], i * 16 + 16)
                    pe.wait_ge(s_gs, k + 1)
                    if not begin:
                        pe.wait_ge(s_xt, k)
                    for t in range(T):
                        for q in range(KC):
                            nc.tensor.transpose(tp[:, q, t, :], xin[:, s, t, q * P:(q + 1) * P], c["ident"][:, :])
                        m = nc.tensor.transpose(gp[:, t, :], gs[:, s, t, :], c["ident"][:, :])
                    m.then_inc(s_tp, 1)

                def product(k, i, s, first, last):
                    if first and s == 0:
                        pe.wait_ge(s_w, 64)
                    pe.wait_ge(s_xt, k + 1)
                    if not (first and s == 0):
                        pe.wait_ge(s_acc, k * NA - NA + 1)
                    for t in range(T):
                        m = nc.tensor.matmul(yb[:, t, :], gt[:, s, t, :], b2r[:, :], start=True, stop=True)
                    m.then_inc(s_y, 1)

                    def up_of(e):
                        for g in range(2):
                            n = e * 2 + g
                            if not (first and s == 0 and n < 2):
                                pe.wait_ge(s_hid, k * (2 * NE) + n - 1)
                            for a in range(2):
                                f = g * 2 + a
                                for q in range(KC):
                                    m = nc.tensor.matmul(up[:, g, a, :, :], w1[:, e, q, f * P:(f + 1) * P],
                                                         xt[:, s, q, :, :], start=(q == 0), stop=(q == KC - 1))
                            m.then_inc(s_up, 1)

                    def down_of(e):
                        pe.wait_ge(s_hid, k * (2 * NE) + 2 * e + 2)
                        if not (first and s == 0 and e < 2):
                            pe.wait_ge(s_acc, k * NA + e if e >= 2 else k * NA - NA + NE + e)
                        for t in range(T):
                            for f in range(FC):
                                m = nc.tensor.matmul(yp[:, e % 2, t, :], hid[:, e % 2, f, t, :], w2[:, e, f, :],
                                                     start=(f == 0), stop=(f == FC - 1))
                        m.then_inc(s_y, 1)
                    up_of(0)
                    for e in range(NE):
                        if e + 1 < NE:
                            up_of(e + 1)
                        down_of(e)
                        if e == 1 and not last:
                            turn(k + 1, i + s, 1 - s, False)
                turn(0, 0, 0, True)
                pairs(pe, groups, product)

            @block.scalar
            def _(act):
                def act_group(k, i, s, first, last):
                    for e in range(NE):
                        for g in range(2):
                            n = e * 2 + g
                            act.wait_ge(s_up, k * (2 * NE) + n + 1)
                            if not (first and s == 0 and e < 2):
                                act.wait_ge(s_y, k * NA + e if e >= 2 else k * NA - NA + NE + e)
                            for a in range(2):
                                f = g * 2 + a
                                m = nc.scalar.activation(hid[:, e % 2, f, :, :], up[:, g, a, :, :], ACT.Gelu,
                                                         bias=b1c[:, e, f:f + 1])
                            m.then_inc(s_hid, 1)
                pairs(act, groups, act_group)

            @block.vector
            def _(dve):
                def pass_gates(k, s, first):
                    if not first:
                        dve.wait_ge(s_tp, k - 1)
                    nc.vector.tensor_copy(gs[:, s, :, :], gates[:, bass.ds(k * T, T), :]).then_inc(s_gs, 1)

                def take_turned(k, s):
                    dve.wait_ge(s_tp, k + 1)
                    nc.vector.tensor_copy(xt[:, s, :, :, :], tp[:, :, :, :])
                    nc.vector.tensor_copy(gt[:, s, :, :], gp[:, :, :]).then_inc(s_xt, 1)

                def sum_group(k, i, s, first, last):
                    dve.wait_ge(s_res[s], i * 16 + 16)
                    dve.wait_ge(s_y, k * NA + 1)
                    nc.vector.tensor_tensor(res[:, s, :, :], res[:, s, :, :], yb[:, :, :], ALU.add).then_inc(s_acc, 1)
                    for e in range(NE):
                        dve.wait_ge(s_y, k * NA + e + 2)
                        dve.wait_ge(s_acc, k * NA + e + 1)
                        for t in range(T):
                            m = nc.vector.scalar_tensor_tensor(res[:, s, t, :], yp[:, e % 2, t, :], gs[:, s, t, e:e + 1],
                                                               res[:, s, t, :], ALU.mult, ALU.add)
                        m.then_inc(s_acc, 1)
                        if e == 0 and not last:
                            pass_gates(k + 1, 1 - s, first and s == 0)
                        if e == 1 and not last:
                            take_turned(k + 1, 1 - s)
                pass_gates(0, 0, True)
                take_turned(0, 0)
                pairs(dve, groups, sum_group)


def gnn_ffn(nc, x, src, dst, gW1, gb1, gW2, gb2, ggamma, gbeta, wgat, att_src, att_dst, b_gat, ln_gamma, ln_beta,
            fW1, fb1, fW2, fb2, edge_index, out):
    def dram(name, shape, dt=F32):
        return nc.dram_tensor(name, shape, dt, kind="Internal").ap()
    gnn_slots, ffn_slots = blocks_bound(E_GNN), blocks_bound(E_FFN)
    gnn_list = dram("gnn_list", [columns_of(E_GNN) * P, 2], I32)
    src_rows = dram("src_rows", [columns_of(E_GNN), P], I32)
    dst_rows = dram("dst_rows", [columns_of(E_GNN), P], I32)
    ffn_list = dram("ffn_list", [ffn_slots * P, 2], I32)
    rows1 = dram("rows1", [NP, D])
    rows2 = dram("rows2", [NP, D])
    x2 = dram("x2", [NP, D])
    xn = dram("xn", [NP, D])
    rows3 = dram("rows3", [NP, ROW])
    with ExitStack() as ctx:
        def sb(name, shape, dt=F32):
            return ctx.enter_context(nc.sbuf_tensor(name, shape, dt))
        c = make_consts(nc, ctx, Signals(nc))
        ps = ctx.enter_context(nc.psum_tensor("ps", [P, 8, BANK], F32))
        ffn_idx = sb("ffn_idx", [P, ffn_slots], U32)
        ffn_lo = sb("ffn_lo", [P, ffn_slots])
        ffn_win = sb("ffn_win", [1, ffn_slots], I32)
        runs = (sb("same", [P, ffn_slots]), sb("last_tile", [1, NW], I32), sb("filled", [P, NW]))
        heads = sb("heads", [P, NW, ROW])
        adst = sb("adst", [P, NW, HEADS])
        with ExitStack() as gctx:
            def gsb(name, shape, dt=F32):
                return gctx.enter_context(nc.sbuf_tensor(name, shape, dt))
            gnn_idx = gsb("gnn_idx", [P, gnn_slots], U32)
            gnn_lo = gsb("gnn_lo", [P, gnn_slots])
            gnn_win = gsb("gnn_win", [1, gnn_slots], I32)
            deg = gsb("deg", [P, NW])
            dinv = gsb("dinv", [P, NW])
            falls = gsb("windows_fall", [1, 1], I32)
            copy_rows(nc, c, src, dst, src_rows, dst_rows)
            c["sems"].give_back()
            bin_edges(nc, c, ps, edge_index[0], edge_index[1], ffn_list, ffn_idx, ffn_lo, ffn_win, runs, dst, deg, falls)
            c["sems"].give_back()
            fall = nc.values_load(falls[0:1, 0:1], min_val=0, max_val=2 * P)
            with nc.If(fall != 0):
                group_edges(nc, c, ps, deg, src, dst, gnn_list, src_rows, dst_rows)
                c["sems"].give_back()
            take_tiles(nc, c, ps, deg, src_rows, dst_rows, gnn_idx, gnn_lo, gnn_win)
            c["sems"].give_back()
            with nc.sbuf_tensor("Z", [P, NW, D], F32) as Z:
                first_norm(nc, c, x, Z, deg, dinv, rows1)
                c["sems"].give_back()
                convolve(nc, c, ps, "u_", rows1, Z, gnn_idx, gnn_lo, gnn_win)
                c["sems"].give_back()
                between(nc, c, ps, gW1, gb1, gW2, Z, dinv, rows2)
                c["sems"].give_back()
                convolve(nc, c, ps, "v_", rows2, Z, gnn_idx, gnn_lo, gnn_win)
                c["sems"].give_back()
                batch_norm(nc, c, ps, x, gb2, ggamma, gbeta, wgat, att_src, att_dst, Z, dinv, x2, xn, heads, adst, rows3)
                c["sems"].give_back()
        gates = sb("gates", [P, NW, NE])
        with ExitStack() as actx:
            def asb(name, shape, dt=F32):
                return actx.enter_context(nc.sbuf_tensor(name, shape, dt))
            H = asb("H", [P, tiles_bound(E_FFN), ROW])
            top = asb("top", [P, NW, HEADS])
            node = asb("node", [P, NW, 3, 2 * HEADS], BF16)
            sums = asb("sums", [P, NW, ROW])
            with nc.sbuf_tensor("most", [P, tiles_bound(E_FFN), HEADS], F32) as most:
                attention_max(nc, c, ps, rows3, ffn_idx, ffn_lo, H, most)
                c["sems"].give_back()
                node_maxima(nc, c, most, runs, adst, heads, top, node, sums)
            attention_sums(nc, c, ps, H, ffn_lo, ffn_win, node)
            c["sems"].give_back()
            gates_of(nc, c, H, runs, sums, b_gat, ln_gamma, ln_beta, gates)
            c["sems"].give_back()
        experts(nc, c, ps, x2, xn, fW1, fb1, fW2, fb2, gates, out)


_INS = ["x", "src", "dst", "L0_gnn_W1", "L0_gnn_b1", "L0_gnn_W2", "L0_gnn_b2", "L0_gnn_gamma", "L0_gnn_beta",
        "L0_ffn_W_gat", "L0_ffn_att_src", "L0_ffn_att_dst", "L0_ffn_b_gat", "L0_ffn_ln_gamma", "L0_ffn_ln_beta",
        "L0_ffn_W1", "L0_ffn_b1", "L0_ffn_W2", "L0_ffn_b2", "L0_ffn_edge_index"]


def kernel(**inputs):
    import concourse.bacc as bacc
    from concourse.bass_utils import run_bass_kernel_spmd

    nc = bacc.Bacc("TRN2", target_bir_lowering=False, num_devices=1)
    arrays, args = {}, []
    for name in _INS:
        a = np.ascontiguousarray(inputs[name])
        arrays[f"in_{name}"] = a
        args.append(nc.dram_tensor(f"in_{name}", a.shape, mybir.dt.from_np(a.dtype), kind="ExternalInput").ap())
    args.append(nc.dram_tensor("out", (N, D), F32, kind="ExternalOutput").ap())
    gnn_ffn(nc, *args)
    r = run_bass_kernel_spmd(nc, [arrays], core_ids=[0])
    return r.results[0]["out"]
```
